# Optimizing a Trainium2 kernel written in Bass

```python
import numpy as np
import jax
import jax.numpy as jnp

def _softmax(x, axis=-1):
    return jax.nn.softmax(x, axis=axis)

def _gelu(x):
    return jax.nn.gelu(x, approximate=True)

def _silu(x):
    return jax.nn.silu(x)

def _sigmoid(x):
    return jax.nn.sigmoid(x)

def _layernorm(x, axis=-1, eps=1e-05):
    m = jnp.mean(x, axis=axis, keepdims=True)
    v = jnp.var(x, axis=axis, keepdims=True)
    return (x - m) / jnp.sqrt(v + eps)

def _scatter_add(tgt, idx, src, axis=0):
    return tgt.at[idx].add(src)

def _segment_sum(src, seg, n):
    return jax.ops.segment_sum(src, seg, n)
kernel_name = 'mk_adaln_attn_ffn_d2_seqx_r8_dee0a3'

def setup_inputs(seed: int=0):
    np.random.seed(seed)
    _w = jnp.asarray

    def _rec_inputs():
        import jax
        import jax.numpy as jnp
        _rk = jax.random.key(seed)
        x = -0.0003929 + 0.9999 * jax.random.normal(jax.random.fold_in(_rk, 1), (32, 32, 512), jnp.float32)
        _lenS = 32 - jax.random.randint(jax.random.fold_in(_rk, 7), (32,), 0, max(1, 32 // 4) + 1, jnp.int32)
        _lenS2 = 32 - jax.random.randint(jax.random.fold_in(_rk, 8), (32,), 0, max(1, 32 // 4) + 1, jnp.int32)
        cond_512 = 0.00782532 + 1.00527 * jax.random.normal(jax.random.fold_in(_rk, 11), (32, 64), jnp.float32)
        return (x, cond_512)
    x, cond_512 = _rec_inputs()

    def _L0_cond_setup():
        import jax, jax.numpy as jnp
        from jax import lax
        import numpy as np
        CIN, COUT, K, STYLE_DIM = (32, 32, 3, 64)
        N_LAYERS = 4
        TYPES = ('same', 'upsample', 'same', 'downsample')
        SCALE = 1.0 / float(np.sqrt(CIN * K ** 2))
        EPS = 1e-08
        _BK = np.array([1.0, 3.0, 3.0, 1.0], dtype=np.float32)
        BLUR_K = _BK / _BK.sum()

        def _blur(x, kern, pad):
            B, C, _ = x.shape
            xp = jnp.pad(x, ((0, 0), (0, 0), (pad[0], pad[1])))
            w = jnp.broadcast_to(kern.astype(x.dtype)[None, None, :], (C, 1, kern.shape[0]))
            return lax.conv_general_dilated(xp, w, (1,), 'VALID', feature_group_count=C, dimension_numbers=('NCH', 'OIH', 'NCH'))

        def _conv_same(x, w):
            p = (K - 1) // 2
            return lax.conv_general_dilated(x[None], w, (1,), [(p, p)], dimension_numbers=('NCH', 'OIH', 'NCH'))[0]

        def _conv_down(x, w):
            return lax.conv_general_dilated(x[None], w, (2,), 'VALID', dimension_numbers=('NCH', 'OIH', 'NCH'))[0]

        def _conv_up(x, w_t):
            return lax.conv_transpose(x[None], w_t, (2,), 'VALID', dimension_numbers=('NCH', 'IOH', 'NCH'), transpose_kernel=True)[0]

        def _layer(x, style, w, b, mw, mb, typ):
            s = style @ mw.T + mb
            weight = SCALE * w * s[:, None, :, None]
            demod = lax.rsqrt(jnp.sum(weight * weight, axis=(2, 3)) + EPS)
            weight = weight * demod[:, :, None, None]
            blur_k = jnp.asarray(BLUR_K)
            if typ == 'same':
                out = jax.vmap(_conv_same)(x, weight) + b[None, :, None]
            elif typ == 'upsample':
                out = jax.vmap(_conv_up)(x, weight.transpose(0, 2, 1, 3)) + b[None, :, None]
                out = _blur(out, 2.0 * blur_k, (1, 1))
            elif typ == 'downsample':
                xb = _blur(x, blur_k, (2, 2))
                out = jax.vmap(_conv_down)(xb, weight) + b[None, :, None]
            else:
                raise NotImplementedError(typ)
            return out
        key = jax.random.key(seed)
        ks = jax.random.split(key, 6)
        B, L = (16, 512)
        return {'x': jax.random.normal(ks[0], (B, CIN, L), dtype=jnp.float32), 'style': jax.random.normal(ks[1], (B, STYLE_DIM), dtype=jnp.float32), 'weights': jax.random.normal(ks[2], (N_LAYERS, COUT, CIN, K), dtype=jnp.float32), 'biases': jax.random.normal(ks[3], (N_LAYERS, COUT), dtype=jnp.float32) * 0.1, 'mod_w': jax.random.normal(ks[4], (N_LAYERS, CIN, STYLE_DIM), dtype=jnp.float32) / np.sqrt(STYLE_DIM), 'mod_b': 1.0 + 0.1 * jax.random.normal(ks[5], (N_LAYERS, CIN), dtype=jnp.float32)}
    _L0_cond_all = _L0_cond_setup()
    _L0_cond_in = {k: v for k, v in _L0_cond_all.items() if k in ('weights', 'biases', 'mod_w', 'mod_b')}
    del _L0_cond_all

    def _L0_attn_setup():
        import jax, jax.numpy as jnp
        import numpy as np
        B, S, H = (1, 256, 512)
        N_HEADS, N_KV, HEAD_DIM = (32, 8, 128)
        ROPE_THETA = 10000.0

        def _rope_tables(seqlen, dim, theta):
            inv_freq = 1.0 / theta ** (jnp.arange(0, dim, 2, dtype=jnp.float32) / dim)
            t = jnp.arange(seqlen, dtype=jnp.float32)
            freqs = jnp.outer(t, inv_freq)
            return (jnp.cos(freqs), jnp.sin(freqs))

        def _apply_rope(x, cos, sin):
            d2 = x.shape[-1] // 2
            x1, x2 = (x[..., :d2], x[..., d2:])
            c = cos[None, :, None, :]
            s = sin[None, :, None, :]
            return jnp.concatenate([x1 * c - x2 * s, x1 * s + x2 * c], axis=-1)
        key = jax.random.key(seed)
        k1, k2, k3 = jax.random.split(key, 3)
        hidden_states = jax.random.normal(k1, (B, S, H), dtype=jnp.float32)
        Wqkv = jax.random.normal(k2, ((N_HEADS + 2 * N_KV) * HEAD_DIM, H), dtype=jnp.float32) * 0.02
        Wo = jax.random.normal(k3, (H, N_HEADS * HEAD_DIM), dtype=jnp.float32) * 0.02
        return {'hidden_states': hidden_states, 'Wqkv': Wqkv, 'Wo': Wo}
    _L0_attn_all = _L0_attn_setup()
    _L0_attn_in = {k: v for k, v in _L0_attn_all.items() if k in ('Wqkv', 'Wo')}
    del _L0_attn_all

    def _L0_cond2_setup():
        import jax, jax.numpy as jnp
        from jax import lax
        import numpy as np
        CIN, COUT, K, STYLE_DIM = (32, 32, 3, 64)
        N_LAYERS = 4
        TYPES = ('same', 'upsample', 'same', 'downsample')
        SCALE = 1.0 / float(np.sqrt(CIN * K ** 2))
        EPS = 1e-08
        _BK = np.array([1.0, 3.0, 3.0, 1.0], dtype=np.float32)
        BLUR_K = _BK / _BK.sum()

        def _blur(x, kern, pad):
            B, C, _ = x.shape
            xp = jnp.pad(x, ((0, 0), (0, 0), (pad[0], pad[1])))
            w = jnp.broadcast_to(kern.astype(x.dtype)[None, None, :], (C, 1, kern.shape[0]))
            return lax.conv_general_dilated(xp, w, (1,), 'VALID', feature_group_count=C, dimension_numbers=('NCH', 'OIH', 'NCH'))

        def _conv_same(x, w):
            p = (K - 1) // 2
            return lax.conv_general_dilated(x[None], w, (1,), [(p, p)], dimension_numbers=('NCH', 'OIH', 'NCH'))[0]

        def _conv_down(x, w):
            return lax.conv_general_dilated(x[None], w, (2,), 'VALID', dimension_numbers=('NCH', 'OIH', 'NCH'))[0]

        def _conv_up(x, w_t):
            return lax.conv_transpose(x[None], w_t, (2,), 'VALID', dimension_numbers=('NCH', 'IOH', 'NCH'), transpose_kernel=True)[0]

        def _layer(x, style, w, b, mw, mb, typ):
            s = style @ mw.T + mb
            weight = SCALE * w * s[:, None, :, None]
            demod = lax.rsqrt(jnp.sum(weight * weight, axis=(2, 3)) + EPS)
            weight = weight * demod[:, :, None, None]
            blur_k = jnp.asarray(BLUR_K)
            if typ == 'same':
                out = jax.vmap(_conv_same)(x, weight) + b[None, :, None]
            elif typ == 'upsample':
                out = jax.vmap(_conv_up)(x, weight.transpose(0, 2, 1, 3)) + b[None, :, None]
                out = _blur(out, 2.0 * blur_k, (1, 1))
            elif typ == 'downsample':
                xb = _blur(x, blur_k, (2, 2))
                out = jax.vmap(_conv_down)(xb, weight) + b[None, :, None]
            else:
                raise NotImplementedError(typ)
            return out
        key = jax.random.key(seed)
        ks = jax.random.split(key, 6)
        B, L = (16, 512)
        return {'x': jax.random.normal(ks[0], (B, CIN, L), dtype=jnp.float32), 'style': jax.random.normal(ks[1], (B, STYLE_DIM), dtype=jnp.float32), 'weights': jax.random.normal(ks[2], (N_LAYERS, COUT, CIN, K), dtype=jnp.float32), 'biases': jax.random.normal(ks[3], (N_LAYERS, COUT), dtype=jnp.float32) * 0.1, 'mod_w': jax.random.normal(ks[4], (N_LAYERS, CIN, STYLE_DIM), dtype=jnp.float32) / np.sqrt(STYLE_DIM), 'mod_b': 1.0 + 0.1 * jax.random.normal(ks[5], (N_LAYERS, CIN), dtype=jnp.float32)}
    _L0_cond2_all = _L0_cond2_setup()
    _L0_cond2_in = {k: v for k, v in _L0_cond2_all.items() if k in ('weights', 'biases', 'mod_w', 'mod_b')}
    del _L0_cond2_all

    def _L0_ffn_setup():
        import jax, jax.numpy as jnp
        import numpy as np
        B, S, IN, OUT = (4, 256, 512, 512)
        E, K, R = (8, 2, 16)
        CAP_FACTOR = 3.0
        ALPHA = 1.0 / R
        LN_EPS = 1e-05
        key = jax.random.key(seed)
        ks = jax.random.split(key, 6)
        return {'x': jax.random.normal(ks[0], (B, S, IN), dtype=jnp.float32), 'weight': jax.random.normal(ks[1], (OUT, IN), dtype=jnp.float32) * 0.02, 'lora_A': jax.random.normal(ks[2], (E, IN, R), dtype=jnp.float32) / np.sqrt(R), 'lora_B': jax.random.normal(ks[3], (E, R, OUT), dtype=jnp.float32) * 0.02, 'gw1': jax.random.normal(ks[4], (4 * E, IN), dtype=jnp.float32) * 0.02, 'gb1': jnp.zeros((4 * E,), dtype=jnp.float32), 'ln_gamma': jnp.ones((4 * E,), dtype=jnp.float32), 'ln_beta': jnp.zeros((4 * E,), dtype=jnp.float32), 'gw2': jax.random.normal(ks[5], (E, 4 * E), dtype=jnp.float32) * 0.02, 'gb2': jnp.zeros((E,), dtype=jnp.float32)}
    _L0_ffn_all = _L0_ffn_setup()
    _L0_ffn_in = {k: v for k, v in _L0_ffn_all.items() if k in ('weight', 'lora_A', 'lora_B', 'gw1', 'gb1', 'ln_gamma', 'ln_beta', 'gw2', 'gb2')}
    del _L0_ffn_all

    def _L1_cond_setup():
        import jax, jax.numpy as jnp
        from jax import lax
        import numpy as np
        CIN, COUT, K, STYLE_DIM = (32, 32, 3, 64)
        N_LAYERS = 4
        TYPES = ('same', 'upsample', 'same', 'downsample')
        SCALE = 1.0 / float(np.sqrt(CIN * K ** 2))
        EPS = 1e-08
        _BK = np.array([1.0, 3.0, 3.0, 1.0], dtype=np.float32)
        BLUR_K = _BK / _BK.sum()

        def _blur(x, kern, pad):
            B, C, _ = x.shape
            xp = jnp.pad(x, ((0, 0), (0, 0), (pad[0], pad[1])))
            w = jnp.broadcast_to(kern.astype(x.dtype)[None, None, :], (C, 1, kern.shape[0]))
            return lax.conv_general_dilated(xp, w, (1,), 'VALID', feature_group_count=C, dimension_numbers=('NCH', 'OIH', 'NCH'))

        def _conv_same(x, w):
            p = (K - 1) // 2
            return lax.conv_general_dilated(x[None], w, (1,), [(p, p)], dimension_numbers=('NCH', 'OIH', 'NCH'))[0]

        def _conv_down(x, w):
            return lax.conv_general_dilated(x[None], w, (2,), 'VALID', dimension_numbers=('NCH', 'OIH', 'NCH'))[0]

        def _conv_up(x, w_t):
            return lax.conv_transpose(x[None], w_t, (2,), 'VALID', dimension_numbers=('NCH', 'IOH', 'NCH'), transpose_kernel=True)[0]

        def _layer(x, style, w, b, mw, mb, typ):
            s = style @ mw.T + mb
            weight = SCALE * w * s[:, None, :, None]
            demod = lax.rsqrt(jnp.sum(weight * weight, axis=(2, 3)) + EPS)
            weight = weight * demod[:, :, None, None]
            blur_k = jnp.asarray(BLUR_K)
            if typ == 'same':
                out = jax.vmap(_conv_same)(x, weight) + b[None, :, None]
            elif typ == 'upsample':
                out = jax.vmap(_conv_up)(x, weight.transpose(0, 2, 1, 3)) + b[None, :, None]
                out = _blur(out, 2.0 * blur_k, (1, 1))
            elif typ == 'downsample':
                xb = _blur(x, blur_k, (2, 2))
                out = jax.vmap(_conv_down)(xb, weight) + b[None, :, None]
            else:
                raise NotImplementedError(typ)
            return out
        key = jax.random.key(seed)
        ks = jax.random.split(key, 6)
        B, L = (16, 512)
        return {'x': jax.random.normal(ks[0], (B, CIN, L), dtype=jnp.float32), 'style': jax.random.normal(ks[1], (B, STYLE_DIM), dtype=jnp.float32), 'weights': jax.random.normal(ks[2], (N_LAYERS, COUT, CIN, K), dtype=jnp.float32), 'biases': jax.random.normal(ks[3], (N_LAYERS, COUT), dtype=jnp.float32) * 0.1, 'mod_w': jax.random.normal(ks[4], (N_LAYERS, CIN, STYLE_DIM), dtype=jnp.float32) / np.sqrt(STYLE_DIM), 'mod_b': 1.0 + 0.1 * jax.random.normal(ks[5], (N_LAYERS, CIN), dtype=jnp.float32)}
    _L1_cond_all = _L1_cond_setup()
    _L1_cond_in = {k: v for k, v in _L1_cond_all.items() if k in ('weights', 'biases', 'mod_w', 'mod_b')}
    del _L1_cond_all

    def _L1_attn_setup():
        import math
        import jax, jax.numpy as jnp
        import numpy as np
        H = 32
        NOPE = 64
        ROPE = 64
        VD = 128
        QHD = NOPE + ROPE
        KVR = 32
        EPS = 1e-06

        def _yarn_cos_sin(seq_len, dim=ROPE, base=10000.0, factor=128.0, beta_fast=32.0, beta_slow=1.0, orig_max=1024, mscale=1.0, mscale_all_dim=1.0):

            def corr_dim(r):
                return dim * math.log(orig_max / (r * 2 * math.pi)) / (2 * math.log(base))
            low = max(math.floor(corr_dim(beta_fast)), 0)
            high = min(math.ceil(corr_dim(beta_slow)), dim - 1)
            hi = high + 0.001 if low == high else float(high)
            ramp = np.clip((np.arange(dim // 2, dtype=np.float32) - low) / (hi - low), 0.0, 1.0)
            inv_freq_mask = 1.0 - ramp
            freq_extra = 1.0 / base ** (np.arange(0, dim, 2, dtype=np.float32) / dim)
            freq_inter = freq_extra / factor
            inv_freq = freq_inter * (1.0 - inv_freq_mask) + freq_extra * inv_freq_mask
            t = np.arange(seq_len, dtype=np.float32)
            freqs = np.outer(t, inv_freq)
            emb = np.concatenate([freqs, freqs], axis=-1)

            def gm(s, m):
                return 1.0 if s <= 1 else 0.1 * m * math.log(s) + 1.0
            ms = gm(factor, mscale) / gm(factor, mscale_all_dim)
            return (jnp.asarray(np.cos(emb) * ms), jnp.asarray(np.sin(emb) * ms))

        def _rmsnorm(x, w, eps=EPS):
            var = jnp.mean(jnp.square(x), axis=-1, keepdims=True)
            return x * jax.lax.rsqrt(var + eps) * w

        def _deinterleave(x):
            d = x.shape[-1]
            x = x.reshape(*x.shape[:-1], d // 2, 2)
            return jnp.concatenate([x[..., 0], x[..., 1]], axis=-1)

        def _rotate_half(x):
            d = x.shape[-1] // 2
            return jnp.concatenate([-x[..., d:], x[..., :d]], axis=-1)

        def _apply_rope(x, cos, sin):
            return x * cos + _rotate_half(x) * sin
        key = jax.random.key(seed)
        ks = jax.random.split(key, 6)
        B, S, D = (1, 256, 512)
        std = 0.02
        return {'x': jax.random.normal(ks[0], (B, S, D), dtype=jnp.float32), 'wq_a': jax.random.normal(ks[1], (128, D), dtype=jnp.float32) * std, 'q_a_ln_w': jnp.ones((128,), dtype=jnp.float32), 'wq_b': jax.random.normal(ks[2], (H * QHD, 128), dtype=jnp.float32) * std, 'wkv_a': jax.random.normal(ks[3], (KVR + ROPE, D), dtype=jnp.float32) * std, 'kv_a_ln_w': jnp.ones((KVR,), dtype=jnp.float32), 'wkv_b': jax.random.normal(ks[4], (H * (NOPE + VD), KVR), dtype=jnp.float32) * std, 'wo': jax.random.normal(ks[5], (D, H * VD), dtype=jnp.float32) * std}
    _L1_attn_all = _L1_attn_setup()
    _L1_attn_in = {k: v for k, v in _L1_attn_all.items() if k in ('wq_a', 'q_a_ln_w', 'wq_b', 'wkv_a', 'kv_a_ln_w', 'wkv_b', 'wo')}
    del _L1_attn_all

    def _L1_cond2_setup():
        import jax, jax.numpy as jnp
        from jax import lax
        import numpy as np
        CIN, COUT, K, STYLE_DIM = (32, 32, 3, 64)
        N_LAYERS = 4
        TYPES = ('same', 'upsample', 'same', 'downsample')
        SCALE = 1.0 / float(np.sqrt(CIN * K ** 2))
        EPS = 1e-08
        _BK = np.array([1.0, 3.0, 3.0, 1.0], dtype=np.float32)
        BLUR_K = _BK / _BK.sum()

        def _blur(x, kern, pad):
            B, C, _ = x.shape
            xp = jnp.pad(x, ((0, 0), (0, 0), (pad[0], pad[1])))
            w = jnp.broadcast_to(kern.astype(x.dtype)[None, None, :], (C, 1, kern.shape[0]))
            return lax.conv_general_dilated(xp, w, (1,), 'VALID', feature_group_count=C, dimension_numbers=('NCH', 'OIH', 'NCH'))

        def _conv_same(x, w):
            p = (K - 1) // 2
            return lax.conv_general_dilated(x[None], w, (1,), [(p, p)], dimension_numbers=('NCH', 'OIH', 'NCH'))[0]

        def _conv_down(x, w):
            return lax.conv_general_dilated(x[None], w, (2,), 'VALID', dimension_numbers=('NCH', 'OIH', 'NCH'))[0]

        def _conv_up(x, w_t):
            return lax.conv_transpose(x[None], w_t, (2,), 'VALID', dimension_numbers=('NCH', 'IOH', 'NCH'), transpose_kernel=True)[0]

        def _layer(x, style, w, b, mw, mb, typ):
            s = style @ mw.T + mb
            weight = SCALE * w * s[:, None, :, None]
            demod = lax.rsqrt(jnp.sum(weight * weight, axis=(2, 3)) + EPS)
            weight = weight * demod[:, :, None, None]
            blur_k = jnp.asarray(BLUR_K)
            if typ == 'same':
                out = jax.vmap(_conv_same)(x, weight) + b[None, :, None]
            elif typ == 'upsample':
                out = jax.vmap(_conv_up)(x, weight.transpose(0, 2, 1, 3)) + b[None, :, None]
                out = _blur(out, 2.0 * blur_k, (1, 1))
            elif typ == 'downsample':
                xb = _blur(x, blur_k, (2, 2))
                out = jax.vmap(_conv_down)(xb, weight) + b[None, :, None]
            else:
                raise NotImplementedError(typ)
            return out
        key = jax.random.key(seed)
        ks = jax.random.split(key, 6)
        B, L = (16, 512)
        return {'x': jax.random.normal(ks[0], (B, CIN, L), dtype=jnp.float32), 'style': jax.random.normal(ks[1], (B, STYLE_DIM), dtype=jnp.float32), 'weights': jax.random.normal(ks[2], (N_LAYERS, COUT, CIN, K), dtype=jnp.float32), 'biases': jax.random.normal(ks[3], (N_LAYERS, COUT), dtype=jnp.float32) * 0.1, 'mod_w': jax.random.normal(ks[4], (N_LAYERS, CIN, STYLE_DIM), dtype=jnp.float32) / np.sqrt(STYLE_DIM), 'mod_b': 1.0 + 0.1 * jax.random.normal(ks[5], (N_LAYERS, CIN), dtype=jnp.float32)}
    _L1_cond2_all = _L1_cond2_setup()
    _L1_cond2_in = {k: v for k, v in _L1_cond2_all.items() if k in ('weights', 'biases', 'mod_w', 'mod_b')}
    del _L1_cond2_all

    def _L1_ffn_setup():
        import jax, jax.numpy as jnp
        import numpy as np
        R = 16
        NUM_EXPERTS = 8
        TOP_K = 2
        LORA_ALPHA = 32
        SCALING = LORA_ALPHA / R
        key = jax.random.key(seed)
        ks = jax.random.split(key, 6)
        d_in, d_out = (512, 512)
        x = jax.random.normal(ks[0], (4, 256, d_in), dtype=jnp.float32)
        W_base = jax.random.normal(ks[1], (d_out, d_in), dtype=jnp.float32) * 0.02
        b_base = jax.random.normal(ks[2], (d_out,), dtype=jnp.float32) * 0.02
        W_router = jax.random.normal(ks[3], (NUM_EXPERTS, d_in), dtype=jnp.float32) * 0.01
        A = jax.random.normal(ks[4], (NUM_EXPERTS, R, d_in), dtype=jnp.float32) * 0.02
        B = jax.random.normal(ks[5], (NUM_EXPERTS, d_out, R), dtype=jnp.float32) * 0.02
        return {'x': x, 'W_base': W_base, 'b_base': b_base, 'W_router': W_router, 'A': A, 'B': B}
    _L1_ffn_all = _L1_ffn_setup()
    _L1_ffn_in = {k: v for k, v in _L1_ffn_all.items() if k in ('W_base', 'b_base', 'W_router', 'A', 'B')}
    del _L1_ffn_all
    return {'x': x, 'cond_512': cond_512, 'L0_cond_weights': _L0_cond_in['weights'], 'L0_cond_biases': _L0_cond_in['biases'], 'L0_cond_mod_w': _L0_cond_in['mod_w'], 'L0_cond_mod_b': _L0_cond_in['mod_b'], 'L0_attn_Wqkv': _L0_attn_in['Wqkv'], 'L0_attn_Wo': _L0_attn_in['Wo'], 'L0_cond2_weights': _L0_cond2_in['weights'], 'L0_cond2_biases': _L0_cond2_in['biases'], 'L0_cond2_mod_w': _L0_cond2_in['mod_w'], 'L0_cond2_mod_b': _L0_cond2_in['mod_b'], 'L0_ffn_weight': _L0_ffn_in['weight'], 'L0_ffn_lora_A': _L0_ffn_in['lora_A'], 'L0_ffn_lora_B': _L0_ffn_in['lora_B'], 'L0_ffn_gw1': _L0_ffn_in['gw1'], 'L0_ffn_gb1': _L0_ffn_in['gb1'], 'L0_ffn_ln_gamma': _L0_ffn_in['ln_gamma'], 'L0_ffn_ln_beta': _L0_ffn_in['ln_beta'], 'L0_ffn_gw2': _L0_ffn_in['gw2'], 'L0_ffn_gb2': _L0_ffn_in['gb2'], 'L1_cond_weights': _L1_cond_in['weights'], 'L1_cond_biases': _L1_cond_in['biases'], 'L1_cond_mod_w': _L1_cond_in['mod_w'], 'L1_cond_mod_b': _L1_cond_in['mod_b'], 'L1_attn_wq_a': _L1_attn_in['wq_a'], 'L1_attn_q_a_ln_w': _L1_attn_in['q_a_ln_w'], 'L1_attn_wq_b': _L1_attn_in['wq_b'], 'L1_attn_wkv_a': _L1_attn_in['wkv_a'], 'L1_attn_kv_a_ln_w': _L1_attn_in['kv_a_ln_w'], 'L1_attn_wkv_b': _L1_attn_in['wkv_b'], 'L1_attn_wo': _L1_attn_in['wo'], 'L1_cond2_weights': _L1_cond2_in['weights'], 'L1_cond2_biases': _L1_cond2_in['biases'], 'L1_cond2_mod_w': _L1_cond2_in['mod_w'], 'L1_cond2_mod_b': _L1_cond2_in['mod_b'], 'L1_ffn_W_base': _L1_ffn_in['W_base'], 'L1_ffn_b_base': _L1_ffn_in['b_base'], 'L1_ffn_W_router': _L1_ffn_in['W_router'], 'L1_ffn_A': _L1_ffn_in['A'], 'L1_ffn_B': _L1_ffn_in['B']}

def reference(x, cond_512, L0_cond_weights, L0_cond_biases, L0_cond_mod_w, L0_cond_mod_b, L0_attn_Wqkv, L0_attn_Wo, L0_cond2_weights, L0_cond2_biases, L0_cond2_mod_w, L0_cond2_mod_b, L0_ffn_weight, L0_ffn_lora_A, L0_ffn_lora_B, L0_ffn_gw1, L0_ffn_gb1, L0_ffn_ln_gamma, L0_ffn_ln_beta, L0_ffn_gw2, L0_ffn_gb2, L1_cond_weights, L1_cond_biases, L1_cond_mod_w, L1_cond_mod_b, L1_attn_wq_a, L1_attn_q_a_ln_w, L1_attn_wq_b, L1_attn_wkv_a, L1_attn_kv_a_ln_w, L1_attn_wkv_b, L1_attn_wo, L1_cond2_weights, L1_cond2_biases, L1_cond2_mod_w, L1_cond2_mod_b, L1_ffn_W_base, L1_ffn_b_base, L1_ffn_W_router, L1_ffn_A, L1_ffn_B):
    import jax
    import jax.numpy as jnp

    def _L0_cond_ref(x, style, weights, biases, mod_w, mod_b):
        import jax, jax.numpy as jnp
        from jax import lax
        import numpy as np
        CIN, COUT, K, STYLE_DIM = (32, 32, 3, 64)
        N_LAYERS = 4
        TYPES = ('same', 'upsample', 'same', 'downsample')
        SCALE = 1.0 / float(np.sqrt(CIN * K ** 2))
        EPS = 1e-08
        _BK = np.array([1.0, 3.0, 3.0, 1.0], dtype=np.float32)
        BLUR_K = _BK / _BK.sum()

        def _blur(x, kern, pad):
            B, C, _ = x.shape
            xp = jnp.pad(x, ((0, 0), (0, 0), (pad[0], pad[1])))
            w = jnp.broadcast_to(kern.astype(x.dtype)[None, None, :], (C, 1, kern.shape[0]))
            return lax.conv_general_dilated(xp, w, (1,), 'VALID', feature_group_count=C, dimension_numbers=('NCH', 'OIH', 'NCH'))

        def _conv_same(x, w):
            p = (K - 1) // 2
            return lax.conv_general_dilated(x[None], w, (1,), [(p, p)], dimension_numbers=('NCH', 'OIH', 'NCH'))[0]

        def _conv_down(x, w):
            return lax.conv_general_dilated(x[None], w, (2,), 'VALID', dimension_numbers=('NCH', 'OIH', 'NCH'))[0]

        def _conv_up(x, w_t):
            return lax.conv_transpose(x[None], w_t, (2,), 'VALID', dimension_numbers=('NCH', 'IOH', 'NCH'), transpose_kernel=True)[0]

        def _layer(x, style, w, b, mw, mb, typ):
            s = style @ mw.T + mb
            weight = SCALE * w * s[:, None, :, None]
            demod = lax.rsqrt(jnp.sum(weight * weight, axis=(2, 3)) + EPS)
            weight = weight * demod[:, :, None, None]
            blur_k = jnp.asarray(BLUR_K)
            if typ == 'same':
                out = jax.vmap(_conv_same)(x, weight) + b[None, :, None]
            elif typ == 'upsample':
                out = jax.vmap(_conv_up)(x, weight.transpose(0, 2, 1, 3)) + b[None, :, None]
                out = _blur(out, 2.0 * blur_k, (1, 1))
            elif typ == 'downsample':
                xb = _blur(x, blur_k, (2, 2))
                out = jax.vmap(_conv_down)(xb, weight) + b[None, :, None]
            else:
                raise NotImplementedError(typ)
            return out
        out = x
        for i, typ in enumerate(TYPES):
            out = _layer(out, style, weights[i], biases[i], mod_w[i], mod_b[i], typ)
        return out

    def _L0_attn_ref(hidden_states, Wqkv, Wo):
        import jax, jax.numpy as jnp
        import numpy as np
        B, S, H = (1, 256, 512)
        N_HEADS, N_KV, HEAD_DIM = (32, 8, 128)
        ROPE_THETA = 10000.0

        def _rope_tables(seqlen, dim, theta):
            inv_freq = 1.0 / theta ** (jnp.arange(0, dim, 2, dtype=jnp.float32) / dim)
            t = jnp.arange(seqlen, dtype=jnp.float32)
            freqs = jnp.outer(t, inv_freq)
            return (jnp.cos(freqs), jnp.sin(freqs))

        def _apply_rope(x, cos, sin):
            d2 = x.shape[-1] // 2
            x1, x2 = (x[..., :d2], x[..., d2:])
            c = cos[None, :, None, :]
            s = sin[None, :, None, :]
            return jnp.concatenate([x1 * c - x2 * s, x1 * s + x2 * c], axis=-1)
        b, s, h = hidden_states.shape
        qkv = jnp.einsum('bsh,oh->bso', hidden_states, Wqkv)
        q_end = N_HEADS * HEAD_DIM
        k_end = q_end + N_KV * HEAD_DIM
        xq = qkv[..., :q_end].reshape(b, s, N_HEADS, HEAD_DIM)
        xk = qkv[..., q_end:k_end].reshape(b, s, N_KV, HEAD_DIM)
        xv = qkv[..., k_end:].reshape(b, s, N_KV, HEAD_DIM)
        cos, sin = _rope_tables(s, HEAD_DIM, ROPE_THETA)
        xq = _apply_rope(xq, cos, sin)
        xk = _apply_rope(xk, cos, sin)
        groups = N_HEADS // N_KV
        xk = jnp.repeat(xk, groups, axis=2)
        xv = jnp.repeat(xv, groups, axis=2)
        scale = 1.0 / jnp.sqrt(jnp.float32(HEAD_DIM))
        scores = jnp.einsum('bqhd,bkhd->bhqk', xq, xk) * scale
        causal = jnp.tril(jnp.ones((s, s), dtype=bool))
        scores = jnp.where(causal[None, None, :, :], scores, jnp.float32(-1e+30))
        probs = jax.nn.softmax(scores, axis=-1)
        out = jnp.einsum('bhqk,bkhd->bqhd', probs, xv).reshape(b, s, N_HEADS * HEAD_DIM)
        attn_output = jnp.einsum('bsd,hd->bsh', out, Wo)
        return attn_output

    def _L0_cond2_ref(x, style, weights, biases, mod_w, mod_b):
        import jax, jax.numpy as jnp
        from jax import lax
        import numpy as np
        CIN, COUT, K, STYLE_DIM = (32, 32, 3, 64)
        N_LAYERS = 4
        TYPES = ('same', 'upsample', 'same', 'downsample')
        SCALE = 1.0 / float(np.sqrt(CIN * K ** 2))
        EPS = 1e-08
        _BK = np.array([1.0, 3.0, 3.0, 1.0], dtype=np.float32)
        BLUR_K = _BK / _BK.sum()

        def _blur(x, kern, pad):
            B, C, _ = x.shape
            xp = jnp.pad(x, ((0, 0), (0, 0), (pad[0], pad[1])))
            w = jnp.broadcast_to(kern.astype(x.dtype)[None, None, :], (C, 1, kern.shape[0]))
            return lax.conv_general_dilated(xp, w, (1,), 'VALID', feature_group_count=C, dimension_numbers=('NCH', 'OIH', 'NCH'))

        def _conv_same(x, w):
            p = (K - 1) // 2
            return lax.conv_general_dilated(x[None], w, (1,), [(p, p)], dimension_numbers=('NCH', 'OIH', 'NCH'))[0]

        def _conv_down(x, w):
            return lax.conv_general_dilated(x[None], w, (2,), 'VALID', dimension_numbers=('NCH', 'OIH', 'NCH'))[0]

        def _conv_up(x, w_t):
            return lax.conv_transpose(x[None], w_t, (2,), 'VALID', dimension_numbers=('NCH', 'IOH', 'NCH'), transpose_kernel=True)[0]

        def _layer(x, style, w, b, mw, mb, typ):
            s = style @ mw.T + mb
            weight = SCALE * w * s[:, None, :, None]
            demod = lax.rsqrt(jnp.sum(weight * weight, axis=(2, 3)) + EPS)
            weight = weight * demod[:, :, None, None]
            blur_k = jnp.asarray(BLUR_K)
            if typ == 'same':
                out = jax.vmap(_conv_same)(x, weight) + b[None, :, None]
            elif typ == 'upsample':
                out = jax.vmap(_conv_up)(x, weight.transpose(0, 2, 1, 3)) + b[None, :, None]
                out = _blur(out, 2.0 * blur_k, (1, 1))
            elif typ == 'downsample':
                xb = _blur(x, blur_k, (2, 2))
                out = jax.vmap(_conv_down)(xb, weight) + b[None, :, None]
            else:
                raise NotImplementedError(typ)
            return out
        out = x
        for i, typ in enumerate(TYPES):
            out = _layer(out, style, weights[i], biases[i], mod_w[i], mod_b[i], typ)
        return out

    def _L0_ffn_ref(x, weight, lora_A, lora_B, gw1, gb1, ln_gamma, ln_beta, gw2, gb2):
        import jax, jax.numpy as jnp
        import numpy as np
        B, S, IN, OUT = (4, 256, 512, 512)
        E, K, R = (8, 2, 16)
        CAP_FACTOR = 3.0
        ALPHA = 1.0 / R
        LN_EPS = 1e-05
        orig_shape = x.shape
        xf = x.reshape(-1, orig_shape[-1])
        N = xf.shape[0]
        capacity = int(CAP_FACTOR * N / E)
        h = xf @ gw1.T + gb1
        mu = jnp.mean(h, axis=-1, keepdims=True)
        var = jnp.mean((h - mu) ** 2, axis=-1, keepdims=True)
        h = (h - mu) * jax.lax.rsqrt(var + LN_EPS) * ln_gamma + ln_beta
        h = jax.nn.relu(h)
        gates = h @ gw2.T + gb2
        top_v, top_i = jax.lax.top_k(gates, K)
        top_g = jax.nn.softmax(top_v, axis=-1)
        onehot = (top_i[..., None] == jnp.arange(E)).astype(xf.dtype)
        counts = onehot.sum(axis=0)
        allowed = (counts <= capacity).astype(xf.dtype)
        w = jnp.einsum('nke,nk,ke->ne', onehot, top_g, allowed)
        main = xf @ weight.T
        tmp = jnp.einsum('ni,eir->enr', xf, lora_A)
        tmp = tmp * w.T[:, :, None]
        lora = jnp.einsum('enr,ero->no', tmp, lora_B) * ALPHA
        out = main + lora
        return out.reshape(*orig_shape[:-1], weight.shape[0])

    def _L1_cond_ref(x, style, weights, biases, mod_w, mod_b):
        import jax, jax.numpy as jnp
        from jax import lax
        import numpy as np
        CIN, COUT, K, STYLE_DIM = (32, 32, 3, 64)
        N_LAYERS = 4
        TYPES = ('same', 'upsample', 'same', 'downsample')
        SCALE = 1.0 / float(np.sqrt(CIN * K ** 2))
        EPS = 1e-08
        _BK = np.array([1.0, 3.0, 3.0, 1.0], dtype=np.float32)
        BLUR_K = _BK / _BK.sum()

        def _blur(x, kern, pad):
            B, C, _ = x.shape
            xp = jnp.pad(x, ((0, 0), (0, 0), (pad[0], pad[1])))
            w = jnp.broadcast_to(kern.astype(x.dtype)[None, None, :], (C, 1, kern.shape[0]))
            return lax.conv_general_dilated(xp, w, (1,), 'VALID', feature_group_count=C, dimension_numbers=('NCH', 'OIH', 'NCH'))

        def _conv_same(x, w):
            p = (K - 1) // 2
            return lax.conv_general_dilated(x[None], w, (1,), [(p, p)], dimension_numbers=('NCH', 'OIH', 'NCH'))[0]

        def _conv_down(x, w):
            return lax.conv_general_dilated(x[None], w, (2,), 'VALID', dimension_numbers=('NCH', 'OIH', 'NCH'))[0]

        def _conv_up(x, w_t):
            return lax.conv_transpose(x[None], w_t, (2,), 'VALID', dimension_numbers=('NCH', 'IOH', 'NCH'), transpose_kernel=True)[0]

        def _layer(x, style, w, b, mw, mb, typ):
            s = style @ mw.T + mb
            weight = SCALE * w * s[:, None, :, None]
            demod = lax.rsqrt(jnp.sum(weight * weight, axis=(2, 3)) + EPS)
            weight = weight * demod[:, :, None, None]
            blur_k = jnp.asarray(BLUR_K)
            if typ == 'same':
                out = jax.vmap(_conv_same)(x, weight) + b[None, :, None]
            elif typ == 'upsample':
                out = jax.vmap(_conv_up)(x, weight.transpose(0, 2, 1, 3)) + b[None, :, None]
                out = _blur(out, 2.0 * blur_k, (1, 1))
            elif typ == 'downsample':
                xb = _blur(x, blur_k, (2, 2))
                out = jax.vmap(_conv_down)(xb, weight) + b[None, :, None]
            else:
                raise NotImplementedError(typ)
            return out
        out = x
        for i, typ in enumerate(TYPES):
            out = _layer(out, style, weights[i], biases[i], mod_w[i], mod_b[i], typ)
        return out

    def _L1_attn_ref(x, wq_a, q_a_ln_w, wq_b, wkv_a, kv_a_ln_w, wkv_b, wo):
        import math
        import jax, jax.numpy as jnp
        import numpy as np
        H = 32
        NOPE = 64
        ROPE = 64
        VD = 128
        QHD = NOPE + ROPE
        KVR = 32
        EPS = 1e-06

        def _yarn_cos_sin(seq_len, dim=ROPE, base=10000.0, factor=128.0, beta_fast=32.0, beta_slow=1.0, orig_max=1024, mscale=1.0, mscale_all_dim=1.0):

            def corr_dim(r):
                return dim * math.log(orig_max / (r * 2 * math.pi)) / (2 * math.log(base))
            low = max(math.floor(corr_dim(beta_fast)), 0)
            high = min(math.ceil(corr_dim(beta_slow)), dim - 1)
            hi = high + 0.001 if low == high else float(high)
            ramp = np.clip((np.arange(dim // 2, dtype=np.float32) - low) / (hi - low), 0.0, 1.0)
            inv_freq_mask = 1.0 - ramp
            freq_extra = 1.0 / base ** (np.arange(0, dim, 2, dtype=np.float32) / dim)
            freq_inter = freq_extra / factor
            inv_freq = freq_inter * (1.0 - inv_freq_mask) + freq_extra * inv_freq_mask
            t = np.arange(seq_len, dtype=np.float32)
            freqs = np.outer(t, inv_freq)
            emb = np.concatenate([freqs, freqs], axis=-1)

            def gm(s, m):
                return 1.0 if s <= 1 else 0.1 * m * math.log(s) + 1.0
            ms = gm(factor, mscale) / gm(factor, mscale_all_dim)
            return (jnp.asarray(np.cos(emb) * ms), jnp.asarray(np.sin(emb) * ms))

        def _rmsnorm(x, w, eps=EPS):
            var = jnp.mean(jnp.square(x), axis=-1, keepdims=True)
            return x * jax.lax.rsqrt(var + eps) * w

        def _deinterleave(x):
            d = x.shape[-1]
            x = x.reshape(*x.shape[:-1], d // 2, 2)
            return jnp.concatenate([x[..., 0], x[..., 1]], axis=-1)

        def _rotate_half(x):
            d = x.shape[-1] // 2
            return jnp.concatenate([-x[..., d:], x[..., :d]], axis=-1)

        def _apply_rope(x, cos, sin):
            return x * cos + _rotate_half(x) * sin
        B, S, D = x.shape
        m = 0.1 * 1.0 * math.log(128.0) + 1.0
        softmax_scale = QHD ** (-0.5) * m * m
        q = _rmsnorm(x @ wq_a.T, q_a_ln_w) @ wq_b.T
        q = q.reshape(B, S, H, QHD)
        q_nope, q_pe = (q[..., :NOPE], q[..., NOPE:])
        ckv_kpe = x @ wkv_a.T
        ckv, k_pe = (ckv_kpe[..., :KVR], ckv_kpe[..., KVR:])
        kv = _rmsnorm(ckv, kv_a_ln_w) @ wkv_b.T
        kv = kv.reshape(B, S, H, NOPE + VD)
        k_nope, v = (kv[..., :NOPE], kv[..., NOPE:])
        cos, sin = _yarn_cos_sin(S)
        q_pe = _apply_rope(_deinterleave(q_pe), cos[None, :, None, :], sin[None, :, None, :])
        k_pe = _apply_rope(_deinterleave(k_pe), cos[None, :, :], sin[None, :, :])
        q_full = jnp.concatenate([q_nope, q_pe], axis=-1)
        k_full = jnp.concatenate([k_nope, jnp.broadcast_to(k_pe[:, :, None, :], (B, S, H, ROPE))], axis=-1)
        scores = jnp.einsum('bqhd,bkhd->bhqk', q_full, k_full) * softmax_scale
        causal = jnp.tril(jnp.ones((S, S), dtype=bool))
        scores = jnp.where(causal[None, None], scores, jnp.finfo(scores.dtype).min)
        attn = jax.nn.softmax(scores, axis=-1)
        out = jnp.einsum('bhqk,bkhd->bqhd', attn, v).reshape(B, S, H * VD)
        return out @ wo.T

    def _L1_cond2_ref(x, style, weights, biases, mod_w, mod_b):
        import jax, jax.numpy as jnp
        from jax import lax
        import numpy as np
        CIN, COUT, K, STYLE_DIM = (32, 32, 3, 64)
        N_LAYERS = 4
        TYPES = ('same', 'upsample', 'same', 'downsample')
        SCALE = 1.0 / float(np.sqrt(CIN * K ** 2))
        EPS = 1e-08
        _BK = np.array([1.0, 3.0, 3.0, 1.0], dtype=np.float32)
        BLUR_K = _BK / _BK.sum()

        def _blur(x, kern, pad):
            B, C, _ = x.shape
            xp = jnp.pad(x, ((0, 0), (0, 0), (pad[0], pad[1])))
            w = jnp.broadcast_to(kern.astype(x.dtype)[None, None, :], (C, 1, kern.shape[0]))
            return lax.conv_general_dilated(xp, w, (1,), 'VALID', feature_group_count=C, dimension_numbers=('NCH', 'OIH', 'NCH'))

        def _conv_same(x, w):
            p = (K - 1) // 2
            return lax.conv_general_dilated(x[None], w, (1,), [(p, p)], dimension_numbers=('NCH', 'OIH', 'NCH'))[0]

        def _conv_down(x, w):
            return lax.conv_general_dilated(x[None], w, (2,), 'VALID', dimension_numbers=('NCH', 'OIH', 'NCH'))[0]

        def _conv_up(x, w_t):
            return lax.conv_transpose(x[None], w_t, (2,), 'VALID', dimension_numbers=('NCH', 'IOH', 'NCH'), transpose_kernel=True)[0]

        def _layer(x, style, w, b, mw, mb, typ):
            s = style @ mw.T + mb
            weight = SCALE * w * s[:, None, :, None]
            demod = lax.rsqrt(jnp.sum(weight * weight, axis=(2, 3)) + EPS)
            weight = weight * demod[:, :, None, None]
            blur_k = jnp.asarray(BLUR_K)
            if typ == 'same':
                out = jax.vmap(_conv_same)(x, weight) + b[None, :, None]
            elif typ == 'upsample':
                out = jax.vmap(_conv_up)(x, weight.transpose(0, 2, 1, 3)) + b[None, :, None]
                out = _blur(out, 2.0 * blur_k, (1, 1))
            elif typ == 'downsample':
                xb = _blur(x, blur_k, (2, 2))
                out = jax.vmap(_conv_down)(xb, weight) + b[None, :, None]
            else:
                raise NotImplementedError(typ)
            return out
        out = x
        for i, typ in enumerate(TYPES):
            out = _layer(out, style, weights[i], biases[i], mod_w[i], mod_b[i], typ)
        return out

    def _L1_ffn_ref(x, W_base, b_base, W_router, A, B):
        import jax, jax.numpy as jnp
        import numpy as np
        R = 16
        NUM_EXPERTS = 8
        TOP_K = 2
        LORA_ALPHA = 32
        SCALING = LORA_ALPHA / R
        orig_shape = x.shape
        d_in = x.shape[-1]
        x_flat = x.reshape(-1, d_in)
        logits = x_flat @ W_router.T
        probs = jax.nn.softmax(logits, axis=-1)
        topk_probs, topk_idx = jax.lax.top_k(probs, TOP_K)
        topk_probs = topk_probs / jnp.sum(topk_probs, axis=-1, keepdims=True)
        onehot = jax.nn.one_hot(topk_idx, NUM_EXPERTS, dtype=x.dtype)
        combine = jnp.einsum('nk,nke->ne', topk_probs, onehot)
        h = jnp.einsum('nd,erd->ner', x_flat, A)
        hw = h * combine[:, :, None]
        expert_out = jnp.einsum('ner,eor->no', hw, B) * SCALING
        base_out = x_flat @ W_base.T + b_base
        out = base_out + expert_out
        return out.reshape(*orig_shape[:-1], W_base.shape[0])
    x = x + _L0_attn_ref(_L0_cond_ref(x, cond_512, L0_cond_weights, L0_cond_biases, L0_cond_mod_w, L0_cond_mod_b), L0_attn_Wqkv, L0_attn_Wo)
    x = x + _L0_ffn_ref(_L0_cond2_ref(x, cond_512, L0_cond2_weights, L0_cond2_biases, L0_cond2_mod_w, L0_cond2_mod_b), L0_ffn_weight, L0_ffn_lora_A, L0_ffn_lora_B, L0_ffn_gw1, L0_ffn_gb1, L0_ffn_ln_gamma, L0_ffn_ln_beta, L0_ffn_gw2, L0_ffn_gb2)
    x = x + _L1_attn_ref(_L1_cond_ref(x, cond_512, L1_cond_weights, L1_cond_biases, L1_cond_mod_w, L1_cond_mod_b), L1_attn_wq_a, L1_attn_q_a_ln_w, L1_attn_wq_b, L1_attn_wkv_a, L1_attn_kv_a_ln_w, L1_attn_wkv_b, L1_attn_wo)
    x = x + _L1_ffn_ref(_L1_cond2_ref(x, cond_512, L1_cond2_weights, L1_cond2_biases, L1_cond2_mod_w, L1_cond2_mod_b), L1_ffn_W_base, L1_ffn_b_base, L1_ffn_W_router, L1_ffn_A, L1_ffn_B)
    return x

_drawn_inputs = setup_inputs


def setup_inputs(seed=0):
    import zlib

    import numpy as np

    out = dict(_drawn_inputs(seed))
    spreads = {'L0_ffn_gb1': (0.0, 0.8),
     'L0_ffn_ln_gamma': (1.0, 0.6),
     'L0_ffn_ln_beta': (0.0, 0.8),
     'L0_ffn_gb2': (0.0, 0.628),
     'L1_attn_q_a_ln_w': (1.0, 0.6),
     'L1_attn_kv_a_ln_w': (1.0, 0.6)}
    factors = {'L0_ffn_lora_A': 6.828,
     'L0_ffn_lora_B': 7.041,
     'L0_ffn_gw1': 7.538,
     'L0_ffn_gw2': 7.546,
     'L1_cond_biases': 3.802,
     'L1_cond_mod_b': 6.625,
     'L1_attn_wq_a': 7.652,
     'L1_attn_wq_b': 7.725,
     'L1_ffn_b_base': 3.467}
    for name, (base, spread) in spreads.items():
        noise = np.random.default_rng([zlib.crc32(name.encode()), seed]).standard_normal(out[name].shape)
        drawn = base * np.exp(spread * noise) if base else spread * noise
        out[name] = jnp.asarray(drawn.astype(out[name].dtype))
    for name, factor in factors.items():
        out[name] = (out[name] * factor).astype(out[name].dtype)
    return out
```

```python
import math
from contextlib import ExitStack

import numpy as np
import concourse.bass as bass
from concourse import mybir

F32 = mybir.dt.float32
ACT = mybir.ActivationFunctionType
ALU = mybir.AluOpType
AX = mybir.AxisListType

B, C, L = 32, 32, 512
P = 128
R = P // C
T = L // R
G = 4
NGROUP = B // G
TOK = B * C
NTILE = TOK // P
HALF = 512
NHALF = TOK // HALF
NET, LAYER, TAPS = 4, 4, 3
STYLE = 64
CONV_SCALE = 1.0 / float(np.sqrt(C * TAPS ** 2))
CONV_EPS = 1e-8
HD, NH, NKV = 128, 32, 8
GQ = NH // NKV
MASKED = -1e30
R0_SCALE = 1.0 / float(np.sqrt(HD))

PLAIN = (0, 1, 2, 3)
ORDER_A, ORDER_B = (0, 3, 1, 2), (5, 6, 4, 7)


def shifted(order, by):
    return tuple(p + by for p in order)


BLOCKS = [
    [(PLAIN, po) for po in range(4)] + [(shifted(PLAIN, -4), 0), (shifted(PLAIN, 4), 3)],
    [(PLAIN, po) for po in range(8)] + [(shifted(PLAIN, -4), po) for po in (0, 1)]
    + [(shifted(PLAIN, 4), po) for po in (6, 7)],
    [(PLAIN, po) for po in ORDER_A] + [(PLAIN, po - 4) for po in ORDER_B]
    + [(shifted(PLAIN, -4), 0), (shifted(PLAIN, 4), 3)],
    [(ORDER_A, po) for po in range(4)] + [(ORDER_B, po) for po in range(4)]
    + [(shifted(ORDER_B, -8), 0), (shifted(ORDER_A, 8), 3)],
]
NBLK = [len(b) for b in BLOCKS]
BLK0 = [sum(NBLK[:n]) for n in range(LAYER)]
NBLKS = sum(NBLK)
FFN_BANK = (4, 5, 6, 7, 0, 1, 2, 3)
CONV_STEPS = [(layer, p) for layer in range(LAYER) for p in range(2)]
ADD = dict(start=False, stop=True, skip_group_check=True)
BLUR = [1 / 8, 3 / 8, 3 / 8, 1 / 8]


def tap_factor(layer, pi, po, k):
    if layer == 1:
        j = 2 * pi + k - po + 1
        return 2 * BLUR[j] if 0 <= j < 4 else 0.0
    if layer == 3:
        j = pi - 2 * po - k + 2
        return BLUR[j] if 0 <= j < 4 else 0.0
    return 1.0 if pi - po + 1 == k else 0.0


def tap_factors():
    out = np.zeros((R, C, TAPS, NBLKS), np.float32)
    for layer in range(LAYER):
        for n, (pi, po) in enumerate(BLOCKS[layer]):
            for r in range(R):
                for k in range(TAPS):
                    out[r, :, k, BLK0[layer] + n] = tap_factor(layer, pi[r], po, k)
    return out.reshape(P, TAPS * NBLKS)


def rope0_tables():
    inv = (1.0 / np.float32(10000.0) ** (np.arange(0, HD, 2, dtype=np.float32) / HD)).astype(np.float32)
    f = np.outer(np.arange(C, dtype=np.float32), inv).astype(np.float32).T
    cos, sin = np.cos(f), np.sin(f)
    return np.concatenate([np.concatenate([cos, cos]), np.concatenate([sin, -sin])], 1).astype(np.float32)


def block_mask():
    return np.repeat(np.eye(R, dtype=np.float32), C, 0)


def causal_mask():
    q, k = np.mgrid[0:C, 0:C]
    return np.tile(np.where(k <= q, 0.0, MASKED), (R, 1)).astype(np.float32)


NE, RANK, TOPK = 8, 16, 2
NGATE = 32
NAT0, NAT1 = NGATE + NE * RANK, NE + NE * RANK
CAPACITY = int(3.0 * TOK / NE)
LN_EPS = 1e-5
LORA0, LORA1 = 1.0 / RANK, 32 / RANK

QA, LAT, ROT, NOPE, VD = 128, 32, 64, 64, 128
QK1 = ROT + LAT
RMS_EPS = 1e-6
R1_SCALE = (NOPE + ROT) ** (-0.5) * (0.1 * math.log(128.0) + 1.0) ** 2


def yarn_tables():
    dim, base, factor, orig_max = ROT, 10000.0, 128.0, 1024

    def corr_dim(r):
        return dim * math.log(orig_max / (r * 2 * math.pi)) / (2 * math.log(base))
    low = max(math.floor(corr_dim(32.0)), 0)
    high = min(math.ceil(corr_dim(1.0)), dim - 1)
    hi = high + 0.001 if low == high else float(high)
    ramp = np.clip((np.arange(dim // 2, dtype=np.float32) - low) / (hi - low), 0.0, 1.0)
    keep = 1.0 - ramp
    extra = 1.0 / base ** (np.arange(0, dim, 2, dtype=np.float32) / dim)
    inv = extra / factor * (1.0 - keep) + extra * keep
    f = np.outer(np.arange(C, dtype=np.float32), inv)
    return np.cos(f).astype(np.float32), np.sin(f).astype(np.float32)


def rope1_rows():
    cos, sin = yarn_tables()
    return np.tile(np.concatenate([cos, sin], 1), (R, 1)).astype(np.float32)


def rope1_cols():
    cos, sin = (x.T for x in yarn_tables())
    c = np.concatenate([cos, cos, np.ones((2 * LAT, C), np.float32)])
    z = np.concatenate([sin, -sin, np.zeros((2 * LAT, C), np.float32)])
    return np.stack([c, z], 1).astype(np.float32)


class Chain:

    def __init__(self, eng, sem):
        self.eng, self.sem, self.n = eng, sem, 0

    def mark(self, ins):
        self.n = self.n + 1
        ins.then_inc(self.sem, 1)

    def wait(self):
        self.eng.wait_ge(self.sem, self.n)

    def link(self, ins):
        self.mark(ins)
        self.wait()


def build(nc, a, out, stages=("c0", "a0", "c1", "f0", "c2", "a1", "c3", "f1"), dump="final"):
    ctx = ExitStack()
    with ctx:
        def sb(name, shape):
            return ctx.enter_context(nc.sbuf_tensor(name, shape, F32))

        def sem(name):
            return ctx.enter_context(nc.semaphore(name))

        ps = ctx.enter_context(nc.psum_tensor("ps", [P, 8, 512], F32))
        stream = sb("stream", [P, B, T])
        xt = sb("xt", [P, R, TOK])
        wblk = sb("wblk", [P, NET, NBLKS, C])
        ident = sb("ident", [P, P])
        in_scale = sb("in_scale", [P, NET, LAYER, B])
        mid_scale = sb("mid_scale", [P, NET, LAYER, B])
        mid_bias = sb("mid_bias", [P, NET, LAYER, B])
        edge = sb("edge", [P, NET, B])
        cbias = sb("cbias", [P, NET, LAYER])
        NACT = 2 * G * (T + 2)
        acts = sb("acts", [P, 6 * NACT])
        act0, act1 = (acts[:, n * NACT:(n + 1) * NACT].rearrange("p (a g t) -> p a g t", a=2, g=G) for n in range(2))
        act2, act3 = (acts[:, n * NACT:(n + 2) * NACT].rearrange("p (a h g t) -> p a h g t", a=2, h=2, g=G)
                      for n in (2, 4))
        fresh = sb("fresh", [P, B, R, C])
        w_qkv = sb("w_qkv", [P, 2, R, 6 * HD])
        w_o = sb("w_o", [P, GQ, R, P])
        rope0 = sb("rope0", [P, 2, C])
        causal = sb("causal", [P, C])
        eps = sb("eps", [P, 1])

        ARENA = 18560
        arena = sb("arena", [P, ARENA])

        class Region:
            def __init__(self):
                self.at = 0

            def take(self, *shape, parts=P):
                n = int(np.prod(shape))
                v = arena[0:parts, self.at:self.at + n]
                self.at += n
                assert self.at <= ARENA, self.at
                if len(shape) == 1:
                    return v
                names = "abcd"[:len(shape)]
                return v.rearrange(f"p ({' '.join(names)}) -> p {' '.join(names)}", **dict(zip(names, shape)))

        spare = w_qkv[:, :, :, :].rearrange("p a r n -> p (a r n)")

        class Spare(Region):
            def take(self, *shape):
                n = int(np.prod(shape))
                v = spare[:, self.at:self.at + n]
                self.at += n
                assert self.at <= 2 * R * 6 * HD, self.at
                names = "abcd"[:len(shape)]
                return v.rearrange(f"p ({' '.join(names)}) -> p {' '.join(names)}", **dict(zip(names, shape)))

        sp0 = Spare()
        f1_in = sp0.take(R, NAT1)
        f1_out = sp0.take(R, P)
        f1_bias = sp0.take(1, R)
        sp1 = Spare()
        sp1.at = sp0.at
        f0_in = sp1.take(R, NAT0)
        f0_main = sp1.take(R, R, P)
        f0_out = sp1.take(R, P)
        f0_rows = sp1.take(1, 3 * NGATE + NE * NGATE + NE)
        sp2 = Spare()
        sp2.at = sp0.at
        late = sp2.take(4, TOK)
        sp3 = Spare()
        sp3.at = sp0.at
        nat1 = sp3.take(NTILE, QA + QK1)
        keys_n = sp3.take(NTILE, QK1)
        tmp_k = sp3.take(2, NTILE, QA)
        f1_main = w_o
        rank_const = sb("rank_const", [P, NE])
        ones = sb("ones", [P, P])
        rms_eps = sb("rms_eps", [P, 2])

        conv = Region()
        act4 = conv.take(2, G, T)
        setup = Region()
        setup.at = 2048
        wrep = setup.take(NET * LAYER, TAPS, C)
        factor = setup.take(TAPS, NBLKS)
        tmpw = setup.take(2, 12 * C)
        modw = setup.take(NET * LAYER, P, parts=STYLE)
        style = setup.take(B, parts=STYLE)
        modb = setup.take(NET * LAYER)
        wsq = setup.take(NET * LAYER, TAPS, C, parts=C)
        wsum = setup.take(NET * LAYER, C, parts=C)
        wsum4 = setup.take(NET * LAYER, P, parts=C)
        sval = setup.take(NET * LAYER, B)
        ssq = setup.take(NET * LAYER, B)
        dval = setup.take(NET * LAYER, B)
        att0 = Region()
        rot = att0.take(2, 2, HALF)
        qk = att0.take(1 + GQ, TOK)
        vals = att0.take(2, NTILE, HD)
        probs = att0.take(2, 16, C)
        probs_t = att0.take(NTILE, GQ, G, C)
        heads = att0.take(GQ, TOK)
        stat = att0.take(2, 2, 16)
        ffn = Region()
        ffn.at = 2048
        nat = ffn.take(NTILE, NAT0)
        gate_a = ffn.take(NTILE, NGATE)
        gate_b = ffn.take(NTILE, NGATE)
        gate_p = ffn.take(NTILE, NE, NGATE)
        vote = ffn.take(8, NTILE, NE)
        both = ffn.take(NTILE, 2, NE)
        col = ffn.take(8, NTILE)
        count = ffn.take(2, 2 * NE)
        lora_t = ffn.take(TOK)
        att1 = Region()
        rot1 = att1.take(2, 2, HALF)
        a1_in = att1.take(R, QA + QK1)
        wq1 = att1.take(NH, QK1)
        wcomb = att1.take(8, R, P)
        qa_t = att1.take(TOK)
        keys_t = att1.take(TOK)
        a1_ln = att1.take(1, 1 + LAT)
        rope1r = att1.take(2, LAT)
        rope1c = att1.take(2, C)
        stat1 = att1.take(2, 2, 16)
        rms = att1.take(4, NTILE)
        probs1 = att1.take(2, 16, C)
        values1 = att1.take(NTILE, LAT)
        q1 = [att1.take(GQ, TOK),
              acts[:, 2 * NACT:2 * NACT + GQ * TOK].rearrange("p (g n) -> p g n", g=GQ)]
        flat = acts[:, 0:2 * 16 * C].rearrange("p (t n q) -> p t n q", t=2, n=16)
        att1b = Region()
        att1b.at = att1.at - GQ * TOK
        wo1 = att1b.take(2, GQ, R * P)
        probs1_t = fresh[:, :, :, :].rearrange("p b r c -> p (b r c)").rearrange(
            "p (a g j q) -> p a g j q", a=NTILE, g=GQ, j=G)
        made = fresh[:, :, :, :].rearrange("p b r c -> p (b r c)")
        w_nope = made[:, 0:2048].rearrange("p (a b) -> p a b", a=16)
        w_kb = made[:, 2048:3072].rearrange("p (a b) -> p a b", a=16)
        w_v = made[:, 3072:4096].rearrange("p (a b) -> p a b", a=NH)

        WIDE = [[0, 1], [2, 3]]
        NARROW = [4, 5]
        TURN = [6, 7]

        s_setup = sem("setup_loaded")
        s_stream = [sem(f"stream_pair{i}_loaded") for i in range(NGROUP // 2)]
        s_const = sem("constants_made")
        s_style = sem("style_product_done")
        s_sq = sem("squares_ready")
        s_demod = sem("demod_sums_done")
        s_sqrt = sem("demod_roots_ready")
        s_scales = sem("scales_ready")
        s_wblk = [sem(f"net{n}_conv_blocks_ready") for n in range(NET)]
        dve_steps = sem("dve_steps")
        pool_steps = sem("pool_steps")
        s_in = sem("conv_input_ready")
        s_conv = [sem(f"conv_layer{k}_done") for k in range(LAYER)]
        s_eva = [sem(f"conv_layer{k}_act_part") for k in range(LAYER)]
        s_evd = [sem(f"conv_layer{k}_dve_part") for k in range(LAYER)]
        s_turn = sem("conv_output_turned")
        s_xt = [sem(f"tokens_ready{p}") for p in range(2)]
        s_out = sem("outputs_written")
        s_const_loaded = sem("tables_loaded")
        s_zero = sem("zeros_made")
        s_w0 = [sem(f"l0_qkv_weights{p}_loaded") for p in range(2)]
        s_wo = sem("l0_wo_loaded")
        s_qkv = sem("l0_qkv_tile_done")
        s_rot = sem("l0_rotary_products_done")
        s_rope = sem("l0_rotary_sum_done")
        s_v = sem("l0_values_copied")
        s_score = sem("l0_scores_done")
        s_pull = sem("scores_turned")
        s_masked = sem("scores_masked")
        s_max = sem("row_maxima_ready")
        s_shift = sem("scores_shifted")
        s_exp = sem("exponentials_ready")
        s_recip = sem("row_sums_inverted")
        s_prob = sem("probabilities_ready")
        s_pt = sem("probabilities_turned")
        s_pv = sem("l0_pv_done")
        s_head = sem("l0_heads_copied")
        s_proj = sem("l0_projection_done")
        s_fresh = sem("l0_fresh_added")
        s_fw = [sem(f"ffn{n}_weights_loaded") for n in range(2)]
        s_nat = [sem(f"ffn{n}_token_products_done") for n in range(2)]
        s_natc = [sem(f"ffn{n}_token_products_copied") for n in range(2)]
        s_gact = [sem(f"ffn{n}_gate_scalar_steps") for n in range(2)]
        s_gate = [sem(f"ffn{n}_gate_waiting_for_scalar") for n in range(2)]
        s_both = sem("choices_ready")
        s_count = sem("choices_counted")
        s_lora = [sem(f"ffn{n}_lora_weighted") for n in range(2)]
        s_lturn = [sem(f"ffn{n}_lora_turned") for n in range(2)]
        s_lcopy = [sem(f"ffn{n}_lora_copied") for n in range(2)]
        s_ffn = [sem(f"ffn{n}_output_tile_done") for n in range(2)]
        s_fact = [sem(f"ffn{n}_act_copied") for n in range(2)]
        s_fdve = [sem(f"ffn{n}_dve_copied") for n in range(2)]
        s1_w = sem("l1_arena_weights_loaded")
        s1_wm = sem("l1_factor_weights_loaded")
        s1_wo = [sem(f"l1_wo{p}_loaded") for p in range(2)]
        s1_nat = sem("l1_projection_bank_done")
        s1_natc = sem("l1_projection_copied")
        s1_sq = sem("l1_square_sums_ready")
        s1_root = sem("l1_roots_ready")
        s1_qn = sem("l1_queries_normalised")
        s1_kn = sem("l1_keys_ready")
        s1_turn = sem("l1_turned")
        s1_turnc = sem("l1_turned_copied")
        s1_wq = sem("l1_absorbed_query_done")
        s1_wqc = sem("l1_absorbed_query_copied")
        s1_wc = sem("l1_absorbed_output_done")
        s1_wcc = sem("l1_absorbed_output_copied")
        s1_zero = sem("l1_zeros_made")
        s1_q = sem("l1_query_tile_done")
        s1_rot = sem("l1_rotary_products_done")
        s1_rope = sem("l1_rotary_sum_done")
        s1_pv = sem("l1_pv_done")
        s1_head = sem("l1_heads_copied")
        s1_flat = sem("l1_probabilities_flat")
        s1_place = sem("l1_probabilities_placed")
        s1_out = sem("l1_output_tile_done")
        s1_oact = sem("l1_act_copied")
        s1_odve = sem("l1_dve_copied")
        s_back = [sem(f"stage{n}_turned_back") for n in range(4)]
        s_added = [sem(f"stage{n}_stream_updated") for n in range(4)]

        nets = [int(s[1]) for s in stages if s[0] == "c"]

        SOFT0 = 2 * NKV if "a0" in stages else 0

        def done(net, per):
            return nets.index(net) * per
        block = ctx.enter_context(nc.Block())

        def tokens_of(g):
            return xt[:, :, g * P:(g + 1) * P].rearrange("t r (b c) -> t b r c", b=G)

        def turned(p):
            return ps[:, TURN[p], :].rearrange("t (b r c) -> t b r c", b=G, r=R)

        def latent(i):
            return xt[:, i, :] if i < R else late[:, i - R, :]

        def conv_blocks(eng, ch, tmp, net):
            for layer in range(LAYER):
                n, b = NBLK[layer], BLK0[layer]
                acc = wblk[:, net, b:b + n, :]
                t = tmp[:, 0:n * C].rearrange("p (n c) -> p n c", c=C)
                for k in range(TAPS):
                    w = wrep[:, net * LAYER + layer, k, :].unsqueeze(1).broadcast_to([P, n, C])
                    f = factor[:, k, b:b + n].unsqueeze(2).broadcast_to([P, n, C])
                    ch.link(eng.tensor_tensor(acc if k == 0 else t, w, f, ALU.mult))
                    if k:
                        last = eng.tensor_tensor(acc, acc, t, ALU.add)
                        if k < TAPS - 1:
                            ch.link(last)
                if layer < LAYER - 1:
                    ch.link(last)
            last.then_inc(s_wblk[net], 1)

        @block.sync
        def _(sp):
            sp.dma_start(style[:, :], a["style"]).then_inc(s_setup, 16)
            sp.dma_start(modw[:, :, :], a["modw"]).then_inc(s_setup, 16)
            sp.dma_start(modb[:, :], a["modb"]).then_inc(s_setup, 16)
            sp.dma_start(wsq[:, :, :, :], a["wsq"]).then_inc(s_setup, 16)
            sp.dma_start(cbias[:, :, :], a["cbias"]).then_inc(s_setup, 16)
            sp.dma_start(factor[:, :, :], a["factor"]).then_inc(s_setup, 16)
            sp.dma_start(ident[:, :], a["ident"]).then_inc(s_setup, 16)
            for r in range(R):
                sp.dma_start(wrep[r * C:(r + 1) * C, :, :, :], a["wrep"]).then_inc(s_setup, 16)
            for i in range(NGROUP // 2):
                pair = slice(2 * i * G, 2 * (i + 1) * G)
                sp.dma_start(stream[:, pair, :], a["x"][:, pair, :]).then_inc(s_stream[i], 16)
            sp.dma_start(rope0[:, :, :], a["rope0"]).then_inc(s_const_loaded, 16)
            sp.dma_start(causal[:, :], a["causal"]).then_inc(s_const_loaded, 16)
            sp.dma_start(rank_const[:, :], a["rank"]).then_inc(s_const_loaded, 16)
            if "a0" in stages:
                for i in range(NKV):
                    if i == 0:
                        sp.dma_start(w_qkv[:, 0, :, :], a["w_qkv"][0]).then_inc(s_w0[0], 16)
                    if i + 1 < NKV:
                        if i >= 1:
                            sp.wait_ge(s_qkv, 12 * i)
                        sp.dma_start(w_qkv[:, (i + 1) % 2, :, :], a["w_qkv"][i + 1]).then_inc(s_w0[(i + 1) % 2], 16)
                    if i >= 1:
                        sp.wait_ge(s_proj, 8 * i)
                    sp.dma_start(w_o[:, :, :, :], a["w_o"][i]).then_inc(s_wo, 16)
            if "a0" in stages:
                sp.wait_ge(s_qkv, 12 * NKV)
            if "f0" in stages:
                sp.dma_start(f0_in, a["f0_in"]).then_inc(s_fw[0], 16)
                sp.dma_start(f0_main, a["f0_main"]).then_inc(s_fw[0], 16)
                sp.dma_start(f0_out, a["f0_out"]).then_inc(s_fw[0], 16)
                sp.dma_start(f0_rows[:, 0, :], a["f0_rows"]).then_inc(s_fw[0], 16)
            if "f1" in stages:
                sp.dma_start(f1_in, a["f1_in"]).then_inc(s_fw[1], 16)
                sp.dma_start(f1_out, a["f1_out"]).then_inc(s_fw[1], 16)
                sp.dma_start(f1_bias[:, 0, :], a["f1_bias"]).then_inc(s_fw[1], 16)
                if "a0" in stages:
                    sp.wait_ge(s_proj, 8 * NKV)
                sp.dma_start(f1_main[:, :, :, :], a["f1_main"]).then_inc(s_fw[1], 16)
            if "a1" in stages:
                if "f0" in stages:
                    sp.wait_ge(s_fact[0], 4)
                    sp.wait_ge(s_fdve[0], 4)
                sp.dma_start(a1_in, a["a1_in"]).then_inc(s1_w, 16)
                sp.dma_start(wq1[:, :, 0:ROT], a["a1_pe"]).then_inc(s1_w, 16)
                sp.dma_start(a1_ln[:, 0, :], a["a1_ln"]).then_inc(s1_w, 16)
                sp.dma_start(rope1r, a["rope1r"]).then_inc(s1_w, 16)
                sp.dma_start(rope1c, a["rope1c"]).then_inc(s1_w, 16)
                for i in range(2):
                    sp.dma_start(wo1[:, i], a["a1_wo"][i]).then_inc(s1_wo[i], 16)
                if "f0" in stages:
                    sp.wait_ge(s_back[1], NGROUP)
                sp.dma_start(w_nope, a["a1_nope"]).then_inc(s1_wm, 16)
                sp.dma_start(w_kb, a["a1_kb"]).then_inc(s1_wm, 16)
                sp.dma_start(w_v, a["a1_v"]).then_inc(s1_wm, 16)
                for i in range(2, 8):
                    sp.wait_ge(s1_wc, i - 1)
                    sp.dma_start(wo1[:, i % 2], a["a1_wo"][i]).then_inc(s1_wo[i % 2], 16)
            if dump == "final":
                for i in range(NGROUP // 2):
                    pair = slice(2 * i * G, 2 * (i + 1) * G)
                    sp.wait_ge(s_added[3], 2 * i + 2)
                    sp.dma_start(out[:, pair, :], stream[:, pair, :]).then_inc(s_out, 16)
                sp.wait_ge(s_out, 16 * (NGROUP // 2))
            if dump == "stream":
                sp.wait_ge(s_added[nets[-1]], NGROUP)
                sp.dma_start(out, stream[:, :, :].rearrange("p b t -> p (b t)")).then_inc(s_out, 16)
                sp.wait_ge(s_out, 16)
            if dump == "xt":
                for p in range(2):
                    sp.wait_ge(s_xt[p], done(nets[-1], 4) + NGROUP // 2)
                sp.dma_start(out, xt[:, :, :].rearrange("p r n -> p (r n)")).then_inc(s_out, 16)
                sp.wait_ge(s_out, 16)

        N_SETUP = 16 * 11

        @block.tensor
        def _(pe):
            pe.wait_ge(s_setup, N_SETUP)
            for n in range(NET * LAYER):
                last = pe.matmul(ps[:, 0, n * B:(n + 1) * B], modw[:, n, :], style[:, :], start=True, stop=True)
            last.then_inc(s_style, 1)
            pe.wait_ge(s_sq, 2)
            for n in range(NET * LAYER):
                last = pe.matmul(ps[:, 1, n * B:(n + 1) * B], wsum4[:, n, :], ssq[0:C, n, :], start=True, stop=True)
            last.then_inc(s_demod, 1)

            def blk(net, layer, first, count=4):
                b = BLK0[layer] + first
                return wblk[:, net, b:b + count, :].rearrange("p n c -> p (n c)")

            def conv_stack(net):
                pe.wait_ge(s_wblk[net], 1)
                if net == NET - 1 and "a1" in stages:
                    pe.wait_ge(s_const, 3)
                def first(i, p):
                    g = 2 * i + p
                    o = ps[:, NARROW[p], :]
                    pe.wait_ge(s_in, done(net, 8) + g + 1)
                    x = act0[:, p]
                    pe.matmul(o, blk(net, 0, 0), x[:, :, 1:T + 1], start=True, stop=True)
                    pe.matmul(o[0:32], blk(net, 0, 4, 1), x[:, :, 0:T], **ADD)
                    pe.matmul(o[96:128], blk(net, 0, 5, 1), x[:, :, 2:T + 2], **ADD).then_inc(s_conv[0], 1)

                first(0, 0)
                first(0, 1)
                for i in range(NGROUP // 2):
                    for p in range(2):
                        g = 2 * i + p
                        pe.wait_ge((s_eva, s_evd)[p][0], done(net, 4) + i + 1)
                        oa, ob = ps[:, WIDE[p][0], :], ps[:, WIDE[p][1], :]
                        x = act1[:, p]
                        pe.matmul(oa, blk(net, 1, 0), x[:, :, 1:T + 1], start=True, stop=True)
                        pe.matmul(ob, blk(net, 1, 4), x[:, :, 1:T + 1], start=True, stop=True)
                        pe.matmul(oa[0:64], blk(net, 1, 8, 2), x[:, :, 0:T], **ADD)\
                            .then_inc(s_conv[1], 1)
                        pe.matmul(ob[64:128], blk(net, 1, 10, 2), x[:, :, 2:T + 2], **ADD)\
                            .then_inc(s_conv[1], 1)
                    for p in range(2):
                        g = 2 * i + p
                        pe.wait_ge(s_evd[1], done(net, 8) + g + 1)
                        oa, ob = ps[:, WIDE[p][0], :], ps[:, WIDE[p][1], :]
                        xa, xb = act2[:, p, 0], act2[:, p, 1]
                        pe.matmul(oa, blk(net, 2, 0), xa[:, :, 1:T + 1], start=True, stop=True)
                        pe.matmul(ob, blk(net, 2, 4), xb[:, :, 1:T + 1], start=True, stop=True)
                        pe.matmul(oa[0:32], blk(net, 2, 8, 1), xb[:, :, 0:T], **ADD)
                        pe.matmul(oa[32:64], blk(net, 2, 9, 1), xb[:, :, 1:T + 1], **ADD)
                        pe.matmul(ob[64:96], blk(net, 2, 8, 1), xa[:, :, 1:T + 1], **ADD)
                        pe.matmul(ob[96:128], blk(net, 2, 9, 1), xa[:, :, 2:T + 2], **ADD)\
                            .then_inc(s_conv[2], 2)
                    for p in range(2):
                        g = 2 * i + p
                        pe.wait_ge(s_eva[2], done(net, 8) + g + 1)
                        pe.wait_ge(s_evd[2], done(net, 8) + g + 1)
                        o = ps[:, NARROW[p], :]
                        xa, xb = act3[:, p, 0], act3[:, p, 1]
                        pe.matmul(o, blk(net, 3, 0), xa[:, :, 1:T + 1], start=True, stop=True)
                        pe.matmul(o, blk(net, 3, 4), xb[:, :, 1:T + 1], **ADD)
                        pe.matmul(o[0:32], blk(net, 3, 8, 1), xb[:, :, 0:T], **ADD)
                        pe.matmul(o[96:128], blk(net, 3, 9, 1), xa[:, :, 2:T + 2], **ADD)\
                            .then_inc(s_conv[3], 1)
                    for p in range(2):
                        g = 2 * i + p
                        pe.wait_ge((s_eva, s_evd)[p][3], done(net, 4) + i + 1)
                        if i:
                            pe.wait_ge(s_xt[p], done(net, 4) + i)
                        for j in range(G):
                            last = pe.transpose(ps[:, TURN[p], j * P:(j + 1) * P], act4[:, p, j, :], ident[:, :])
                        last.then_inc(s_turn, 1)
                        if g + 2 < NGROUP:
                            first(i + 1, p)

            def attention0(net):
                def qkv(i):
                    pe.wait_ge(s_w0[i % 2], 16 * (i // 2 + 1))
                    for k in range(12):
                        if k < 3 and i:
                            pe.wait_ge(s_rot, 10 * i) if k == 0 else pe.wait_ge(s_v, 2 * (i - 1) + k)
                        if k >= 3:
                            pe.wait_ge(s_rot, 10 * i + k - 2)
                        o = ps[:, k % 3, :]
                        if k < 10:
                            chunk, half = k // 2, k % 2
                            for r in range(R):
                                last = pe.matmul(o, w_qkv[:, i % 2, r, chunk * HD:(chunk + 1) * HD],
                                                 xt[:, r, half * HALF:(half + 1) * HALF],
                                                 start=(r == 0), stop=(r == R - 1))
                        else:
                            for m in range(4):
                                tile = 4 * (k - 10) + m
                                for r in range(R):
                                    last = pe.matmul(o[:, m * HD:(m + 1) * HD], xt[:, r, tile * P:(tile + 1) * P],
                                                     w_qkv[:, i % 2, r, 5 * HD:6 * HD],
                                                     start=(r == 0), stop=(r == R - 1))
                        last.then_inc(s_qkv, 1)

                def scores(i):
                    pe.wait_ge(s_rope, 10 * (i + 1))
                    for t in range(2):
                        if i:
                            pe.wait_ge(s_pull, 2 * (i - 1) + t + 1)
                        for m in range(4):
                            for j in range(G):
                                b = (4 * t + m) * G + j
                                last = pe.matmul(ps[32 * j:32 * j + 32, 3 + t, m * P:(m + 1) * P],
                                                 qk[:, 0, b * C:(b + 1) * C], qk[:, 1:1 + GQ, b * C:(b + 1) * C],
                                                 start=True, stop=True)
                        last.then_inc(s_score, 1)

                def pv(i):
                    if i:
                        pe.wait_ge(s_fresh, 8 * i)
                    pe.wait_ge(s_v, 2 * i + 2)
                    for q in range(NTILE):
                        if q % 4 == 0:
                            pe.wait_ge(s_pt, 2 * i + q // 4 + 1)
                        if q >= 2:
                            pe.wait_ge(s_head, 8 * i + q - 1)
                        pe.matmul(ps[:, 5 + q % 2, :], vals[:, i % 2, q, :],
                                  probs_t[:, q, :, :, :].rearrange("k g j q -> k (g j q)"),
                                  start=True, stop=True).then_inc(s_pv, 1)

                def project(i):
                    pe.wait_ge(s_wo, 16 * (i + 1))
                    for n in range(8):
                        half, r = n // 4, n % 4
                        pe.wait_ge(s_head, 8 * i + (4, 7, 8)[n] if n < 3 else 8 * i + 8)
                        if n >= 3:
                            pe.wait_ge(s_fresh, 8 * i + n - 2)
                        for g in range(GQ):
                            last = pe.matmul(ps[:, (7, 5, 6)[n % 3], :], w_o[:, g, r, :],
                                             heads[:, g, half * HALF:(half + 1) * HALF],
                                             start=(g == 0), stop=(g == GQ - 1))
                        last.then_inc(s_proj, 1)

                for p in range(2):
                    pe.wait_ge(s_xt[p], done(net, 4) + NGROUP // 2)
                qkv(0)
                scores(0)
                for i in range(NKV):
                    if i + 1 < NKV:
                        qkv(i + 1)
                    pv(i)
                    project(i)
                    if i + 1 < NKV:
                        scores(i + 1)

            def ffn(n):
                w_in, width, lora_at = ((f0_in, NAT0, NGATE), (f1_in, NAT1, NE))[n]
                w_main, w_out = ((f0_main, f0_out), (f1_main, f1_out))[n]
                for p in range(2):
                    pe.wait_ge(s_xt[p], done(2 * n + 1, 4) + NGROUP // 2)
                pe.wait_ge(s_fw[n], 64)
                for m in range(NTILE):
                    o = ps[:, m // 2, (m % 2) * 256:(m % 2) * 256 + width]
                    for r in range(R):
                        last = pe.matmul(o, xt[:, r, m * P:(m + 1) * P], w_in[:, r, :],
                                         start=(r == 0), stop=(r == R - 1))
                    if m % 2:
                        last.then_inc(s_nat[n], 1)

                def main(k):
                    half, r_out = k // 4, k % 4
                    for r in range(R):
                        pe.matmul(ps[:, FFN_BANK[k], :], w_main[:, r, r_out, :],
                                  xt[:, r, half * HALF:(half + 1) * HALF], start=(r == 0), stop=False)

                def lora(k):
                    half, r_out = k // 4, k % 4
                    pe.matmul(ps[:, FFN_BANK[k], :], w_out[:, r_out, :], lora_t[:, half * HALF:(half + 1) * HALF],
                              start=False, stop=True).then_inc(s_ffn[n], 1)

                for k in range(6):
                    if k >= 4:
                        pe.wait_ge(s_natc[n], k - 3)
                    main(k)
                pe.wait_ge(s_natc[n], 4)
                if n == 0:
                    pe.wait_ge(s_both, 1)
                    pe.matmul(ps[:, 2, 0:P], ones[:, :], both.rearrange("p m k e -> p (m k e)"),
                              start=True, stop=True).then_inc(s_count, 1)
                pe.wait_ge(s_lora[n], 1)
                for m in range(NTILE):
                    last = pe.transpose(ps[:, 2 + m // 4, (m % 4) * P:(m % 4 + 1) * P],
                                        nat[:, m, lora_at:lora_at + P], ident[:, :])
                    if m % 4 == 3:
                        last.then_inc(s_lturn[n], 1)
                pe.wait_ge(s_lcopy[n], 2)
                for k in range(6):
                    lora(k)
                for k in range(6, 8):
                    main(k)
                    lora(k)

            def attention1():
                for p in range(2):
                    pe.wait_ge(s_xt[p], done(2, 4) + NGROUP // 2)
                pe.wait_ge(s1_w, 80)
                pe.wait_ge(s1_wm, 48)

                def project(m):
                    o = ps[:, m // 2, (m % 2) * 256:(m % 2) * 256 + QA + QK1]
                    for r in range(R):
                        last = pe.matmul(o, xt[:, r, m * P:(m + 1) * P], a1_in[:, r, :],
                                         start=(r == 0), stop=(r == R - 1))
                    if m % 2:
                        last.then_inc(s1_nat, 1)

                def absorb_keys(m):
                    ins = pe.matmul(ps[:, 4 + m // 8, (m % 8) * 64:(m % 8 + 1) * 64], w_nope[:, m, :], w_kb[:, m, :],
                                    start=True, stop=True)
                    if m % 8 == 7:
                        ins.then_inc(s1_wq, 1)

                def absorb_output(i):
                    pe.wait_ge(s1_wo[i % 2], 16 * (i // 2 + 1))
                    if i >= 2:
                        pe.wait_ge(s1_wcc, i - 1)
                    for g in range(GQ):
                        last = pe.matmul(ps[32 * g:32 * g + 32, 6 + i % 2, :], w_v[:, GQ * i + g, :],
                                         wo1[:, i % 2, g, :], start=True, stop=True)
                    last.then_inc(s1_wc, 1)

                for i in range(8):
                    for m in ((2 * i, 2 * i + 1) if i < 4 else ()):
                        project(m)
                    for m in (range(4 * (i - 4), 4 * (i - 3)) if i >= 4 else ()):
                        absorb_keys(m)
                    absorb_output(i)
                pe.wait_ge(s1_natc, 4)
                pe.wait_ge(s1_qn, 1)
                for m in range(NTILE):
                    last = pe.transpose(ps[:, m // 4, (m % 4) * P:(m % 4 + 1) * P], nat1[:, m, 0:QA], ident[:, :])
                    if m % 4 == 3:
                        last.then_inc(s1_turn, 1)
                pe.wait_ge(s1_kn, 1)
                for m in range(NTILE):
                    last = pe.transpose(ps[0:QK1, 2 + m // 4, (m % 4) * P:(m % 4 + 1) * P], keys_n[:, m, :],
                                        ident[:, :])
                    if m % 4 == 3:
                        last.then_inc(s1_turn, 1)

                def queries(i, tiles):
                    for k in tiles:
                        if k >= 4 or i:
                            pe.wait_ge(s1_rot, 8 * i + k - 3)
                        g, half = k // 2, k % 2
                        pe.matmul(ps[0:QK1, (0, 1, 2, 7)[k % 4], :], wq1[:, GQ * i + g, :],
                                  qa_t[:, half * HALF:(half + 1) * HALF], start=True, stop=True).then_inc(s1_q, 1)

                def scores(i):
                    pe.wait_ge(s1_rope, 8 * (i + 1))
                    for t in range(2):
                        if i:
                            pe.wait_ge(s_pull, SOFT0 + 2 * (i - 1) + t + 1)
                        for m in range(4):
                            for j in range(G):
                                b = (4 * t + m) * G + j
                                last = pe.matmul(ps[32 * j:32 * j + 32, 3 + t, m * P:(m + 1) * P],
                                                 keys_t[0:QK1, b * C:(b + 1) * C],
                                                 q1[i % 2][0:QK1, :, b * C:(b + 1) * C], start=True, stop=True)
                        last.then_inc(s_score, 1)

                def pv(i):
                    for half in range(2):
                        pe.wait_ge(s1_place, 2 * i + half + 1)
                        if i:
                            pe.wait_ge(s1_head, 2 * i + half - 1)
                        for m in range(4):
                            q = 4 * half + m
                            for g in range(GQ):
                                last = pe.matmul(ps[32 * g:32 * g + 32, 5 + half, m * P:(m + 1) * P],
                                                 values1[:, q, :], probs1_t[:, q, g, :, :].rearrange("k j q -> k (j q)"),
                                                 start=True, stop=True)
                        last.then_inc(s1_pv, 1)

                pe.wait_ge(s1_turnc, 4)
                pe.wait_ge(s1_wqc, 2)
                pe.wait_ge(s1_wcc, 8)
                queries(0, range(8))
                queries(1, range(4))
                scores(0)
                queries(1, range(4, 8))
                for i in range(8):
                    if i + 2 < 8:
                        queries(i + 2, range(4))
                    if i:
                        pv(i - 1)
                    if i + 2 < 8:
                        queries(i + 2, range(4, 8))
                    if i + 1 < 8:
                        scores(i + 1)
                pv(7)
                pe.wait_ge(s1_head, 16)
                for n in range(8):
                    half, r_out = n // 4, n % 4
                    for i in range(8):
                        last = pe.matmul(ps[:, FFN_BANK[n], :], wcomb[:, i, r_out, :],
                                         latent(i)[:, half * HALF:(half + 1) * HALF], start=(i == 0), stop=(i == 7))
                    last.then_inc(s1_out, 1)

            def turn_back(stage, ready):
                for what, count in ready:
                    pe.wait_ge(what, count)
                for g in range(NGROUP):
                    if g >= 2:
                        pe.wait_ge(s_added[stage], g - 1)
                    for j in range(G):
                        last = pe.transpose(ps[:, TURN[g % 2], j * P:(j + 1) * P],
                                            fresh[:, g * G + j, :, :].rearrange("t r c -> t (r c)"), ident[:, :])
                    last.then_inc(s_back[stage], 1)

            for st in stages:
                if st[0] == "c":
                    conv_stack(int(st[1]))
                if st == "a0":
                    attention0(0)
                    turn_back(0, ((s_fresh, 8 * NKV),))
                if st == "f0":
                    ffn(0)
                    turn_back(1, ((s_fact[0], 4), (s_fdve[0], 4)))
                if st == "a1":
                    attention1()
                    turn_back(2, ((s1_oact, 4), (s1_odve, 4)))
                if st == "f1":
                    ffn(1)
                    turn_back(3, ((s_fact[1], 4), (s_fdve[1], 4)))

        @block.scalar
        def _(act):
            act.wait_ge(s_setup, N_SETUP)
            act.activation(wsq[:, :, :, :], wsq[:, :, :, :], ACT.Square).then_inc(s_sq, 1)
            act.wait_ge(s_demod, 1)
            act.wait_ge(s_const, 2)
            act.activation(dval[:, :, :], ps[:, 1, :].rearrange("p (n b) -> p n b", b=B), ACT.Sqrt,
                           bias=eps[:, 0:1], scale=CONV_SCALE ** 2).then_inc(s_sqrt, 1)

            def conv_stack(net):
                if net == nets[0]:
                    act.wait_ge(s_scales, 1)
                for i in range(NGROUP // 2):
                    for layer, p in CONV_STEPS:
                        g = 2 * i + p
                        wide = layer in (1, 2)
                        if not wide and p == 1:
                            continue
                        bank = ps[:, WIDE[p][0] if wide else NARROW[p], :]
                        dst = [act1[:, p], act2[:, p, 0], act3[:, p, 0], act4[:, p]][layer]
                        off = 0 if layer == 3 else 1
                        act.wait_ge(s_conv[layer], done(net, 16) + 2 * g + 1 if wide else done(net, 8) + g + 1)
                        for j in range(G):
                            b = g * G + j
                            bias = cbias[:, net, 3:4] if layer == 3 else mid_bias[:, net, layer, b:b + 1]
                            last = act.activation(dst[:, j, off:off + T], bank[:, j * T:(j + 1) * T],
                                                  ACT.Identity, bias=bias, scale=mid_scale[:, net, layer, b:b + 1])
                        last.then_inc(s_eva[layer], 1)
                    g = 2 * i
                    act.wait_ge(s_turn, done(net, 8) + g + 1)
                    act.activation(tokens_of(g), turned(0), ACT.Copy).then_inc(s_xt[0], 1)

            def attention0():
                def values(i):
                    for v in range(2):
                        act.wait_ge(s_qkv, 12 * i + 11 + v)
                        if i >= 2:
                            act.wait_ge(s_pv, 8 * (i - 1))
                        act.activation(vals[:, i % 2, 4 * v:4 * v + 4, :].rearrange("p a b -> p (a b)"),
                                       ps[:, (10 + v) % 3, :], ACT.Copy).then_inc(s_v, 1)

                values(0)
                for i in range(NKV):
                    for t in range(2):
                        act.wait_ge(s_shift, 2 * i + t + 1)
                        x = probs[:, t, :, :].rearrange("p a b -> p (a b)")
                        act.activation(x, x, ACT.Exp, scale=R0_SCALE).then_inc(s_exp, 1)
                    if i + 1 < NKV:
                        values(i + 1)
                    for q in range(NTILE):
                        act.wait_ge(s_pv, 8 * i + q + 1)
                        if i:
                            act.wait_ge(s_proj, 8 * i)
                        act.activation(heads[:, :, q * P:(q + 1) * P],
                                       ps[:, 5 + q % 2, :].rearrange("d (g n) -> d g n", g=GQ),
                                       ACT.Copy).then_inc(s_head, 1)

            def ffn(n):
                width = (NAT0, NAT1)[n]
                for q in range(4):
                    act.wait_ge(s_nat[n], q + 1)
                    act.activation(nat[:, 2 * q:2 * q + 2, 0:width],
                                   ps[:, q, :].rearrange("p (a b) -> p a b", a=2)[:, :, 0:width],
                                   ACT.Copy).then_inc(s_natc[n], 1)
                act.wait_ge(s_gate[n], 1)
                if n == 0:
                    act.activation(col[:, 1, :], col[:, 1, :], ACT.Sqrt, bias=rms_eps[:, 1:2],
                                   scale=1.0 / NGATE).then_inc(s_gact[n], 1)
                    act.wait_ge(s_gate[n], 2)
                    act.activation(col[:, 4, :], col[:, 4, :], ACT.Exp).then_inc(s_gact[n], 1)
                else:
                    act.activation(vote[:, 0], vote[:, 0], ACT.Exp).then_inc(s_gact[n], 1)
                for q in range(2):
                    act.wait_ge(s_lturn[n], q + 1)
                    act.activation(lora_t[:, q * HALF:(q + 1) * HALF], ps[:, 2 + q, :], ACT.Copy)\
                        .then_inc(s_lcopy[n], 1)
                for k in range(0, 8, 2):
                    half, r_out = k // 4, k % 4
                    act.wait_ge(s_ffn[n], k + 1)
                    act.activation(fresh[:, half * 16:half * 16 + 16, r_out, :],
                                   ps[:, FFN_BANK[k], :].rearrange("p (b c) -> p b c", c=C),
                                   ACT.Identity, bias=f1_bias[:, 0, r_out:r_out + 1] if n else 0.0)\
                        .then_inc(s_fact[n], 1)

            def attention1():
                def copy_projection(q):
                    act.wait_ge(s1_nat, q + 1)
                    act.activation(nat1[:, 2 * q:2 * q + 2, :],
                                   ps[:, q, :].rearrange("p (a b) -> p a b", a=2)[:, :, 0:QA + QK1],
                                   ACT.Copy).then_inc(s1_natc, 1)

                def copy_query_weights(q):
                    act.wait_ge(s1_wq, q + 1)
                    act.activation(wq1[:, 16 * q:16 * q + 16, ROT:QK1],
                                   ps[:, 4 + q, :].rearrange("p (h l) -> p h l", l=LAT), ACT.Copy).then_inc(s1_wqc, 1)

                def copy_output_weights(i):
                    act.wait_ge(s1_wc, i + 1)
                    act.activation(wcomb[:, i].rearrange("p r t -> p (r t)"), ps[:, 6 + i % 2, :], ACT.Copy)\
                        .then_inc(s1_wcc, 1)

                for i in range(8):
                    if i < 4:
                        copy_projection(i)
                    elif i % 2:
                        copy_query_weights(i // 2 - 2)
                    copy_output_weights(i)
                act.wait_ge(s1_sq, 1)
                act.activation(rms[:, 2, :], rms[:, 0, :], ACT.Sqrt, bias=rms_eps[:, 0:1], scale=1.0 / QA)\
                    .then_inc(s1_root, 1)
                act.activation(rms[:, 3, :], rms[:, 1, :], ACT.Sqrt, bias=rms_eps[:, 0:1], scale=1.0 / LAT)\
                    .then_inc(s1_root, 1)
                for q in range(2):
                    act.wait_ge(s1_turn, q + 1)
                    act.activation(qa_t[:, q * HALF:(q + 1) * HALF], ps[:, q, :], ACT.Copy,
                                   scale=a1_ln[:, 0, 0:1]).then_inc(s1_turnc, 1)
                for q in range(2):
                    act.wait_ge(s1_turn, q + 3)
                    act.activation(keys_t[0:QK1, q * HALF:(q + 1) * HALF], ps[0:QK1, 2 + q, :], ACT.Copy)\
                        .then_inc(s1_turnc, 1)
                for i in range(8):
                    for t in range(2):
                        act.wait_ge(s_shift, SOFT0 + 2 * i + t + 1)
                        x = probs1[:, t, :, :].rearrange("p a b -> p (a b)")
                        act.activation(x, x, ACT.Exp, scale=R1_SCALE).then_inc(s_exp, 1)
                    for t in range(2):
                        act.wait_ge(s1_flat, 2 * i + t + 1)
                        if i:
                            act.wait_ge(s1_pv, 2 * (i - 1) + t + 1)
                        for j in range(G):
                            q = slice(32 * j, 32 * j + 32)
                            last = act.activation(
                                probs1_t[q, 4 * t:4 * t + 4, :, j, :].rearrange("p a g q -> p (a g) q"),
                                flat[q, t, :, :], ACT.Copy)
                        last.then_inc(s1_place, 1)
                    for half in range(2):
                        act.wait_ge(s1_pv, 2 * i + half + 1)
                        act.activation(latent(i)[:, half * HALF:(half + 1) * HALF], ps[:, 5 + half, :],
                                       ACT.Copy).then_inc(s1_head, 1)
                for k in range(0, 8, 2):
                    half, r_out = k // 4, k % 4
                    act.wait_ge(s1_out, k + 1)
                    act.activation(fresh[:, half * 16:half * 16 + 16, r_out, :],
                                   ps[:, FFN_BANK[k], :].rearrange("p (b c) -> p b c", c=C),
                                   ACT.Copy).then_inc(s1_oact, 1)

            for st in stages:
                if st[0] == "c":
                    conv_stack(int(st[1]))
                if st == "a0":
                    attention0()
                if st == "f0":
                    ffn(0)
                if st == "a1":
                    attention1()
                if st == "f1":
                    ffn(1)

        @block.vector
        def _(dve):
            ch = Chain(dve, dve_steps)
            dve.memset(rms_eps[:, 0:1], RMS_EPS)
            dve.memset(rms_eps[:, 1:2], LN_EPS)
            dve.memset(ones[:, :], 1.0)
            dve.memset(eps[:, :], CONV_EPS).then_inc(s_const, 1)

            def zero_pads():
                rows_of = acts[:, :].rearrange("p (n t) -> p n t", t=T + 2)
                dve.memset(rows_of[:, :, 0:1], 0.0)
                dve.memset(rows_of[:, :, T + 1:T + 2], 0.0).then_inc(s_const, 1)

            zero_pads()
            dve.wait_ge(s_sq, 1)
            ch.link(dve.tensor_tensor(wsum[:, :, :], wsq[:, :, 0, :], wsq[:, :, 1, :], ALU.add))
            over_r = [C, NET * LAYER, R, C]
            ch.link(dve.tensor_tensor(wsum4[:, :, :].rearrange("i n (r o) -> i n r o", r=R),
                                      wsum[:, :, :].unsqueeze(2).broadcast_to(over_r),
                                      wsq[:, :, 2, :].unsqueeze(2).broadcast_to(over_r), ALU.add))
            dve.wait_ge(s_style, 1)
            ch.link(dve.tensor_tensor(sval[:, :, :], ps[:, 0, :].rearrange("p (n b) -> p n b", b=B),
                                      modb[:, :].unsqueeze(2).broadcast_to([P, NET * LAYER, B]), ALU.add))
            dve.tensor_tensor(ssq[:, :, :], sval[:, :, :], sval[:, :, :], ALU.mult).then_inc(s_sq, 1)
            conv_blocks(dve, ch, tmpw[:, 0, :], nets[0])
            dve.wait_ge(s_sqrt, 1)
            ch.link(dve.reciprocal(dval[:, :, :], dval[:, :, :]))
            s4 = sval[:, :, :].rearrange("p (n l) b -> p n l b", l=LAYER)
            d4 = dval[:, :, :].rearrange("p (n l) b -> p n l b", l=LAYER)
            dve.tensor_copy(in_scale[:, :, 0, :], s4[:, :, 0, :])
            dve.tensor_copy(in_scale[:, :, 1, :], d4[:, :, 1, :])
            dve.tensor_copy(in_scale[:, :, 2:4, :], s4[:, :, 2:4, :])
            ch.link(dve.tensor_scalar(cbias[:, :, 1], cbias[:, :, 1], 2.0, None, ALU.mult))
            for k in range(3):
                src = s4 if k == 1 else d4
                dve.scalar_tensor_tensor(mid_scale[:, :, k, :], src[:, :, k, :], CONV_SCALE, in_scale[:, :, k + 1, :],
                                         ALU.mult, ALU.mult)
                ch.mark(dve.tensor_tensor(mid_bias[:, :, k, :], in_scale[:, :, k + 1, :],
                                          cbias[:, :, k].unsqueeze(2).broadcast_to([P, NET, B]), ALU.mult))
            dve.tensor_scalar(mid_scale[:, :, 3, :], d4[:, :, 3, :], CONV_SCALE, None, ALU.mult)
            ch.wait()
            dve.tensor_scalar(edge[:, :, :], mid_bias[:, :, 1, :], -0.125, None, ALU.mult).then_inc(s_scales, 1)

            def conv_stack(net):
                for i in range(NGROUP // 2):
                    for layer, p in CONV_STEPS:
                        g = 2 * i + p
                        wide = layer in (1, 2)
                        if not wide and p == 0:
                            continue
                        bank = ps[:, WIDE[p][1] if wide else NARROW[p], :]
                        dst = [act1[:, p], act2[:, p, 1], act3[:, p, 1], act4[:, p]][layer]
                        off = 0 if layer == 3 else 1
                        dve.wait_ge(s_conv[layer], done(net, 16) + 2 * g + 2 if wide else done(net, 8) + g + 1)
                        for j in range(G):
                            b = g * G + j
                            bias = cbias[:, net, 3:4] if layer == 3 else mid_bias[:, net, layer, b:b + 1]
                            last = dve.tensor_scalar(dst[:, j, off:off + T], bank[:, j * T:(j + 1) * T],
                                                     mid_scale[:, net, layer, b:b + 1], bias, ALU.mult, ALU.add)
                        if layer == 1:
                            ch.link(last)
                            samples = slice(g * G, (g + 1) * G)
                            end = act2[96:128, p, 1, :, T]
                            dve.tensor_tensor(end, end, edge[96:128, net, samples], ALU.add)
                            dve.wait_ge(s_eva[layer], done(net, 8) + g + 1)
                            end = act2[0:32, p, 0, :, 1]
                            last = dve.tensor_tensor(end, end, edge[0:32, net, samples], ALU.add)
                        last.then_inc(s_evd[layer], 1)
                    g = 2 * i + 1
                    dve.wait_ge(s_turn, done(net, 8) + g + 1)
                    dve.tensor_copy(tokens_of(g), turned(1)).then_inc(s_xt[1], 1)

            def soft_pull(i, n0, probs):
                for t in range(2):
                    dve.wait_ge(s_score, n0 + 2 * i + t + 1)
                    dve.transpose(probs[:, t, :, :].rearrange("p a b -> p (a b)"), ps[:, 3 + t, :])\
                        .then_inc(s_pull, 1)

            def soft_max(i, n0, probs, stat):
                for t in range(2):
                    dve.wait_ge(s_masked, n0 + 2 * i + t + 1)
                    dve.tensor_reduce(stat[:, t, 0, :], probs[:, t, :, :], AX.X, ALU.max).then_inc(s_max, 1)

            def soft_sum(i, n0, probs, stat):
                for t in range(2):
                    dve.wait_ge(s_exp, n0 + 2 * i + t + 1)
                    ch.link(dve.tensor_reduce(stat[:, t, 1, :], probs[:, t, :, :], AX.X, ALU.add))
                    dve.reciprocal(stat[:, t, 1, :], stat[:, t, 1, :]).then_inc(s_recip, 1)

            def soft_turn(i, n0, probs, turned, used, per):
                for t in range(2):
                    dve.wait_ge(s_prob, n0 + 2 * i + t + 1)
                    if i:
                        dve.wait_ge(used, per * i)
                    for j in range(G):
                        q = slice(32 * j, 32 * j + 32)
                        last = dve.transpose(turned[q, 4 * t:4 * t + 4, :, j, :].rearrange("p a g q -> p (a g) q"),
                                             probs[q, t, :, :])
                    last.then_inc(s_pt, 1)

            def attention0():
                cos = rope0[:, 0, :]
                sin = rope0[:, 1, :]

                def rotate(i, k):
                    dve.wait_ge(s_qkv, 12 * i + k + 1)
                    n = 10 * i + k
                    if n >= 2:
                        dve.wait_ge(s_rope, n - 1)
                    x = ps[:, k % 3, :].rearrange("p (b s) -> p b s", s=C)
                    y = rot[:, k % 2, :, :].rearrange("p a (b s) -> p a b s", s=C)
                    dve.tensor_tensor(y[:, 0], x, cos.unsqueeze(1).broadcast_to([P, HALF // C, C]), ALU.mult)
                    for h in range(2):
                        src, dst = slice(64 * h, 64 * h + 64), slice(64 - 64 * h, 128 - 64 * h)
                        last = dve.tensor_tensor(y[dst, 1], x[src],
                                                 sin[src].unsqueeze(1).broadcast_to([64, HALF // C, C]), ALU.mult)
                    last.then_inc(s_rot, 1)

                for k in range(10):
                    rotate(0, k)
                for i in range(NKV):
                    soft_pull(i, 0, probs)
                    for k in range(10):
                        if i + 1 < NKV:
                            rotate(i + 1, k)
                        if k == 0:
                            soft_max(i, 0, probs, stat)
                        if k == 3:
                            soft_sum(i, 0, probs, stat)
                        if k == 6:
                            soft_turn(i, 0, probs, probs_t, s_pv, 8)
                    for n in range(8):
                        half, r = n // 4, n % 4
                        dve.wait_ge(s_proj, 8 * i + n + 1)
                        dst = fresh[:, half * 16:half * 16 + 16, r, :]
                        dve.tensor_tensor(dst, ps[:, (7, 5, 6)[n % 3], :].rearrange("p (b c) -> p b c", c=C), dst,
                                          ALU.add).then_inc(s_fresh, 1)

            def add_back(stage):
                for g in range(NGROUP):
                    dve.wait_ge(s_back[stage], g + 1)
                    x = stream[:, g * G:(g + 1) * G, :]
                    dve.tensor_tensor(x, ps[:, TURN[g % 2], :].rearrange("p (b t) -> p b t", t=T), x, ALU.add)\
                        .then_inc(s_added[stage], 1)

            def over(x, shape):
                return x.unsqueeze(len(shape) - 1).broadcast_to(shape)

            def choose(v, first, second, m1, m2, key, top):
                shape = [P, NTILE, NE]
                rank = rank_const[:, :].unsqueeze(1).broadcast_to(shape)
                for src, hot, most in ((v, first, m1), (key, second, m2)):
                    ch.link(dve.tensor_reduce(most, src, AX.X, ALU.max))
                    ch.link(dve.tensor_tensor(hot, src, over(most, shape), ALU.is_equal))
                    ch.link(dve.tensor_tensor(hot, hot, rank, ALU.mult))
                    ch.link(dve.tensor_reduce(top, hot, AX.X, ALU.max))
                    ch.link(dve.tensor_tensor(hot, hot, over(top, shape), ALU.is_equal))
                    if hot is first:
                        ch.link(dve.scalar_tensor_tensor(key, first, MASKED, v, ALU.mult, ALU.add))

            def gate0():
                row = lambda k, n: f0_rows[:, 0, k:k + n]
                tiles = [P, NTILE, NGATE]
                shape = [P, NTILE, NE]
                per_tile = lambda x: x.unsqueeze(1).broadcast_to([P, NTILE, x.shape[-1]])
                dve.wait_ge(s_fw[0], 64)
                dve.wait_ge(s_natc[0], 4)
                ch.link(dve.tensor_tensor(gate_a, nat[:, :, 0:NGATE], per_tile(row(0, NGATE)), ALU.add))
                ch.link(dve.tensor_reduce(col[:, 0, :], gate_a, AX.X, ALU.add))
                ch.link(dve.tensor_scalar(col[:, 0, :], col[:, 0, :], 1.0 / NGATE, None, ALU.mult))
                ch.link(dve.tensor_tensor(gate_a, gate_a, over(col[:, 0, :], tiles), ALU.subtract))
                ch.link(dve.tensor_tensor(gate_b, gate_a, gate_a, ALU.mult))
                dve.tensor_reduce(col[:, 1, :], gate_b, AX.X, ALU.add).then_inc(s_gate[0], 1)
                dve.wait_ge(s_gact[0], 1)
                ch.link(dve.reciprocal(col[:, 1, :], col[:, 1, :]))
                ch.link(dve.tensor_tensor(gate_a, gate_a, over(col[:, 1, :], tiles), ALU.mult))
                ch.link(dve.tensor_tensor(gate_a, gate_a, per_tile(row(NGATE, NGATE)), ALU.mult))
                ch.link(dve.tensor_tensor(gate_a, gate_a, per_tile(row(2 * NGATE, NGATE)), ALU.add))
                ch.link(dve.tensor_scalar(gate_a, gate_a, 0.0, None, ALU.max))
                big = [P, NTILE, NE, NGATE]
                w2 = row(3 * NGATE, NE * NGATE).rearrange("p (e k) -> p e k", e=NE)
                ch.link(dve.tensor_tensor(gate_p, gate_a.unsqueeze(2).broadcast_to(big),
                                          w2.unsqueeze(1).broadcast_to(big), ALU.mult))
                gates, first, second, key, w = (vote[:, n] for n in range(5))
                ch.link(dve.tensor_reduce(gates, gate_p, AX.X, ALU.add))
                ch.link(dve.tensor_tensor(gates, gates, per_tile(row(3 * NGATE + NE * NGATE, NE)), ALU.add))
                first, second = both[:, :, 0, :], both[:, :, 1, :]
                choose(gates, first, second, col[:, 2, :], col[:, 3, :], key, col[:, 5, :])
                dve.tensor_tensor(col[:, 4, :], col[:, 3, :], col[:, 2, :], ALU.subtract).then_inc(s_both, 1)
                dve.engine_nop().then_inc(s_gate[0], 1)
                dve.wait_ge(s_gact[0], 2)
                ch.link(dve.tensor_scalar(col[:, 5, :], col[:, 4, :], 1.0, None, ALU.add))
                ch.link(dve.reciprocal(col[:, 5, :], col[:, 5, :]))
                ch.link(dve.tensor_tensor(col[:, 6, :], col[:, 5, :], col[:, 4, :], ALU.mult))
                dve.wait_ge(s_count, 1)
                ch.link(dve.tensor_reduce(count[:, 0, :], ps[:, 2, 0:P].rearrange("p (m k) -> p k m", m=NTILE),
                                          AX.X, ALU.add))
                ch.link(dve.tensor_scalar(count[:, 1, :], count[:, 0, :], float(CAPACITY), LORA0, ALU.is_le, ALU.mult))
                for n, g in ((0, 5), (1, 6)):
                    hot = both[:, :, n, :]
                    ch.link(dve.tensor_tensor(hot, hot, per_tile(count[:, 1, n * NE:(n + 1) * NE]), ALU.mult))
                    ch.link(dve.tensor_tensor(hot, hot, over(col[:, g, :], shape), ALU.mult))
                ch.link(dve.tensor_tensor(w, first, second, ALU.add))
                weigh(0, w, NGATE)

            def weigh(n, w, at):
                x = nat[:, :, at:at + P].rearrange("p m (e k) -> p m e k", e=NE)
                dve.tensor_tensor(x, x, w.unsqueeze(3).broadcast_to([P, NTILE, NE, RANK]), ALU.mult)\
                    .then_inc(s_lora[n], 1)

            def gate1():
                shape = [P, NTILE, NE]
                p, first, second, key, w = (vote[:, n] for n in range(5))
                dve.wait_ge(s_natc[1], 4)
                ch.link(dve.tensor_reduce(col[:, 0, :], nat[:, :, 0:NE], AX.X, ALU.max))
                dve.tensor_tensor(p, nat[:, :, 0:NE], over(col[:, 0, :], shape), ALU.subtract).then_inc(s_gate[1], 1)
                dve.wait_ge(s_gact[1], 1)
                ch.link(dve.tensor_reduce(col[:, 1, :], p, AX.X, ALU.add))
                ch.link(dve.reciprocal(col[:, 1, :], col[:, 1, :]))
                ch.link(dve.tensor_tensor(p, p, over(col[:, 1, :], shape), ALU.mult))
                choose(p, first, second, col[:, 2, :], col[:, 3, :], key, col[:, 5, :])
                ch.link(dve.tensor_tensor(col[:, 4, :], col[:, 2, :], col[:, 3, :], ALU.add))
                ch.link(dve.reciprocal(col[:, 4, :], col[:, 4, :]))
                ch.link(dve.tensor_tensor(w, first, second, ALU.add))
                ch.link(dve.tensor_tensor(w, w, p, ALU.mult))
                ch.link(dve.tensor_scalar(col[:, 4, :], col[:, 4, :], LORA1, None, ALU.mult))
                ch.link(dve.tensor_tensor(w, w, over(col[:, 4, :], shape), ALU.mult))
                weigh(1, w, NE)

            def ffn(n):
                (gate0, gate1)[n]()
                for k in range(1, 8, 2):
                    half, r_out = k // 4, k % 4
                    dve.wait_ge(s_ffn[n], k + 1)
                    dst = fresh[:, half * 16:half * 16 + 16, r_out, :]
                    src = ps[:, FFN_BANK[k], :].rearrange("p (b c) -> p b c", c=C)
                    if n:
                        last = dve.tensor_scalar(dst, src, f1_bias[:, 0, r_out:r_out + 1], None, ALU.add)
                    else:
                        last = dve.tensor_copy(dst, src)
                    last.then_inc(s_fdve[n], 1)

            def attention1():
                dve.wait_ge(s1_w, 80)
                dve.wait_ge(s1_natc, 4)
                q, pe1, pe2, lat = (nat1[:, :, x:y] for x, y in ((0, QA), (QA, QA + 32), (QA + 32, QA + 64),
                                                                (QA + 64, QA + 96)))
                sq, t1 = tmp_k[:, 0], tmp_k[:, 1]
                ch.link(dve.tensor_tensor(sq, q, q, ALU.mult))
                ch.link(dve.tensor_reduce(rms[:, 0, :], sq, AX.X, ALU.add))
                ch.link(dve.tensor_tensor(t1[:, :, 0:LAT], lat, lat, ALU.mult))
                dve.tensor_reduce(rms[:, 1, :], t1[:, :, 0:LAT], AX.X, ALU.add).then_inc(s1_sq, 1)
                cos, sin = (rope1r[:, n, :].unsqueeze(1).broadcast_to([P, NTILE, 32]) for n in range(2))
                parts = [sq[:, :, 32 * n:32 * n + 32] for n in range(4)]
                ch.wait()
                for dst, x, y in zip(parts, (pe1, pe2, pe2, pe1), (cos, sin, cos, sin)):
                    ch.mark(dve.tensor_tensor(dst, x, y, ALU.mult))
                ch.wait()
                dve.tensor_tensor(keys_n[:, :, 0:32], parts[0], parts[1], ALU.subtract)
                dve.tensor_tensor(keys_n[:, :, 32:64], parts[2], parts[3], ALU.add)
                dve.wait_ge(s1_root, 2)
                ch.link(dve.reciprocal(rms[:, 2:4, :], rms[:, 2:4, :]))
                dve.tensor_tensor(q, q, over(rms[:, 2, :], [P, NTILE, QA]), ALU.mult).then_inc(s1_qn, 1)
                ch.link(dve.tensor_tensor(values1, lat, over(rms[:, 3, :], [P, NTILE, LAT]), ALU.mult))
                ch.link(dve.tensor_tensor(values1, values1, a1_ln[:, 0, 1:1 + LAT].unsqueeze(1)
                                          .broadcast_to([P, NTILE, LAT]), ALU.mult))
                dve.tensor_copy(keys_n[:, :, 64:96], values1).then_inc(s1_kn, 1)

                def rotate(i, k):
                    dve.wait_ge(s1_q, 8 * i + k + 1)
                    n = 8 * i + k
                    if n >= 2:
                        dve.wait_ge(s1_rope, n - 1)
                    x = ps[0:QK1, (0, 1, 2, 7)[k % 4], :].rearrange("p (b s) -> p b s", s=C)
                    y = rot1[0:QK1, k % 2, :, :].rearrange("p a (b s) -> p a b s", s=C)
                    dve.tensor_tensor(y[:, 0], x, rope1c[0:QK1, 0, :].unsqueeze(1)
                                      .broadcast_to([QK1, HALF // C, C]), ALU.mult)
                    for h in range(2):
                        src, dst = slice(32 * h, 32 * h + 32), slice(32 - 32 * h, 64 - 32 * h)
                        last = dve.tensor_tensor(y[dst, 1], x[src], rope1c[src, 1, :].unsqueeze(1)
                                                 .broadcast_to([32, HALF // C, C]), ALU.mult)
                    last.then_inc(s1_rot, 1)

                ch.link(dve.memset(rot1[64:96, :, 1, :], 0.0))
                dve.wait_ge(s1_zero, 1)
                def turn_flat(i):
                    for t in range(2):
                        dve.wait_ge(s_prob, SOFT0 + 2 * i + t + 1)
                        if i:
                            dve.wait_ge(s1_place, 2 * (i - 1) + t + 1)
                        dve.transpose(flat[:, t, :, :].rearrange("p a b -> p (a b)"),
                                      probs1[:, t, :, :].rearrange("p a b -> p (a b)")).then_inc(s1_flat, 1)

                for k in range(16):
                    rotate(k // 8, k % 8)
                for i in range(8):
                    if i:
                        dve.wait_ge(s1_flat, 2 * i)
                    soft_pull(i, SOFT0, probs1)
                    for k in range(8):
                        if i + 2 < 8:
                            rotate(i + 2, k)
                        if k == 0:
                            soft_max(i, SOFT0, probs1, stat1)
                        if k == 3:
                            soft_sum(i, SOFT0, probs1, stat1)
                        if k == 6:
                            turn_flat(i)
                for k in range(1, 8, 2):
                    half, r_out = k // 4, k % 4
                    dve.wait_ge(s1_out, k + 1)
                    dve.tensor_copy(fresh[:, half * 16:half * 16 + 16, r_out, :],
                                    ps[:, FFN_BANK[k], :].rearrange("p (b c) -> p b c", c=C)).then_inc(s1_odve, 1)

            for st in stages:
                if st[0] == "c":
                    conv_stack(int(st[1]))
                if st == "a0":
                    dve.wait_ge(s_const_loaded, 48)
                    dve.wait_ge(s_zero, 2)
                    attention0()
                    add_back(0)
                if st == "f0":
                    ffn(0)
                    add_back(1)
                if st == "a1":
                    attention1()
                    dve.wait_ge(s_score, SOFT0 + 16)
                    dve.wait_ge(s1_place, 16)
                    zero_pads()
                    add_back(2)
                if st == "f1":
                    ffn(1)
                    add_back(3)

        @block.gpsimd
        def _(pool):
            ch = Chain(pool, pool_steps)
            pool.wait_ge(s_setup, N_SETUP)
            pool.wait_ge(s_scales, 1)

            def conv_stack(net):
                for g in range(NGROUP):
                    if net != nets[0]:
                        pool.wait_ge(s_added[net - 1], g + 1)
                    elif g % 2 == 0:
                        pool.wait_ge(s_stream[g // 2], 16)
                    if g >= 2:
                        pool.wait_ge(s_conv[0], done(net, 8) + g - 1)
                    pool.tensor_tensor(act0[:, g % 2, :, 1:T + 1], stream[:, g * G:(g + 1) * G, :],
                                       in_scale[:, net, 0, g * G:(g + 1) * G].unsqueeze(2).broadcast_to([P, G, T]),
                                       ALU.mult).then_inc(s_in, 1)
                if net == nets[0]:
                    for later in nets[1:]:
                        conv_blocks(pool, ch, tmpw[:, 1, :], later)

            def soft_mask(i, n0, probs):
                for t in range(2):
                    pool.wait_ge(s_pull, n0 + 2 * i + t + 1)
                    pool.tensor_tensor(probs[:, t], probs[:, t], causal[:, :].unsqueeze(1)
                                       .broadcast_to([P, 16, C]), ALU.add).then_inc(s_masked, 1)

            def soft_shift(i, n0, probs, stat):
                for t in range(2):
                    pool.wait_ge(s_max, n0 + 2 * i + t + 1)
                    pool.tensor_tensor(probs[:, t], probs[:, t], stat[:, t, 0, :].unsqueeze(2)
                                       .broadcast_to([P, 16, C]), ALU.subtract).then_inc(s_shift, 1)

            def soft_scale(i, n0, probs, stat):
                for t in range(2):
                    pool.wait_ge(s_recip, n0 + 2 * i + t + 1)
                    pool.tensor_tensor(probs[:, t], probs[:, t], stat[:, t, 1, :].unsqueeze(2)
                                       .broadcast_to([P, 16, C]), ALU.mult).then_inc(s_prob, 1)

            def attention1():
                pool.wait_ge(s1_wcc, 8)
                pool.wait_ge(s1_wqc, 2)
                pool.memset(made, 0.0).then_inc(s1_zero, 1)
                pool.wait_ge(s1_zero, 1)

                def rope_add(i, k):
                    n = 8 * i + k
                    pool.wait_ge(s1_rot, n + 1)
                    if i >= 2 and k == 0:
                        pool.wait_ge(s_score, SOFT0 + 2 * (i - 1))
                    pool.tensor_tensor(q1[i % 2][0:QK1, k // 2, (k % 2) * HALF:(k % 2 + 1) * HALF],
                                       rot1[0:QK1, k % 2, 0, :], rot1[0:QK1, k % 2, 1, :],
                                       ALU.add).then_inc(s1_rope, 1)

                for k in range(16):
                    rope_add(k // 8, k % 8)
                for i in range(8):
                    soft_mask(i, SOFT0, probs1)
                    for k in range(8):
                        if i + 2 < 8:
                            rope_add(i + 2, k)
                        if k == 1:
                            soft_shift(i, SOFT0, probs1, stat1)
                        if k == 4:
                            soft_scale(i, SOFT0, probs1, stat1)

            def attention0():
                def rope_add(i, k):
                    n = 10 * i + k
                    pool.wait_ge(s_rot, n + 1)
                    if i and k == 0:
                        pool.wait_ge(s_score, 2 * i)
                    pool.tensor_tensor(qk[:, k // 2, (k % 2) * HALF:(k % 2 + 1) * HALF], rot[:, k % 2, 0, :],
                                       rot[:, k % 2, 1, :], ALU.add).then_inc(s_rope, 1)

                for k in range(10):
                    rope_add(0, k)
                for i in range(NKV):
                    soft_mask(i, 0, probs)
                    for k in range(10):
                        if i + 1 < NKV:
                            rope_add(i + 1, k)
                        if k == 1:
                            soft_shift(i, 0, probs, stat)
                        if k == 4:
                            soft_scale(i, 0, probs, stat)

            for st in stages:
                if st[0] == "c":
                    conv_stack(int(st[1]))
                if st == "a0":
                    pool.wait_ge(s_xt[1], done(0, 4) + NGROUP // 2)
                    pool.memset(fresh[:, :, :, :], 0.0).then_inc(s_zero, 1)
                    pool.memset(probs_t[:, :, :, :, :], 0.0).then_inc(s_zero, 1)
                    attention0()
                if st == "a1":
                    attention1()

def lay_out(inp):
    a = {}
    a["x"] = inp["x"].reshape(B, C, T, R).transpose(3, 1, 0, 2).reshape(P, B, T)
    a["style"] = inp["cond_512"].T
    nets = ["L0_cond", "L0_cond2", "L1_cond", "L1_cond2"]
    n = NET * LAYER
    mod_w = np.stack([inp[k + "_mod_w"] for k in nets]).reshape(n, 1, C, STYLE)
    a["modw"] = np.broadcast_to(mod_w, (n, R, C, STYLE)).reshape(n, P, STYLE).transpose(2, 0, 1)
    mod_b = np.stack([inp[k + "_mod_b"] for k in nets]).reshape(n, 1, C)
    a["modb"] = np.broadcast_to(mod_b, (n, R, C)).reshape(n, P).T
    bias = np.stack([inp[k + "_biases"] for k in nets]).reshape(NET, LAYER, 1, C)
    a["cbias"] = np.broadcast_to(bias, (NET, LAYER, R, C)).reshape(NET, LAYER, P).transpose(2, 0, 1)
    w = np.stack([inp[k + "_weights"] for k in nets]).reshape(NET, LAYER, C, C, TAPS)
    by_in = w.transpose(3, 0, 1, 4, 2)
    a["wsq"] = by_in.reshape(C, n, TAPS, C)
    contracted = by_in.copy()
    contracted[:, :, 1] = w.transpose(2, 0, 1, 4, 3)[:, :, 1]
    a["wrep"] = contracted.reshape(C, n, TAPS, C)

    qkv = inp["L0_attn_Wqkv"].reshape((NH + 2 * NKV) * HD, T, R)
    q = qkv[:NH * HD].reshape(NKV, GQ, HD, T, R)
    k = qkv[NH * HD:(NH + NKV) * HD].reshape(NKV, 1, HD, T, R)
    v = qkv[(NH + NKV) * HD:].reshape(NKV, 1, HD, T, R)
    a["w_qkv"] = np.concatenate([k, q, v], 1).transpose(0, 3, 4, 1, 2).reshape(NKV, T, R, 6 * HD)
    a["w_o"] = inp["L0_attn_Wo"].reshape(T, R, NKV, GQ, HD).transpose(2, 4, 3, 1, 0)

    def into(x):
        return x.reshape(x.shape[0], T, R).transpose(1, 2, 0)

    def out_of(x):
        return x.reshape(T, R, x.shape[1]).transpose(2, 1, 0)

    def rows(*vs):
        v = np.concatenate([x.reshape(-1) for x in vs])
        return np.broadcast_to(v, (P, v.size))

    lora_a = inp["L0_ffn_lora_A"].transpose(0, 2, 1).reshape(NE * RANK, L)
    a["f0_in"] = np.concatenate([into(inp["L0_ffn_gw1"]), into(lora_a)], 2)
    a["f0_main"] = inp["L0_ffn_weight"].reshape(T, R, T, R).transpose(2, 3, 1, 0)
    a["f0_out"] = out_of(inp["L0_ffn_lora_B"].transpose(2, 0, 1).reshape(L, NE * RANK))
    a["f0_rows"] = rows(*(inp["L0_ffn_" + k] for k in ("gb1", "ln_gamma", "ln_beta", "gw2", "gb2")))
    a["f1_in"] = np.concatenate([into(inp["L1_ffn_W_router"]), into(inp["L1_ffn_A"].reshape(NE * RANK, L))], 2)
    a["f1_main"] = inp["L1_ffn_W_base"].reshape(T, R, T, R).transpose(2, 3, 1, 0)
    a["f1_out"] = out_of(inp["L1_ffn_B"].transpose(1, 0, 2).reshape(L, NE * RANK))
    a["f1_bias"] = inp["L1_ffn_b_base"].reshape(T, R)

    kv_a = inp["L1_attn_wkv_a"]
    a["a1_in"] = np.concatenate([into(inp["L1_attn_wq_a"]), into(kv_a[LAT::2]), into(kv_a[LAT + 1::2]),
                                 into(kv_a[:LAT])], 2)
    q_b = inp["L1_attn_wq_b"].reshape(NH, NOPE + ROT, QA)
    a["a1_pe"] = np.concatenate([q_b[:, NOPE::2], q_b[:, NOPE + 1::2]], 1).transpose(2, 0, 1)
    a["a1_nope"] = q_b[:, :NOPE].reshape(NH // 2, 2 * NOPE, QA).transpose(1, 0, 2)
    kv_b = inp["L1_attn_wkv_b"].reshape(NH, NOPE + VD, LAT)
    pairs = np.zeros((2, NOPE, NH // 2, 2, LAT), np.float32)
    for h in range(2):
        pairs[h, :, :, h] = kv_b[h::2, :NOPE].transpose(1, 0, 2)
    a["a1_kb"] = pairs.reshape(2 * NOPE, NH // 2, 2 * LAT)
    a["a1_v"] = kv_b[:, NOPE:].transpose(1, 0, 2)
    a["a1_wo"] = inp["L1_attn_wo"].reshape(T, R, NH // GQ, GQ, VD).transpose(2, 4, 3, 1, 0)\
        .reshape(NH // GQ, VD, GQ, L)
    a["a1_ln"] = np.concatenate([inp["L1_attn_q_a_ln_w"].reshape(QA, 1), rows(inp["L1_attn_kv_a_ln_w"])], 1)

    a["factor"] = tap_factors().reshape(P, TAPS, NBLKS)
    a["ident"] = np.eye(P, dtype=np.float32)
    a["rope0"] = rope0_tables().reshape(P, 2, C)
    a["rope1r"] = rope1_rows().reshape(P, 2, LAT)
    a["rope1c"] = rope1_cols()
    a["causal"] = causal_mask()
    a["rank"] = np.tile(np.arange(NE, 0, -1, dtype=np.float32), (P, 1))
    return {k: np.ascontiguousarray(v) for k, v in a.items()}


def kernel(**inputs):
    import concourse.bacc as bacc
    from concourse.bass_utils import run_bass_kernel_spmd

    arrays = lay_out({k: np.asarray(v) for k, v in inputs.items()})
    nc = bacc.Bacc("TRN2", target_bir_lowering=False, num_devices=1)
    args = {k: nc.dram_tensor(f"in_{k}_dram", v.shape, F32, kind="ExternalInput").ap() for k, v in arrays.items()}
    out = nc.dram_tensor("out_dram", (P, B, T), F32, kind="ExternalOutput").ap()
    build(nc, args, out)
    r = run_bass_kernel_spmd(nc, [{f"in_{k}_dram": v for k, v in arrays.items()}], core_ids=[0])
    y = r.results[0]["out_dram"]
    return y.reshape(R, C, B, T).transpose(2, 1, 3, 0).reshape(B, C, L)
```

```python
import math
from contextlib import ExitStack

import numpy as np
import concourse.bass as bass
from concourse import mybir

F32 = mybir.dt.float32
F32R = mybir.dt.float32r
ACT = mybir.ActivationFunctionType
ALU = mybir.AluOpType
AX = mybir.AxisListType

B, C, L = 32, 32, 512
P = 128
R = P // C
T = L // R
G = 4
NGROUP = B // G
TOK = B * C
NTILE = TOK // P
HALF = 512
NHALF = TOK // HALF
NET, LAYER, TAPS = 4, 4, 3
STYLE = 64
CONV_SCALE = 1.0 / float(np.sqrt(C * TAPS ** 2))
CONV_EPS = 1e-8
HD, NH, NKV = 128, 32, 8
GQ = NH // NKV
MASKED = -1e30
R0_SCALE = 1.0 / float(np.sqrt(HD))

PLAIN = (0, 1, 2, 3)
ORDER_A, ORDER_B = (0, 3, 1, 2), (5, 6, 4, 7)


def shifted(order, by):
    return tuple(p + by for p in order)


BLOCKS = [
    [(PLAIN, po) for po in range(4)] + [(shifted(PLAIN, -4), 0), (shifted(PLAIN, 4), 3)],
    [(PLAIN, po) for po in range(8)] + [(shifted(PLAIN, -4), po) for po in (0, 1)]
    + [(shifted(PLAIN, 4), po) for po in (6, 7)],
    [(PLAIN, po) for po in ORDER_A] + [(PLAIN, po - 4) for po in ORDER_B]
    + [(shifted(PLAIN, -4), 0), (shifted(PLAIN, 4), 3)],
    [(ORDER_A, po) for po in range(4)] + [(ORDER_B, po) for po in range(4)]
    + [(shifted(ORDER_B, -8), 0), (shifted(ORDER_A, 8), 3)],
]
NBLK = [len(b) for b in BLOCKS]
BLK0 = [sum(NBLK[:n]) for n in range(LAYER)]
NBLKS = sum(NBLK)
FFN_BANK = (4, 5, 6, 7, 0, 1, 2, 3)
CONV_STEPS = [(layer, p) for layer in range(LAYER) for p in range(2)]
ADD = dict(start=False, stop=True, skip_group_check=True)
BLUR = [1 / 8, 3 / 8, 3 / 8, 1 / 8]


def tap_factor(layer, pi, po, k):
    if layer == 1:
        j = 2 * pi + k - po + 1
        return 2 * BLUR[j] if 0 <= j < 4 else 0.0
    if layer == 3:
        j = pi - 2 * po - k + 2
        return BLUR[j] if 0 <= j < 4 else 0.0
    return 1.0 if pi - po + 1 == k else 0.0


def tap_factors():
    out = np.zeros((R, C, TAPS, NBLKS), np.float32)
    for layer in range(LAYER):
        for n, (pi, po) in enumerate(BLOCKS[layer]):
            for r in range(R):
                for k in range(TAPS):
                    out[r, :, k, BLK0[layer] + n] = tap_factor(layer, pi[r], po, k)
    return out.reshape(P, TAPS * NBLKS)


def rope0_tables():
    inv = (1.0 / np.float32(10000.0) ** (np.arange(0, HD, 2, dtype=np.float32) / HD)).astype(np.float32)
    f = np.outer(np.arange(C, dtype=np.float32), inv).astype(np.float32).T
    cos, sin = np.cos(f), np.sin(f)
    return np.concatenate([np.concatenate([cos, cos]), np.concatenate([sin, -sin])], 1).astype(np.float32)


def block_mask():
    return np.repeat(np.eye(R, dtype=np.float32), C, 0)


def causal_mask():
    q, k = np.mgrid[0:C, 0:C]
    return np.tile(np.where(k <= q, 0.0, MASKED), (R, 1)).astype(np.float32)


NE, RANK, TOPK = 8, 16, 2
NGATE = 32
NAT0, NAT1 = NGATE + NE * RANK, NE + NE * RANK
CAPACITY = int(3.0 * TOK / NE)
LN_EPS = 1e-5
LORA0, LORA1 = 1.0 / RANK, 32 / RANK

QA, LAT, ROT, NOPE, VD = 128, 32, 64, 64, 128
QK1 = ROT + LAT
RMS_EPS = 1e-6
R1_SCALE = (NOPE + ROT) ** (-0.5) * (0.1 * math.log(128.0) + 1.0) ** 2


def yarn_tables():
    dim, base, factor, orig_max = ROT, 10000.0, 128.0, 1024

    def corr_dim(r):
        return dim * math.log(orig_max / (r * 2 * math.pi)) / (2 * math.log(base))
    low = max(math.floor(corr_dim(32.0)), 0)
    high = min(math.ceil(corr_dim(1.0)), dim - 1)
    hi = high + 0.001 if low == high else float(high)
    ramp = np.clip((np.arange(dim // 2, dtype=np.float32) - low) / (hi - low), 0.0, 1.0)
    keep = 1.0 - ramp
    extra = 1.0 / base ** (np.arange(0, dim, 2, dtype=np.float32) / dim)
    inv = extra / factor * (1.0 - keep) + extra * keep
    f = np.outer(np.arange(C, dtype=np.float32), inv)
    return np.cos(f).astype(np.float32), np.sin(f).astype(np.float32)


def rope1_rows():
    cos, sin = yarn_tables()
    return np.tile(np.concatenate([cos, sin], 1), (R, 1)).astype(np.float32)


def rope1_cols():
    cos, sin = (x.T for x in yarn_tables())
    c = np.concatenate([cos, cos, np.ones((2 * LAT, C), np.float32)])
    z = np.concatenate([sin, -sin, np.zeros((2 * LAT, C), np.float32)])
    return np.stack([c, z], 1).astype(np.float32)


class Chain:

    def __init__(self, eng, sem):
        self.eng, self.sem, self.n = eng, sem, 0

    def mark(self, ins):
        self.n = self.n + 1
        ins.then_inc(self.sem, 1)

    def wait(self):
        self.eng.wait_ge(self.sem, self.n)

    def link(self, ins):
        self.mark(ins)
        self.wait()


def build(nc, a, out, stages=("c0", "a0", "c1", "f0", "c2", "a1", "c3", "f1"), dump="final"):
    ctx = ExitStack()
    with ctx:
        place = {}

        def sb(name, shape):
            at = place[name] = -(-nc.sbuf_base // 32) * 32
            t = ctx.enter_context(nc.sbuf_tensor(name, shape, F32))
            assert nc.sbuf_base == at + 4 * int(np.prod(shape[1:]))
            return t

        def rounded(name, shape, where, skip=0):
            return nc.alloc_sbuf_tensor_at(name, shape, F32R, offset=place[where] + 4 * skip)

        def sem(name):
            return ctx.enter_context(nc.semaphore(name))

        ps = ctx.enter_context(nc.psum_tensor("ps", [P, 8, 512], F32))
        stream = sb("stream", [P, B, T])
        xt = sb("xt", [P, R, TOK])
        wblk = sb("wblk", [P, NET, NBLKS, C])
        ident = sb("ident", [P, P])
        in_scale = sb("in_scale", [P, NET, LAYER, B])
        mid_scale = sb("mid_scale", [P, NET, LAYER, B])
        mid_bias = sb("mid_bias", [P, NET, LAYER, B])
        edge = sb("edge", [P, NET, B])
        cbias = sb("cbias", [P, NET, LAYER])
        NACT = 2 * G * (T + 2)
        acts = sb("acts", [P, 6 * NACT])
        act0, act1 = (acts[:, n * NACT:(n + 1) * NACT].rearrange("p (a g t) -> p a g t", a=2, g=G) for n in range(2))
        act2, act3 = (acts[:, n * NACT:(n + 2) * NACT].rearrange("p (a h g t) -> p a h g t", a=2, h=2, g=G)
                      for n in (2, 4))
        fresh = sb("fresh", [P, B, R, C])
        WPART = 7 * HD
        w_l0 = sb("w_l0", [P, 2 * R * WPART + GQ * R * P])
        w_hi = rounded("w_hi", [P, R, WPART], "w_l0")
        w_lo = rounded("w_lo", [P, R, WPART], "w_l0", R * WPART)
        wo_lo = rounded("wo_lo", [P, GQ, R, P], "w_l0", 2 * R * WPART)
        wo_hi = rounded("wo_hi", [P, GQ, R, P], "acts", R * WPART)
        xt_hi = rounded("xt_hi", [P, R, TOK], "xt")
        xt_lo = rounded("xt_lo", [P, NGROUP, R, P], "stream")
        rope0 = sb("rope0", [P, 2, C])
        causal = sb("causal", [P, C])
        eps = sb("eps", [P, 1])

        ARENA = 18496
        arena = sb("arena", [P, ARENA])

        class Region:
            def __init__(self):
                self.at = 0

            def take(self, *shape, parts=P):
                n = int(np.prod(shape))
                v = arena[0:parts, self.at:self.at + n]
                self.at += n
                assert self.at <= ARENA, self.at
                if len(shape) == 1:
                    return v
                names = "abcd"[:len(shape)]
                return v.rearrange(f"p ({' '.join(names)}) -> p {' '.join(names)}", **dict(zip(names, shape)))

        NSPARE = 12 * R * HD
        spare = w_l0[:, 0:NSPARE]

        class Spare(Region):
            def take(self, *shape):
                n = int(np.prod(shape))
                v = spare[:, self.at:self.at + n]
                self.at += n
                assert self.at <= NSPARE, self.at
                names = "abcd"[:len(shape)]
                return v.rearrange(f"p ({' '.join(names)}) -> p {' '.join(names)}", **dict(zip(names, shape)))

        sp0 = Spare()
        f1_in = sp0.take(R, NAT1)
        f1_out = sp0.take(R, P)
        f1_bias = sp0.take(1, R)
        sp1 = Spare()
        sp1.at = sp0.at
        f0_in = sp1.take(R, NAT0)
        f0_main = sp1.take(R, R, P)
        f0_out = sp1.take(R, P)
        f0_rows = sp1.take(1, 3 * NGATE + NE * NGATE + NE)
        sp2 = Spare()
        sp2.at = sp0.at
        late = sp2.take(4, TOK)
        sp3 = Spare()
        sp3.at = sp0.at
        nat1 = sp3.take(NTILE, QA + QK1)
        keys_n = sp3.take(NTILE, QK1)
        tmp_k = sp3.take(2, NTILE, QA)
        f1_main = w_l0[:, NSPARE:NSPARE + R * R * P].rearrange("p (a r t) -> p a r t", a=R, r=R)
        rank_const = sb("rank_const", [P, NE])
        ones = sb("ones", [P, P])
        rms_eps = sb("rms_eps", [P, 2])

        conv = Region()
        act4 = conv.take(2, G, T)
        setup = Region()
        setup.at = 2048
        wrep = setup.take(NET * LAYER, TAPS, C)
        factor = setup.take(TAPS, NBLKS)
        tmpw = setup.take(2, 12 * C)
        modw = setup.take(NET * LAYER, P, parts=STYLE)
        style = setup.take(B, parts=STYLE)
        modb = setup.take(NET * LAYER)
        wsq = setup.take(NET * LAYER, TAPS, C, parts=C)
        wsum = setup.take(NET * LAYER, C, parts=C)
        wsum4 = setup.take(NET * LAYER, P, parts=C)
        sval = setup.take(NET * LAYER, B)
        ssq = setup.take(NET * LAYER, B)
        dval = setup.take(NET * LAYER, B)
        att0 = Region()
        rot = att0.take(2, 2, HALF)
        qk = att0.take(1 + GQ, TOK)
        vals = att0.take(2, NTILE, HD)
        probs = att0.take(2, 16, C)
        probs_t = att0.take(NTILE, GQ, G, C)
        h_hi = rounded("h_hi", [P, GQ, HALF], "arena", att0.at)
        h_lo = rounded("h_lo", [P, GQ, HALF], "arena", att0.at + GQ * HALF)
        assert setup.at <= att0.at
        stage0 = att0.take(R, WPART)
        att0.take(2 * GQ * HALF - R * WPART)
        stat = att0.take(2, 2, 16)
        ffn = Region()
        ffn.at = 2048
        nat = ffn.take(NTILE, NAT0)
        gate_a = ffn.take(NTILE, NGATE)
        gate_b = ffn.take(NTILE, NGATE)
        gate_p = ffn.take(NTILE, NE, NGATE)
        vote = ffn.take(8, NTILE, NE)
        both = ffn.take(NTILE, 2, NE)
        col = ffn.take(8, NTILE)
        count = ffn.take(2, 2 * NE)
        lora_t = ffn.take(TOK)
        att1 = Region()
        rot1 = att1.take(2, 2, HALF)
        a1_in = att1.take(R, QA + QK1)
        wq1 = att1.take(NH, QK1)
        wcomb = att1.take(8, R, P)
        qa_t = att1.take(TOK)
        keys_t = att1.take(TOK)
        a1_ln = att1.take(1, 1 + LAT)
        rope1r = att1.take(2, LAT)
        rope1c = att1.take(2, C)
        stat1 = att1.take(2, 2, 16)
        rms = att1.take(4, NTILE)
        probs1 = att1.take(2, 16, C)
        values1 = att1.take(NTILE, LAT)
        q1 = [att1.take(GQ, TOK),
              acts[:, 2 * NACT:2 * NACT + GQ * TOK].rearrange("p (g n) -> p g n", g=GQ)]
        stage1 = acts[:, 0:R * WPART]
        assert R * WPART + GQ * R * P <= 6 * NACT
        flat = acts[:, 0:2 * 16 * C].rearrange("p (t n q) -> p t n q", t=2, n=16)
        att1b = Region()
        att1b.at = att1.at - GQ * TOK
        wo1 = att1b.take(2, GQ, R * P)
        probs1_t = fresh[:, :, :, :].rearrange("p b r c -> p (b r c)").rearrange(
            "p (a g j q) -> p a g j q", a=NTILE, g=GQ, j=G)
        made = fresh[:, :, :, :].rearrange("p b r c -> p (b r c)")
        w_nope = made[:, 0:2048].rearrange("p (a b) -> p a b", a=16)
        w_kb = made[:, 2048:3072].rearrange("p (a b) -> p a b", a=16)
        w_v = made[:, 3072:4096].rearrange("p (a b) -> p a b", a=NH)

        WIDE = [[0, 1], [2, 3]]
        NARROW = [4, 5]
        TURN = [6, 7]

        s_setup = sem("setup_loaded")
        s_stream = [sem(f"stream_pair{i}_loaded") for i in range(NGROUP // 2)]
        s_const = sem("constants_made")
        s_style = sem("style_product_done")
        s_sq = sem("squares_ready")
        s_demod = sem("demod_sums_done")
        s_sqrt = sem("demod_roots_ready")
        s_scales = sem("scales_ready")
        s_wblk = [sem(f"net{n}_conv_blocks_ready") for n in range(NET)]
        dve_steps = sem("dve_steps")
        pool_steps = sem("pool_steps")
        s_in = sem("conv_input_ready")
        s_conv = [sem(f"conv_layer{k}_done") for k in range(LAYER)]
        s_eva = [sem(f"conv_layer{k}_act_part") for k in range(LAYER)]
        s_evd = [sem(f"conv_layer{k}_dve_part") for k in range(LAYER)]
        s_turn = sem("conv_output_turned")
        s_xt = [sem(f"tokens_ready{p}") for p in range(2)]
        s_out = sem("outputs_written")
        s_const_loaded = sem("tables_loaded")
        s_zero = sem("zeros_made")
        s_xhi = sem("l0_tokens_rounded")
        s_wst = sem("l0_weights_loaded")
        s_whi = sem("l0_weights_rounded")
        s_wlo = sem("l0_weights_split")
        s_again = sem("stream_loaded_again")
        s_qkv = sem("l0_kq_tile_done")
        s_vt = sem("l0_value_tile_done")
        s_rot = sem("l0_rotary_products_done")
        s_rope = sem("l0_rotary_sum_done")
        s_v = sem("l0_values_copied")
        s_score = sem("l0_scores_done")
        s_pull = sem("scores_turned")
        s_masked = sem("scores_masked")
        s_max = sem("row_maxima_ready")
        s_shift = sem("scores_shifted")
        s_exp = sem("exponentials_ready")
        s_recip = sem("row_sums_inverted")
        s_prob = sem("probabilities_ready")
        s_pt = sem("probabilities_turned")
        s_pv = sem("l0_pv_done")
        s_hhi = sem("l0_heads_rounded")
        s_head = sem("l0_heads_split")
        s_proj = sem("l0_projection_done")
        s_fresh = sem("l0_fresh_added")
        s_fw = [sem(f"ffn{n}_weights_loaded") for n in range(2)]
        s_nat = [sem(f"ffn{n}_token_products_done") for n in range(2)]
        s_natc = [sem(f"ffn{n}_token_products_copied") for n in range(2)]
        s_gact = [sem(f"ffn{n}_gate_scalar_steps") for n in range(2)]
        s_gate = [sem(f"ffn{n}_gate_waiting_for_scalar") for n in range(2)]
        s_both = sem("choices_ready")
        s_count = sem("choices_counted")
        s_lora = [sem(f"ffn{n}_lora_weighted") for n in range(2)]
        s_lturn = [sem(f"ffn{n}_lora_turned") for n in range(2)]
        s_lcopy = [sem(f"ffn{n}_lora_copied") for n in range(2)]
        s_ffn = [sem(f"ffn{n}_output_tile_done") for n in range(2)]
        s_fact = [sem(f"ffn{n}_act_copied") for n in range(2)]
        s_fdve = [sem(f"ffn{n}_dve_copied") for n in range(2)]
        s1_w = sem("l1_arena_weights_loaded")
        s1_wm = sem("l1_factor_weights_loaded")
        s1_wo = [sem(f"l1_wo{p}_loaded") for p in range(2)]
        s1_nat = sem("l1_projection_bank_done")
        s1_natc = sem("l1_projection_copied")
        s1_sq = sem("l1_square_sums_ready")
        s1_root = sem("l1_roots_ready")
        s1_qn = sem("l1_queries_normalised")
        s1_kn = sem("l1_keys_ready")
        s1_turn = sem("l1_turned")
        s1_turnc = sem("l1_turned_copied")
        s1_wq = sem("l1_absorbed_query_done")
        s1_wqc = sem("l1_absorbed_query_copied")
        s1_wc = sem("l1_absorbed_output_done")
        s1_wcc = sem("l1_absorbed_output_copied")
        s1_zero = sem("l1_zeros_made")
        s1_q = sem("l1_query_tile_done")
        s1_rot = sem("l1_rotary_products_done")
        s1_rope = sem("l1_rotary_sum_done")
        s1_pv = sem("l1_pv_done")
        s1_head = sem("l1_heads_copied")
        s1_flat = sem("l1_probabilities_flat")
        s1_place = sem("l1_probabilities_placed")
        s1_out = sem("l1_output_tile_done")
        s1_oact = sem("l1_act_copied")
        s1_odve = sem("l1_dve_copied")
        s_back = [sem(f"stage{n}_turned_back") for n in range(4)]
        s_added = [sem(f"stage{n}_stream_updated") for n in range(4)]

        nets = [int(s[1]) for s in stages if s[0] == "c"]

        SOFT0 = 2 * NKV if "a0" in stages else 0

        def done(net, per):
            return nets.index(net) * per
        block = ctx.enter_context(nc.Block())

        def tokens_of(g):
            return xt[:, :, g * P:(g + 1) * P].rearrange("t r (b c) -> t b r c", b=G)

        def tokens_hi(g):
            return xt_hi[:, :, g * P:(g + 1) * P].rearrange("t r (b c) -> t b r c", b=G)

        def tokens_lo(g):
            return xt_lo[:, g, :, :].rearrange("t r (b c) -> t b r c", b=G)

        def turned(p):
            return ps[:, TURN[p], :].rearrange("t (b r c) -> t b r c", b=G, r=R)

        def part(i):
            return 2 * i - 1 if i else 0

        def part_o(i):
            return min(2 * i + 2, 2 * NKV - 1)

        def wcols(i):
            return WPART if i % 2 == 0 else 5 * HD

        def latent(i):
            return xt[:, i, :] if i < R else late[:, i - R, :]

        def conv_blocks(eng, ch, tmp, net):
            for layer in range(LAYER):
                n, b = NBLK[layer], BLK0[layer]
                acc = wblk[:, net, b:b + n, :]
                t = tmp[:, 0:n * C].rearrange("p (n c) -> p n c", c=C)
                for k in range(TAPS):
                    w = wrep[:, net * LAYER + layer, k, :].unsqueeze(1).broadcast_to([P, n, C])
                    f = factor[:, k, b:b + n].unsqueeze(2).broadcast_to([P, n, C])
                    ch.link(eng.tensor_tensor(acc if k == 0 else t, w, f, ALU.mult))
                    if k:
                        last = eng.tensor_tensor(acc, acc, t, ALU.add)
                        if k < TAPS - 1:
                            ch.link(last)
                if layer < LAYER - 1:
                    ch.link(last)
            last.then_inc(s_wblk[net], 1)

        @block.sync
        def _(sp):
            sp.dma_start(style[:, :], a["style"]).then_inc(s_setup, 16)
            sp.dma_start(modw[:, :, :], a["modw"]).then_inc(s_setup, 16)
            sp.dma_start(modb[:, :], a["modb"]).then_inc(s_setup, 16)
            sp.dma_start(wsq[:, :, :, :], a["wsq"]).then_inc(s_setup, 16)
            sp.dma_start(cbias[:, :, :], a["cbias"]).then_inc(s_setup, 16)
            sp.dma_start(factor[:, :, :], a["factor"]).then_inc(s_setup, 16)
            sp.dma_start(ident[:, :], a["ident"]).then_inc(s_setup, 16)
            for r in range(R):
                sp.dma_start(wrep[r * C:(r + 1) * C, :, :, :], a["wrep"]).then_inc(s_setup, 16)
            for i in range(NGROUP // 2):
                pair = slice(2 * i * G, 2 * (i + 1) * G)
                sp.dma_start(stream[:, pair, :], a["x"][:, pair, :]).then_inc(s_stream[i], 16)
            sp.dma_start(rope0[:, :, :], a["rope0"]).then_inc(s_const_loaded, 16)
            sp.dma_start(causal[:, :], a["causal"]).then_inc(s_const_loaded, 16)
            sp.dma_start(rank_const[:, :], a["rank"]).then_inc(s_const_loaded, 16)
            if "a0" in stages:
                sp.dma_start(stage0, a["w_qkv"][0]).then_inc(s_wst, 16)

                def load_qkv(i):
                    sp.wait_ge(s_wlo, part(i))
                    n = wcols(i)
                    sp.dma_start(stage1.rearrange("p (r n) -> p r n", r=R)[:, :, 0:n],
                                 a["w_qkv"][i][:, :, 0:n]).then_inc(s_wst, 16)

                for p in range(2):
                    sp.wait_ge(s_xt[p], done(0, 4) + NGROUP // 2)
                load_qkv(1)
                for i in range(NKV):
                    sp.wait_ge(s_wlo, part_o(i))
                    sp.dma_start(stage1[:, 0:GQ * R * P], a["w_o"][i].rearrange("d g r t -> d (g r t)"))\
                        .then_inc(s_wst, 16)
                    if i + 2 < NKV:
                        load_qkv(i + 2)
                sp.wait_ge(s_qkv, 10 * NKV)
                sp.wait_ge(s_vt, 2 * NKV)
                sp.dma_start(stream[:, :, :], a["x"]).then_inc(s_again, 16)
            if "f0" in stages:
                sp.dma_start(f0_in, a["f0_in"]).then_inc(s_fw[0], 16)
                sp.dma_start(f0_main, a["f0_main"]).then_inc(s_fw[0], 16)
                sp.dma_start(f0_out, a["f0_out"]).then_inc(s_fw[0], 16)
                sp.dma_start(f0_rows[:, 0, :], a["f0_rows"]).then_inc(s_fw[0], 16)
            if "f1" in stages:
                sp.dma_start(f1_in, a["f1_in"]).then_inc(s_fw[1], 16)
                sp.dma_start(f1_out, a["f1_out"]).then_inc(s_fw[1], 16)
                sp.dma_start(f1_bias[:, 0, :], a["f1_bias"]).then_inc(s_fw[1], 16)
                if "a0" in stages:
                    sp.wait_ge(s_proj, 8 * NKV)
                sp.dma_start(f1_main, a["f1_main"]).then_inc(s_fw[1], 16)
            if "a1" in stages:
                if "f0" in stages:
                    sp.wait_ge(s_fact[0], 4)
                    sp.wait_ge(s_fdve[0], 4)
                sp.dma_start(a1_in, a["a1_in"]).then_inc(s1_w, 16)
                sp.dma_start(wq1[:, :, 0:ROT], a["a1_pe"]).then_inc(s1_w, 16)
                sp.dma_start(a1_ln[:, 0, :], a["a1_ln"]).then_inc(s1_w, 16)
                sp.dma_start(rope1r, a["rope1r"]).then_inc(s1_w, 16)
                sp.dma_start(rope1c, a["rope1c"]).then_inc(s1_w, 16)
                for i in range(2):
                    sp.dma_start(wo1[:, i], a["a1_wo"][i]).then_inc(s1_wo[i], 16)
                if "f0" in stages:
                    sp.wait_ge(s_back[1], NGROUP)
                sp.dma_start(w_nope, a["a1_nope"]).then_inc(s1_wm, 16)
                sp.dma_start(w_kb, a["a1_kb"]).then_inc(s1_wm, 16)
                sp.dma_start(w_v, a["a1_v"]).then_inc(s1_wm, 16)
                for i in range(2, 8):
                    sp.wait_ge(s1_wc, i - 1)
                    sp.dma_start(wo1[:, i % 2], a["a1_wo"][i]).then_inc(s1_wo[i % 2], 16)
            if dump == "final":
                for i in range(NGROUP // 2):
                    pair = slice(2 * i * G, 2 * (i + 1) * G)
                    sp.wait_ge(s_added[3], 2 * i + 2)
                    sp.dma_start(out[:, pair, :], stream[:, pair, :]).then_inc(s_out, 16)
                sp.wait_ge(s_out, 16 * (NGROUP // 2))
            if dump == "stream":
                sp.wait_ge(s_added[nets[-1]], NGROUP)
                sp.dma_start(out, stream[:, :, :].rearrange("p b t -> p (b t)")).then_inc(s_out, 16)
                sp.wait_ge(s_out, 16)
            if dump == "xt":
                for p in range(2):
                    sp.wait_ge(s_xt[p], done(nets[-1], 4) + NGROUP // 2)
                sp.dma_start(out, xt[:, :, :].rearrange("p r n -> p (r n)")).then_inc(s_out, 16)
                sp.wait_ge(s_out, 16)

        N_SETUP = 16 * 11

        @block.tensor
        def _(pe):
            pe.wait_ge(s_setup, N_SETUP)
            for n in range(NET * LAYER):
                last = pe.matmul(ps[:, 0, n * B:(n + 1) * B], modw[:, n, :], style[:, :], start=True, stop=True)
            last.then_inc(s_style, 1)
            pe.wait_ge(s_sq, 2)
            for n in range(NET * LAYER):
                last = pe.matmul(ps[:, 1, n * B:(n + 1) * B], wsum4[:, n, :], ssq[0:C, n, :], start=True, stop=True)
            last.then_inc(s_demod, 1)

            def blk(net, layer, first, count=4):
                b = BLK0[layer] + first
                return wblk[:, net, b:b + count, :].rearrange("p n c -> p (n c)")

            def conv_stack(net):
                pe.wait_ge(s_wblk[net], 1)
                if net in (1, 3) and f"a{net // 2}" in stages:
                    pe.wait_ge(s_const, 3 + (net // 2 if "a0" in stages else 0))
                def first(i, p):
                    g = 2 * i + p
                    o = ps[:, NARROW[p], :]
                    pe.wait_ge(s_in, done(net, 8) + g + 1)
                    x = act0[:, p]
                    pe.matmul(o, blk(net, 0, 0), x[:, :, 1:T + 1], start=True, stop=True)
                    pe.matmul(o[0:32], blk(net, 0, 4, 1), x[:, :, 0:T], **ADD)
                    pe.matmul(o[96:128], blk(net, 0, 5, 1), x[:, :, 2:T + 2], **ADD).then_inc(s_conv[0], 1)

                first(0, 0)
                first(0, 1)
                for i in range(NGROUP // 2):
                    for p in range(2):
                        g = 2 * i + p
                        pe.wait_ge((s_eva, s_evd)[p][0], done(net, 4) + i + 1)
                        oa, ob = ps[:, WIDE[p][0], :], ps[:, WIDE[p][1], :]
                        x = act1[:, p]
                        pe.matmul(oa, blk(net, 1, 0), x[:, :, 1:T + 1], start=True, stop=True)
                        pe.matmul(ob, blk(net, 1, 4), x[:, :, 1:T + 1], start=True, stop=True)
                        pe.matmul(oa[0:64], blk(net, 1, 8, 2), x[:, :, 0:T], **ADD)\
                            .then_inc(s_conv[1], 1)
                        pe.matmul(ob[64:128], blk(net, 1, 10, 2), x[:, :, 2:T + 2], **ADD)\
                            .then_inc(s_conv[1], 1)
                    for p in range(2):
                        g = 2 * i + p
                        pe.wait_ge(s_evd[1], done(net, 8) + g + 1)
                        oa, ob = ps[:, WIDE[p][0], :], ps[:, WIDE[p][1], :]
                        xa, xb = act2[:, p, 0], act2[:, p, 1]
                        pe.matmul(oa, blk(net, 2, 0), xa[:, :, 1:T + 1], start=True, stop=True)
                        pe.matmul(ob, blk(net, 2, 4), xb[:, :, 1:T + 1], start=True, stop=True)
                        pe.matmul(oa[0:32], blk(net, 2, 8, 1), xb[:, :, 0:T], **ADD)
                        pe.matmul(oa[32:64], blk(net, 2, 9, 1), xb[:, :, 1:T + 1], **ADD)
                        pe.matmul(ob[64:96], blk(net, 2, 8, 1), xa[:, :, 1:T + 1], **ADD)
                        pe.matmul(ob[96:128], blk(net, 2, 9, 1), xa[:, :, 2:T + 2], **ADD)\
                            .then_inc(s_conv[2], 2)
                    for p in range(2):
                        g = 2 * i + p
                        pe.wait_ge(s_eva[2], done(net, 8) + g + 1)
                        pe.wait_ge(s_evd[2], done(net, 8) + g + 1)
                        o = ps[:, NARROW[p], :]
                        xa, xb = act3[:, p, 0], act3[:, p, 1]
                        pe.matmul(o, blk(net, 3, 0), xa[:, :, 1:T + 1], start=True, stop=True)
                        pe.matmul(o, blk(net, 3, 4), xb[:, :, 1:T + 1], **ADD)
                        pe.matmul(o[0:32], blk(net, 3, 8, 1), xb[:, :, 0:T], **ADD)
                        pe.matmul(o[96:128], blk(net, 3, 9, 1), xa[:, :, 2:T + 2], **ADD)\
                            .then_inc(s_conv[3], 1)
                    for p in range(2):
                        g = 2 * i + p
                        pe.wait_ge((s_eva, s_evd)[p][3], done(net, 4) + i + 1)
                        if i:
                            pe.wait_ge(s_xt[p], done(net, 4) + i)
                        for j in range(G):
                            last = pe.transpose(ps[:, TURN[p], j * P:(j + 1) * P], act4[:, p, j, :], ident[:, :])
                        last.then_inc(s_turn, 1)
                        if g + 2 < NGROUP:
                            first(i + 1, p)

            def attention0(net):
                def keys_queries(i, tiles):
                    pe.wait_ge(s_wlo, part(i) + 1)
                    for k in tiles:
                        if k < 3 and i >= 2:
                            pe.wait_ge(s_fresh, 8 * (i - 2) + (7, 8, 8)[k])
                        if k < 3 and i == 1:
                            pe.wait_ge(s_v, (4, 4, 4)[k])
                        if k >= 3:
                            pe.wait_ge(s_rot, 10 * i + k - 2)
                        chunk, half = k // 2, k % 2
                        cols = slice(chunk * HD, (chunk + 1) * HD)
                        for r in range(R):
                            x_hi = xt_hi[:, r, half * HALF:(half + 1) * HALF]
                            x_lo = xt_lo[:, half * G:(half + 1) * G, r, :]
                            for n, (w, x) in enumerate(((w_hi, x_hi), (w_hi, x_lo), (w_lo, x_hi))):
                                last = pe.matmul(ps[:, k % 3, :], w[:, r, cols], x,
                                                 start=(r == 0 and n == 0), stop=(r == R - 1 and n == 2))
                        last.then_inc(s_qkv, 1)

                def values(i):
                    for v in range(4):
                        if v < 3 and i:
                            pe.wait_ge(s_fresh, 8 * (i - 1) + 2 + v)
                        if v < 3 and i == 0:
                            pe.wait_ge(s_rot, (9, 10, 8)[v])
                        if v == 3:
                            pe.wait_ge(s_v, 2 * i + 1)
                        for m in range(2):
                            tile = 2 * v + m
                            for r in range(R):
                                x_hi = xt_hi[:, r, tile * P:(tile + 1) * P]
                                x_lo = xt_lo[:, tile, r, :]
                                for n, (x, w) in enumerate(((x_hi, w_hi), (x_hi, w_lo), (x_lo, w_hi))):
                                    last = pe.matmul(ps[:, (2, 0, 1, 2)[v], m * 2 * HD:(m + 1) * 2 * HD], x,
                                                     w[:, r, 5 * HD:7 * HD],
                                                     start=(r == 0 and n == 0), stop=(r == R - 1 and n == 2))
                        last.then_inc(s_vt, 1)

                def scores(i):
                    pe.wait_ge(s_rope, 10 * (i + 1))
                    for t in range(2):
                        if i:
                            pe.wait_ge(s_pull, 2 * (i - 1) + t + 1)
                        for m in range(4):
                            for j in range(G):
                                b = (4 * t + m) * G + j
                                last = pe.matmul(ps[32 * j:32 * j + 32, 3 + t, m * P:(m + 1) * P],
                                                 qk[:, 0, b * C:(b + 1) * C], qk[:, 1:1 + GQ, b * C:(b + 1) * C],
                                                 start=True, stop=True)
                        last.then_inc(s_score, 1)

                def pv(i, tiles):
                    pe.wait_ge(s_v, 4 * (i // 2) + 4)
                    for q in tiles:
                        if q % 4 == 0:
                            pe.wait_ge(s_pt, 2 * i + q // 4 + 1)
                        if i or q >= 2:
                            pe.wait_ge(s_head, 8 * i + q - 1)
                        pe.matmul(ps[:, 5 + q % 2, :], vals[:, i % 2, q, :],
                                  probs_t[:, q, :, :, :].rearrange("k g j q -> k (g j q)"),
                                  start=True, stop=True).then_inc(s_pv, 1)

                def project(i, half):
                    pe.wait_ge(s_wlo, part_o(i) + 1)
                    pe.wait_ge(s_head, 8 * i + 4 * half + 4)
                    for r in range(R):
                        n = 4 * half + r
                        if i or half:
                            pe.wait_ge(s_fresh, 8 * i + n - 3)
                        if half == 0 and r and i + 1 < NKV:
                            pe.wait_ge(s_rot, 10 * (i + 1) + (9, 10, 8)[r - 1])
                        if half and r and i % 2 and i + 1 < NKV:
                            pe.wait_ge(s_v, 2 * (i + 1) + (4, 2, 3)[r - 1])
                        for g in range(GQ):
                            for m, (w, x) in enumerate(((wo_hi, h_hi), (wo_hi, h_lo), (wo_lo, h_hi))):
                                last = pe.matmul(ps[:, (7, 2, 0, 1)[r], :], w[:, g, r, :], x[:, g, :],
                                                 start=(g == 0 and m == 0), stop=(g == GQ - 1 and m == 2))
                        last.then_inc(s_proj, 1)

                for p in range(2):
                    pe.wait_ge(s_xt[p], done(net, 4) + NGROUP // 2)
                keys_queries(0, range(10))
                values(0)
                scores(0)
                for i in range(NKV):
                    if i + 1 < NKV:
                        keys_queries(i + 1, range(8))
                    pv(i, range(4))
                    if i + 1 < NKV:
                        keys_queries(i + 1, range(8, 10))
                    project(i, 0)
                    pv(i, range(4, 6))
                    if i + 1 < NKV:
                        scores(i + 1)
                    pv(i, range(6, 8))
                    if i % 2 and i + 1 < NKV:
                        values(i + 1)
                    project(i, 1)

            def ffn(n):
                w_in, width, lora_at = ((f0_in, NAT0, NGATE), (f1_in, NAT1, NE))[n]
                w_main, w_out = ((f0_main, f0_out), (f1_main, f1_out))[n]
                for p in range(2):
                    pe.wait_ge(s_xt[p], done(2 * n + 1, 4) + NGROUP // 2)
                pe.wait_ge(s_fw[n], 64)
                for m in range(NTILE):
                    o = ps[:, m // 2, (m % 2) * 256:(m % 2) * 256 + width]
                    for r in range(R):
                        last = pe.matmul(o, xt[:, r, m * P:(m + 1) * P], w_in[:, r, :],
                                         start=(r == 0), stop=(r == R - 1))
                    if m % 2:
                        last.then_inc(s_nat[n], 1)

                def main(k):
                    half, r_out = k // 4, k % 4
                    for r in range(R):
                        pe.matmul(ps[:, FFN_BANK[k], :], w_main[:, r, r_out, :],
                                  xt[:, r, half * HALF:(half + 1) * HALF], start=(r == 0), stop=False)

                def lora(k):
                    half, r_out = k // 4, k % 4
                    pe.matmul(ps[:, FFN_BANK[k], :], w_out[:, r_out, :], lora_t[:, half * HALF:(half + 1) * HALF],
                              start=False, stop=True).then_inc(s_ffn[n], 1)

                for k in range(6):
                    if k >= 4:
                        pe.wait_ge(s_natc[n], k - 3)
                    main(k)
                pe.wait_ge(s_natc[n], 4)
                if n == 0:
                    pe.wait_ge(s_both, 1)
                    pe.matmul(ps[:, 2, 0:P], ones[:, :], both.rearrange("p m k e -> p (m k e)"),
                              start=True, stop=True).then_inc(s_count, 1)
                pe.wait_ge(s_lora[n], 1)
                for m in range(NTILE):
                    last = pe.transpose(ps[:, 2 + m // 4, (m % 4) * P:(m % 4 + 1) * P],
                                        nat[:, m, lora_at:lora_at + P], ident[:, :])
                    if m % 4 == 3:
                        last.then_inc(s_lturn[n], 1)
                pe.wait_ge(s_lcopy[n], 2)
                for k in range(6):
                    lora(k)
                for k in range(6, 8):
                    main(k)
                    lora(k)

            def attention1():
                for p in range(2):
                    pe.wait_ge(s_xt[p], done(2, 4) + NGROUP // 2)
                pe.wait_ge(s1_w, 80)
                pe.wait_ge(s1_wm, 48)

                def project(m):
                    o = ps[:, m // 2, (m % 2) * 256:(m % 2) * 256 + QA + QK1]
                    for r in range(R):
                        last = pe.matmul(o, xt[:, r, m * P:(m + 1) * P], a1_in[:, r, :],
                                         start=(r == 0), stop=(r == R - 1))
                    if m % 2:
                        last.then_inc(s1_nat, 1)

                def absorb_keys(m):
                    ins = pe.matmul(ps[:, 4 + m // 8, (m % 8) * 64:(m % 8 + 1) * 64], w_nope[:, m, :], w_kb[:, m, :],
                                    start=True, stop=True)
                    if m % 8 == 7:
                        ins.then_inc(s1_wq, 1)

                def absorb_output(i):
                    pe.wait_ge(s1_wo[i % 2], 16 * (i // 2 + 1))
                    if i >= 2:
                        pe.wait_ge(s1_wcc, i - 1)
                    for g in range(GQ):
                        last = pe.matmul(ps[32 * g:32 * g + 32, 6 + i % 2, :], w_v[:, GQ * i + g, :],
                                         wo1[:, i % 2, g, :], start=True, stop=True)
                    last.then_inc(s1_wc, 1)

                for i in range(8):
                    for m in ((2 * i, 2 * i + 1) if i < 4 else ()):
                        project(m)
                    for m in (range(4 * (i - 4), 4 * (i - 3)) if i >= 4 else ()):
                        absorb_keys(m)
                    absorb_output(i)
                pe.wait_ge(s1_natc, 4)
                pe.wait_ge(s1_qn, 1)
                for m in range(NTILE):
                    last = pe.transpose(ps[:, m // 4, (m % 4) * P:(m % 4 + 1) * P], nat1[:, m, 0:QA], ident[:, :])
                    if m % 4 == 3:
                        last.then_inc(s1_turn, 1)
                pe.wait_ge(s1_kn, 1)
                for m in range(NTILE):
                    last = pe.transpose(ps[0:QK1, 2 + m // 4, (m % 4) * P:(m % 4 + 1) * P], keys_n[:, m, :],
                                        ident[:, :])
                    if m % 4 == 3:
                        last.then_inc(s1_turn, 1)

                def queries(i, tiles):
                    for k in tiles:
                        if k >= 4 or i:
                            pe.wait_ge(s1_rot, 8 * i + k - 3)
                        g, half = k // 2, k % 2
                        pe.matmul(ps[0:QK1, (0, 1, 2, 7)[k % 4], :], wq1[:, GQ * i + g, :],
                                  qa_t[:, half * HALF:(half + 1) * HALF], start=True, stop=True).then_inc(s1_q, 1)

                def scores(i):
                    pe.wait_ge(s1_rope, 8 * (i + 1))
                    for t in range(2):
                        if i:
                            pe.wait_ge(s_pull, SOFT0 + 2 * (i - 1) + t + 1)
                        for m in range(4):
                            for j in range(G):
                                b = (4 * t + m) * G + j
                                last = pe.matmul(ps[32 * j:32 * j + 32, 3 + t, m * P:(m + 1) * P],
                                                 keys_t[0:QK1, b * C:(b + 1) * C],
                                                 q1[i % 2][0:QK1, :, b * C:(b + 1) * C], start=True, stop=True)
                        last.then_inc(s_score, 1)

                def pv(i):
                    for half in range(2):
                        pe.wait_ge(s1_place, 2 * i + half + 1)
                        if i:
                            pe.wait_ge(s1_head, 2 * i + half - 1)
                        for m in range(4):
                            q = 4 * half + m
                            for g in range(GQ):
                                last = pe.matmul(ps[32 * g:32 * g + 32, 5 + half, m * P:(m + 1) * P],
                                                 values1[:, q, :], probs1_t[:, q, g, :, :].rearrange("k j q -> k (j q)"),
                                                 start=True, stop=True)
                        last.then_inc(s1_pv, 1)

                pe.wait_ge(s1_turnc, 4)
                pe.wait_ge(s1_wqc, 2)
                pe.wait_ge(s1_wcc, 8)
                queries(0, range(8))
                queries(1, range(4))
                scores(0)
                queries(1, range(4, 8))
                for i in range(8):
                    if i + 2 < 8:
                        queries(i + 2, range(4))
                    if i:
                        pv(i - 1)
                    if i + 2 < 8:
                        queries(i + 2, range(4, 8))
                    if i + 1 < 8:
                        scores(i + 1)
                pv(7)
                pe.wait_ge(s1_head, 16)
                for n in range(8):
                    half, r_out = n // 4, n % 4
                    for i in range(8):
                        last = pe.matmul(ps[:, FFN_BANK[n], :], wcomb[:, i, r_out, :],
                                         latent(i)[:, half * HALF:(half + 1) * HALF], start=(i == 0), stop=(i == 7))
                    last.then_inc(s1_out, 1)

            def turn_back(stage, ready):
                for what, count in ready:
                    pe.wait_ge(what, count)
                for g in range(NGROUP):
                    if g >= 2:
                        pe.wait_ge(s_added[stage], g - 1)
                    for j in range(G):
                        last = pe.transpose(ps[:, TURN[g % 2], j * P:(j + 1) * P],
                                            fresh[:, g * G + j, :, :].rearrange("t r c -> t (r c)"), ident[:, :])
                    last.then_inc(s_back[stage], 1)

            for st in stages:
                if st[0] == "c":
                    conv_stack(int(st[1]))
                if st == "a0":
                    attention0(0)
                    turn_back(0, ((s_fresh, 8 * NKV),))
                if st == "f0":
                    ffn(0)
                    turn_back(1, ((s_fact[0], 4), (s_fdve[0], 4)))
                if st == "a1":
                    attention1()
                    turn_back(2, ((s1_oact, 4), (s1_odve, 4)))
                if st == "f1":
                    ffn(1)
                    turn_back(3, ((s_fact[1], 4), (s_fdve[1], 4)))

        @block.scalar
        def _(act):
            act.wait_ge(s_setup, N_SETUP)
            act.activation(wsq[:, :, :, :], wsq[:, :, :, :], ACT.Square).then_inc(s_sq, 1)
            act.wait_ge(s_demod, 1)
            act.wait_ge(s_const, 2)
            act.activation(dval[:, :, :], ps[:, 1, :].rearrange("p (n b) -> p n b", b=B), ACT.Sqrt,
                           bias=eps[:, 0:1], scale=CONV_SCALE ** 2).then_inc(s_sqrt, 1)

            def conv_stack(net):
                if net == nets[0]:
                    act.wait_ge(s_scales, 1)
                for i in range(NGROUP // 2):
                    for layer, p in CONV_STEPS:
                        g = 2 * i + p
                        wide = layer in (1, 2)
                        if not wide and p == 1:
                            continue
                        bank = ps[:, WIDE[p][0] if wide else NARROW[p], :]
                        dst = [act1[:, p], act2[:, p, 0], act3[:, p, 0], act4[:, p]][layer]
                        off = 0 if layer == 3 else 1
                        act.wait_ge(s_conv[layer], done(net, 16) + 2 * g + 1 if wide else done(net, 8) + g + 1)
                        for j in range(G):
                            b = g * G + j
                            bias = cbias[:, net, 3:4] if layer == 3 else mid_bias[:, net, layer, b:b + 1]
                            last = act.activation(dst[:, j, off:off + T], bank[:, j * T:(j + 1) * T],
                                                  ACT.Identity, bias=bias, scale=mid_scale[:, net, layer, b:b + 1])
                        last.then_inc(s_eva[layer], 1)
                    g = 2 * i
                    act.wait_ge(s_turn, done(net, 8) + g + 1)
                    if net:
                        act.activation(tokens_of(g), turned(0), ACT.Copy).then_inc(s_xt[0], 1)
                    else:
                        act.activation(tokens_hi(g), turned(0), ACT.Copy).then_inc(s_xhi, 1)
                        act.wait_ge(s_wst, 16)
                        act.activation(w_hi[:, i, :], stage0[:, i, :], ACT.Copy).then_inc(s_whi, 1)

            def attention0():
                def values(i):
                    for v in range(4):
                        act.wait_ge(s_vt, 2 * i + v + 1)
                        if i:
                            act.wait_ge(s_pv, 8 * i)
                        act.activation(vals[:, :, 2 * v:2 * v + 2, :],
                                       ps[:, (2, 0, 1, 2)[v], :].rearrange("p (m h d) -> p h m d", m=2, h=2),
                                       ACT.Copy).then_inc(s_v, 1)

                def round_qkv(i):
                    act.wait_ge(s_wst, 16 * (part(i) + 1))
                    act.wait_ge(s_qkv, 10 * i)
                    act.wait_ge(s_vt, 4 * ((i - 1) // 2) + 4)
                    n = wcols(i)
                    stage = stage1.rearrange("p (r n) -> p r n", r=R)
                    for r in range(R):
                        act.activation(w_hi[:, r, 0:n], stage[:, r, 0:n], ACT.Copy).then_inc(s_whi, 1)

                def round_o(i):
                    act.wait_ge(s_wst, 16 * (part_o(i) + 1))
                    if i:
                        act.wait_ge(s_proj, 8 * i)
                    for g in range(GQ):
                        act.activation(wo_hi[:, g, :, :].rearrange("d r t -> d (r t)"),
                                       stage1[:, g * R * P:(g + 1) * R * P], ACT.Copy).then_inc(s_whi, 1)

                values(0)
                round_qkv(1)
                for i in range(NKV):
                    for t in range(2):
                        act.wait_ge(s_shift, 2 * i + t + 1)
                        x = probs[:, t, :, :].rearrange("p a b -> p (a b)")
                        act.activation(x, x, ACT.Exp, scale=R0_SCALE).then_inc(s_exp, 1)
                    round_o(i)
                    for q in range(NTILE):
                        act.wait_ge(s_pv, 8 * i + q + 1)
                        if q % 4 == 0 and (i or q):
                            act.wait_ge(s_proj, 8 * i + q)
                        act.activation(h_hi[:, :, (q % 4) * P:(q % 4 + 1) * P],
                                       ps[:, 5 + q % 2, :].rearrange("d (g n) -> d g n", g=GQ),
                                       ACT.Copy).then_inc(s_hhi, 1)
                    if i % 2 and i + 1 < NKV:
                        values(i + 1)
                    if i + 2 < NKV:
                        round_qkv(i + 2)

            def ffn(n):
                width = (NAT0, NAT1)[n]
                for q in range(4):
                    act.wait_ge(s_nat[n], q + 1)
                    act.activation(nat[:, 2 * q:2 * q + 2, 0:width],
                                   ps[:, q, :].rearrange("p (a b) -> p a b", a=2)[:, :, 0:width],
                                   ACT.Copy).then_inc(s_natc[n], 1)
                act.wait_ge(s_gate[n], 1)
                if n == 0:
                    act.activation(col[:, 1, :], col[:, 1, :], ACT.Sqrt, bias=rms_eps[:, 1:2],
                                   scale=1.0 / NGATE).then_inc(s_gact[n], 1)
                    act.wait_ge(s_gate[n], 2)
                    act.activation(col[:, 4, :], col[:, 4, :], ACT.Exp).then_inc(s_gact[n], 1)
                else:
                    act.activation(vote[:, 0], vote[:, 0], ACT.Exp).then_inc(s_gact[n], 1)
                for q in range(2):
                    act.wait_ge(s_lturn[n], q + 1)
                    act.activation(lora_t[:, q * HALF:(q + 1) * HALF], ps[:, 2 + q, :], ACT.Copy)\
                        .then_inc(s_lcopy[n], 1)
                for k in range(0, 8, 2):
                    half, r_out = k // 4, k % 4
                    act.wait_ge(s_ffn[n], k + 1)
                    act.activation(fresh[:, half * 16:half * 16 + 16, r_out, :],
                                   ps[:, FFN_BANK[k], :].rearrange("p (b c) -> p b c", c=C),
                                   ACT.Identity, bias=f1_bias[:, 0, r_out:r_out + 1] if n else 0.0)\
                        .then_inc(s_fact[n], 1)

            def attention1():
                def copy_projection(q):
                    act.wait_ge(s1_nat, q + 1)
                    act.activation(nat1[:, 2 * q:2 * q + 2, :],
                                   ps[:, q, :].rearrange("p (a b) -> p a b", a=2)[:, :, 0:QA + QK1],
                                   ACT.Copy).then_inc(s1_natc, 1)

                def copy_query_weights(q):
                    act.wait_ge(s1_wq, q + 1)
                    act.activation(wq1[:, 16 * q:16 * q + 16, ROT:QK1],
                                   ps[:, 4 + q, :].rearrange("p (h l) -> p h l", l=LAT), ACT.Copy).then_inc(s1_wqc, 1)

                def copy_output_weights(i):
                    act.wait_ge(s1_wc, i + 1)
                    act.activation(wcomb[:, i].rearrange("p r t -> p (r t)"), ps[:, 6 + i % 2, :], ACT.Copy)\
                        .then_inc(s1_wcc, 1)

                for i in range(8):
                    if i < 4:
                        copy_projection(i)
                    elif i % 2:
                        copy_query_weights(i // 2 - 2)
                    copy_output_weights(i)
                act.wait_ge(s1_sq, 1)
                act.activation(rms[:, 2, :], rms[:, 0, :], ACT.Sqrt, bias=rms_eps[:, 0:1], scale=1.0 / QA)\
                    .then_inc(s1_root, 1)
                act.activation(rms[:, 3, :], rms[:, 1, :], ACT.Sqrt, bias=rms_eps[:, 0:1], scale=1.0 / LAT)\
                    .then_inc(s1_root, 1)
                for q in range(2):
                    act.wait_ge(s1_turn, q + 1)
                    act.activation(qa_t[:, q * HALF:(q + 1) * HALF], ps[:, q, :], ACT.Copy,
                                   scale=a1_ln[:, 0, 0:1]).then_inc(s1_turnc, 1)
                for q in range(2):
                    act.wait_ge(s1_turn, q + 3)
                    act.activation(keys_t[0:QK1, q * HALF:(q + 1) * HALF], ps[0:QK1, 2 + q, :], ACT.Copy)\
                        .then_inc(s1_turnc, 1)
                for i in range(8):
                    for t in range(2):
                        act.wait_ge(s_shift, SOFT0 + 2 * i + t + 1)
                        x = probs1[:, t, :, :].rearrange("p a b -> p (a b)")
                        act.activation(x, x, ACT.Exp, scale=R1_SCALE).then_inc(s_exp, 1)
                    for t in range(2):
                        act.wait_ge(s1_flat, 2 * i + t + 1)
                        if i:
                            act.wait_ge(s1_pv, 2 * (i - 1) + t + 1)
                        for j in range(G):
                            q = slice(32 * j, 32 * j + 32)
                            last = act.activation(
                                probs1_t[q, 4 * t:4 * t + 4, :, j, :].rearrange("p a g q -> p (a g) q"),
                                flat[q, t, :, :], ACT.Copy)
                        last.then_inc(s1_place, 1)
                    for half in range(2):
                        act.wait_ge(s1_pv, 2 * i + half + 1)
                        act.activation(latent(i)[:, half * HALF:(half + 1) * HALF], ps[:, 5 + half, :],
                                       ACT.Copy).then_inc(s1_head, 1)
                for k in range(0, 8, 2):
                    half, r_out = k // 4, k % 4
                    act.wait_ge(s1_out, k + 1)
                    act.activation(fresh[:, half * 16:half * 16 + 16, r_out, :],
                                   ps[:, FFN_BANK[k], :].rearrange("p (b c) -> p b c", c=C),
                                   ACT.Copy).then_inc(s1_oact, 1)

            for st in stages:
                if st[0] == "c":
                    conv_stack(int(st[1]))
                if st == "a0":
                    attention0()
                if st == "f0":
                    ffn(0)
                if st == "a1":
                    attention1()
                if st == "f1":
                    ffn(1)

        @block.vector
        def _(dve):
            ch = Chain(dve, dve_steps)
            dve.memset(rms_eps[:, 0:1], RMS_EPS)
            dve.memset(rms_eps[:, 1:2], LN_EPS)
            dve.memset(ones[:, :], 1.0)
            dve.memset(eps[:, :], CONV_EPS).then_inc(s_const, 1)

            def zero_pads():
                rows_of = acts[:, :].rearrange("p (n t) -> p n t", t=T + 2)
                dve.memset(rows_of[:, :, 0:1], 0.0)
                dve.memset(rows_of[:, :, T + 1:T + 2], 0.0).then_inc(s_const, 1)

            zero_pads()
            dve.wait_ge(s_sq, 1)
            ch.link(dve.tensor_tensor(wsum[:, :, :], wsq[:, :, 0, :], wsq[:, :, 1, :], ALU.add))
            over_r = [C, NET * LAYER, R, C]
            ch.link(dve.tensor_tensor(wsum4[:, :, :].rearrange("i n (r o) -> i n r o", r=R),
                                      wsum[:, :, :].unsqueeze(2).broadcast_to(over_r),
                                      wsq[:, :, 2, :].unsqueeze(2).broadcast_to(over_r), ALU.add))
            dve.wait_ge(s_style, 1)
            ch.link(dve.tensor_tensor(sval[:, :, :], ps[:, 0, :].rearrange("p (n b) -> p n b", b=B),
                                      modb[:, :].unsqueeze(2).broadcast_to([P, NET * LAYER, B]), ALU.add))
            dve.tensor_tensor(ssq[:, :, :], sval[:, :, :], sval[:, :, :], ALU.mult).then_inc(s_sq, 1)
            conv_blocks(dve, ch, tmpw[:, 0, :], nets[0])
            dve.wait_ge(s_sqrt, 1)
            ch.link(dve.reciprocal(dval[:, :, :], dval[:, :, :]))
            s4 = sval[:, :, :].rearrange("p (n l) b -> p n l b", l=LAYER)
            d4 = dval[:, :, :].rearrange("p (n l) b -> p n l b", l=LAYER)
            dve.tensor_copy(in_scale[:, :, 0, :], s4[:, :, 0, :])
            dve.tensor_copy(in_scale[:, :, 1, :], d4[:, :, 1, :])
            dve.tensor_copy(in_scale[:, :, 2:4, :], s4[:, :, 2:4, :])
            ch.link(dve.tensor_scalar(cbias[:, :, 1], cbias[:, :, 1], 2.0, None, ALU.mult))
            for k in range(3):
                src = s4 if k == 1 else d4
                dve.scalar_tensor_tensor(mid_scale[:, :, k, :], src[:, :, k, :], CONV_SCALE, in_scale[:, :, k + 1, :],
                                         ALU.mult, ALU.mult)
                ch.mark(dve.tensor_tensor(mid_bias[:, :, k, :], in_scale[:, :, k + 1, :],
                                          cbias[:, :, k].unsqueeze(2).broadcast_to([P, NET, B]), ALU.mult))
            dve.tensor_scalar(mid_scale[:, :, 3, :], d4[:, :, 3, :], CONV_SCALE, None, ALU.mult)
            ch.wait()
            dve.tensor_scalar(edge[:, :, :], mid_bias[:, :, 1, :], -0.125, None, ALU.mult).then_inc(s_scales, 1)

            def conv_stack(net):
                for i in range(NGROUP // 2):
                    for layer, p in CONV_STEPS:
                        g = 2 * i + p
                        wide = layer in (1, 2)
                        if not wide and p == 0:
                            continue
                        bank = ps[:, WIDE[p][1] if wide else NARROW[p], :]
                        dst = [act1[:, p], act2[:, p, 1], act3[:, p, 1], act4[:, p]][layer]
                        off = 0 if layer == 3 else 1
                        dve.wait_ge(s_conv[layer], done(net, 16) + 2 * g + 2 if wide else done(net, 8) + g + 1)
                        for j in range(G):
                            b = g * G + j
                            bias = cbias[:, net, 3:4] if layer == 3 else mid_bias[:, net, layer, b:b + 1]
                            last = dve.tensor_scalar(dst[:, j, off:off + T], bank[:, j * T:(j + 1) * T],
                                                     mid_scale[:, net, layer, b:b + 1], bias, ALU.mult, ALU.add)
                        if layer == 1:
                            ch.link(last)
                            samples = slice(g * G, (g + 1) * G)
                            end = act2[96:128, p, 1, :, T]
                            dve.tensor_tensor(end, end, edge[96:128, net, samples], ALU.add)
                            dve.wait_ge(s_eva[layer], done(net, 8) + g + 1)
                            end = act2[0:32, p, 0, :, 1]
                            last = dve.tensor_tensor(end, end, edge[0:32, net, samples], ALU.add)
                        last.then_inc(s_evd[layer], 1)
                    g = 2 * i + 1
                    dve.wait_ge(s_turn, done(net, 8) + g + 1)
                    if net:
                        dve.tensor_copy(tokens_of(g), turned(1)).then_inc(s_xt[1], 1)
                        continue
                    ch.link(dve.tensor_copy(tokens_hi(g), turned(1)))
                    dve.tensor_tensor(tokens_lo(g), turned(1), tokens_hi(g).bitcast(F32), ALU.subtract)\
                        .then_inc(s_xt[1], 1)
                    dve.wait_ge(s_xhi, i + 1)
                    dve.tensor_tensor(tokens_lo(g - 1), turned(0), tokens_hi(g - 1).bitcast(F32), ALU.subtract)\
                        .then_inc(s_xt[0], 1)

            def soft_pull(i, n0, probs):
                for t in range(2):
                    dve.wait_ge(s_score, n0 + 2 * i + t + 1)
                    dve.transpose(probs[:, t, :, :].rearrange("p a b -> p (a b)"), ps[:, 3 + t, :])\
                        .then_inc(s_pull, 1)

            def soft_max(i, n0, probs, stat):
                for t in range(2):
                    dve.wait_ge(s_masked, n0 + 2 * i + t + 1)
                    dve.tensor_reduce(stat[:, t, 0, :], probs[:, t, :, :], AX.X, ALU.max).then_inc(s_max, 1)

            def soft_sum(i, n0, probs, stat):
                for t in range(2):
                    dve.wait_ge(s_exp, n0 + 2 * i + t + 1)
                    ch.link(dve.tensor_reduce(stat[:, t, 1, :], probs[:, t, :, :], AX.X, ALU.add))
                    dve.reciprocal(stat[:, t, 1, :], stat[:, t, 1, :]).then_inc(s_recip, 1)

            def soft_turn(i, n0, probs, turned, used, per):
                for t in range(2):
                    dve.wait_ge(s_prob, n0 + 2 * i + t + 1)
                    if i:
                        dve.wait_ge(used, per * i)
                    for j in range(G):
                        q = slice(32 * j, 32 * j + 32)
                        last = dve.transpose(turned[q, 4 * t:4 * t + 4, :, j, :].rearrange("p a g q -> p (a g) q"),
                                             probs[q, t, :, :])
                    last.then_inc(s_pt, 1)

            def attention0():
                cos = rope0[:, 0, :]
                sin = rope0[:, 1, :]

                def rotate(i, k):
                    dve.wait_ge(s_qkv, 10 * i + k + 1)
                    n = 10 * i + k
                    if n >= 2:
                        dve.wait_ge(s_rope, n - 1)
                    x = ps[:, k % 3, :].rearrange("p (b s) -> p b s", s=C)
                    y = rot[:, k % 2, :, :].rearrange("p a (b s) -> p a b s", s=C)
                    dve.tensor_tensor(y[:, 0], x, cos.unsqueeze(1).broadcast_to([P, HALF // C, C]), ALU.mult)
                    for h in range(2):
                        src, dst = slice(64 * h, 64 * h + 64), slice(64 - 64 * h, 128 - 64 * h)
                        last = dve.tensor_tensor(y[dst, 1], x[src],
                                                 sin[src].unsqueeze(1).broadcast_to([64, HALF // C, C]), ALU.mult)
                    last.then_inc(s_rot, 1)

                def split_heads(i, tiles):
                    for q in tiles:
                        dve.wait_ge(s_hhi, 8 * i + q + 1)
                        cols = slice((q % 4) * P, (q % 4 + 1) * P)
                        dve.tensor_tensor(h_lo[:, :, cols], ps[:, 5 + q % 2, :].rearrange("d (g n) -> d g n", g=GQ),
                                          h_hi[:, :, cols].bitcast(F32), ALU.subtract).then_inc(s_head, 1)

                def add_projection(i, tiles):
                    for n in tiles:
                        half, r = n // 4, n % 4
                        dve.wait_ge(s_proj, 8 * i + n + 1)
                        dst = fresh[:, half * 16:half * 16 + 16, r, :]
                        dve.tensor_tensor(dst, ps[:, (7, 2, 0, 1)[r], :].rearrange("p (b c) -> p b c", c=C), dst,
                                          ALU.add).then_inc(s_fresh, 1)

                for k in range(10):
                    rotate(0, k)
                dve.wait_ge(s_zero, 2)
                for i in range(NKV):
                    soft_pull(i, 0, probs)
                    for k in range(10):
                        if i + 1 < NKV:
                            rotate(i + 1, k)
                        if k == 0:
                            soft_max(i, 0, probs, stat)
                        if k == 3:
                            soft_sum(i, 0, probs, stat)
                        if k == 6:
                            soft_turn(i, 0, probs, probs_t, s_pv, 8)
                        if k == 7:
                            split_heads(i, range(4))
                    add_projection(i, range(4))
                    split_heads(i, range(4, 8))
                    add_projection(i, range(4, 8))

            def add_back(stage):
                for g in range(NGROUP):
                    dve.wait_ge(s_back[stage], g + 1)
                    x = stream[:, g * G:(g + 1) * G, :]
                    dve.tensor_tensor(x, ps[:, TURN[g % 2], :].rearrange("p (b t) -> p b t", t=T), x, ALU.add)\
                        .then_inc(s_added[stage], 1)

            def over(x, shape):
                return x.unsqueeze(len(shape) - 1).broadcast_to(shape)

            def choose(v, first, second, m1, m2, key, top):
                shape = [P, NTILE, NE]
                rank = rank_const[:, :].unsqueeze(1).broadcast_to(shape)
                for src, hot, most in ((v, first, m1), (key, second, m2)):
                    ch.link(dve.tensor_reduce(most, src, AX.X, ALU.max))
                    ch.link(dve.tensor_tensor(hot, src, over(most, shape), ALU.is_equal))
                    ch.link(dve.tensor_tensor(hot, hot, rank, ALU.mult))
                    ch.link(dve.tensor_reduce(top, hot, AX.X, ALU.max))
                    ch.link(dve.tensor_tensor(hot, hot, over(top, shape), ALU.is_equal))
                    if hot is first:
                        ch.link(dve.scalar_tensor_tensor(key, first, MASKED, v, ALU.mult, ALU.add))

            def gate0():
                row = lambda k, n: f0_rows[:, 0, k:k + n]
                tiles = [P, NTILE, NGATE]
                shape = [P, NTILE, NE]
                per_tile = lambda x: x.unsqueeze(1).broadcast_to([P, NTILE, x.shape[-1]])
                dve.wait_ge(s_fw[0], 64)
                dve.wait_ge(s_natc[0], 4)
                ch.link(dve.tensor_tensor(gate_a, nat[:, :, 0:NGATE], per_tile(row(0, NGATE)), ALU.add))
                ch.link(dve.tensor_reduce(col[:, 0, :], gate_a, AX.X, ALU.add))
                ch.link(dve.tensor_scalar(col[:, 0, :], col[:, 0, :], 1.0 / NGATE, None, ALU.mult))
                ch.link(dve.tensor_tensor(gate_a, gate_a, over(col[:, 0, :], tiles), ALU.subtract))
                ch.link(dve.tensor_tensor(gate_b, gate_a, gate_a, ALU.mult))
                dve.tensor_reduce(col[:, 1, :], gate_b, AX.X, ALU.add).then_inc(s_gate[0], 1)
                dve.wait_ge(s_gact[0], 1)
                ch.link(dve.reciprocal(col[:, 1, :], col[:, 1, :]))
                ch.link(dve.tensor_tensor(gate_a, gate_a, over(col[:, 1, :], tiles), ALU.mult))
                ch.link(dve.tensor_tensor(gate_a, gate_a, per_tile(row(NGATE, NGATE)), ALU.mult))
                ch.link(dve.tensor_tensor(gate_a, gate_a, per_tile(row(2 * NGATE, NGATE)), ALU.add))
                ch.link(dve.tensor_scalar(gate_a, gate_a, 0.0, None, ALU.max))
                big = [P, NTILE, NE, NGATE]
                w2 = row(3 * NGATE, NE * NGATE).rearrange("p (e k) -> p e k", e=NE)
                ch.link(dve.tensor_tensor(gate_p, gate_a.unsqueeze(2).broadcast_to(big),
                                          w2.unsqueeze(1).broadcast_to(big), ALU.mult))
                gates, first, second, key, w = (vote[:, n] for n in range(5))
                ch.link(dve.tensor_reduce(gates, gate_p, AX.X, ALU.add))
                ch.link(dve.tensor_tensor(gates, gates, per_tile(row(3 * NGATE + NE * NGATE, NE)), ALU.add))
                first, second = both[:, :, 0, :], both[:, :, 1, :]
                choose(gates, first, second, col[:, 2, :], col[:, 3, :], key, col[:, 5, :])
                dve.tensor_tensor(col[:, 4, :], col[:, 3, :], col[:, 2, :], ALU.subtract).then_inc(s_both, 1)
                dve.engine_nop().then_inc(s_gate[0], 1)
                dve.wait_ge(s_gact[0], 2)
                ch.link(dve.tensor_scalar(col[:, 5, :], col[:, 4, :], 1.0, None, ALU.add))
                ch.link(dve.reciprocal(col[:, 5, :], col[:, 5, :]))
                ch.link(dve.tensor_tensor(col[:, 6, :], col[:, 5, :], col[:, 4, :], ALU.mult))
                dve.wait_ge(s_count, 1)
                ch.link(dve.tensor_reduce(count[:, 0, :], ps[:, 2, 0:P].rearrange("p (m k) -> p k m", m=NTILE),
                                          AX.X, ALU.add))
                ch.link(dve.tensor_scalar(count[:, 1, :], count[:, 0, :], float(CAPACITY), LORA0, ALU.is_le, ALU.mult))
                for n, g in ((0, 5), (1, 6)):
                    hot = both[:, :, n, :]
                    ch.link(dve.tensor_tensor(hot, hot, per_tile(count[:, 1, n * NE:(n + 1) * NE]), ALU.mult))
                    ch.link(dve.tensor_tensor(hot, hot, over(col[:, g, :], shape), ALU.mult))
                ch.link(dve.tensor_tensor(w, first, second, ALU.add))
                weigh(0, w, NGATE)

            def weigh(n, w, at):
                x = nat[:, :, at:at + P].rearrange("p m (e k) -> p m e k", e=NE)
                dve.tensor_tensor(x, x, w.unsqueeze(3).broadcast_to([P, NTILE, NE, RANK]), ALU.mult)\
                    .then_inc(s_lora[n], 1)

            def gate1():
                shape = [P, NTILE, NE]
                p, first, second, key, w = (vote[:, n] for n in range(5))
                dve.wait_ge(s_natc[1], 4)
                ch.link(dve.tensor_reduce(col[:, 0, :], nat[:, :, 0:NE], AX.X, ALU.max))
                dve.tensor_tensor(p, nat[:, :, 0:NE], over(col[:, 0, :], shape), ALU.subtract).then_inc(s_gate[1], 1)
                dve.wait_ge(s_gact[1], 1)
                ch.link(dve.tensor_reduce(col[:, 1, :], p, AX.X, ALU.add))
                ch.link(dve.reciprocal(col[:, 1, :], col[:, 1, :]))
                ch.link(dve.tensor_tensor(p, p, over(col[:, 1, :], shape), ALU.mult))
                choose(p, first, second, col[:, 2, :], col[:, 3, :], key, col[:, 5, :])
                ch.link(dve.tensor_tensor(col[:, 4, :], col[:, 2, :], col[:, 3, :], ALU.add))
                ch.link(dve.reciprocal(col[:, 4, :], col[:, 4, :]))
                ch.link(dve.tensor_tensor(w, first, second, ALU.add))
                ch.link(dve.tensor_tensor(w, w, p, ALU.mult))
                ch.link(dve.tensor_scalar(col[:, 4, :], col[:, 4, :], LORA1, None, ALU.mult))
                ch.link(dve.tensor_tensor(w, w, over(col[:, 4, :], shape), ALU.mult))
                weigh(1, w, NE)

            def ffn(n):
                (gate0, gate1)[n]()
                for k in range(1, 8, 2):
                    half, r_out = k // 4, k % 4
                    dve.wait_ge(s_ffn[n], k + 1)
                    dst = fresh[:, half * 16:half * 16 + 16, r_out, :]
                    src = ps[:, FFN_BANK[k], :].rearrange("p (b c) -> p b c", c=C)
                    if n:
                        last = dve.tensor_scalar(dst, src, f1_bias[:, 0, r_out:r_out + 1], None, ALU.add)
                    else:
                        last = dve.tensor_copy(dst, src)
                    last.then_inc(s_fdve[n], 1)

            def attention1():
                dve.wait_ge(s1_w, 80)
                dve.wait_ge(s1_natc, 4)
                q, pe1, pe2, lat = (nat1[:, :, x:y] for x, y in ((0, QA), (QA, QA + 32), (QA + 32, QA + 64),
                                                                (QA + 64, QA + 96)))
                sq, t1 = tmp_k[:, 0], tmp_k[:, 1]
                ch.link(dve.tensor_tensor(sq, q, q, ALU.mult))
                ch.link(dve.tensor_reduce(rms[:, 0, :], sq, AX.X, ALU.add))
                ch.link(dve.tensor_tensor(t1[:, :, 0:LAT], lat, lat, ALU.mult))
                dve.tensor_reduce(rms[:, 1, :], t1[:, :, 0:LAT], AX.X, ALU.add).then_inc(s1_sq, 1)
                cos, sin = (rope1r[:, n, :].unsqueeze(1).broadcast_to([P, NTILE, 32]) for n in range(2))
                parts = [sq[:, :, 32 * n:32 * n + 32] for n in range(4)]
                ch.wait()
                for dst, x, y in zip(parts, (pe1, pe2, pe2, pe1), (cos, sin, cos, sin)):
                    ch.mark(dve.tensor_tensor(dst, x, y, ALU.mult))
                ch.wait()
                dve.tensor_tensor(keys_n[:, :, 0:32], parts[0], parts[1], ALU.subtract)
                dve.tensor_tensor(keys_n[:, :, 32:64], parts[2], parts[3], ALU.add)
                dve.wait_ge(s1_root, 2)
                ch.link(dve.reciprocal(rms[:, 2:4, :], rms[:, 2:4, :]))
                dve.tensor_tensor(q, q, over(rms[:, 2, :], [P, NTILE, QA]), ALU.mult).then_inc(s1_qn, 1)
                ch.link(dve.tensor_tensor(values1, lat, over(rms[:, 3, :], [P, NTILE, LAT]), ALU.mult))
                ch.link(dve.tensor_tensor(values1, values1, a1_ln[:, 0, 1:1 + LAT].unsqueeze(1)
                                          .broadcast_to([P, NTILE, LAT]), ALU.mult))
                dve.tensor_copy(keys_n[:, :, 64:96], values1).then_inc(s1_kn, 1)

                def rotate(i, k):
                    dve.wait_ge(s1_q, 8 * i + k + 1)
                    n = 8 * i + k
                    if n >= 2:
                        dve.wait_ge(s1_rope, n - 1)
                    x = ps[0:QK1, (0, 1, 2, 7)[k % 4], :].rearrange("p (b s) -> p b s", s=C)
                    y = rot1[0:QK1, k % 2, :, :].rearrange("p a (b s) -> p a b s", s=C)
                    dve.tensor_tensor(y[:, 0], x, rope1c[0:QK1, 0, :].unsqueeze(1)
                                      .broadcast_to([QK1, HALF // C, C]), ALU.mult)
                    for h in range(2):
                        src, dst = slice(32 * h, 32 * h + 32), slice(32 - 32 * h, 64 - 32 * h)
                        last = dve.tensor_tensor(y[dst, 1], x[src], rope1c[src, 1, :].unsqueeze(1)
                                                 .broadcast_to([32, HALF // C, C]), ALU.mult)
                    last.then_inc(s1_rot, 1)

                ch.link(dve.memset(rot1[64:96, :, 1, :], 0.0))
                dve.wait_ge(s1_zero, 1)
                def turn_flat(i):
                    for t in range(2):
                        dve.wait_ge(s_prob, SOFT0 + 2 * i + t + 1)
                        if i:
                            dve.wait_ge(s1_place, 2 * (i - 1) + t + 1)
                        dve.transpose(flat[:, t, :, :].rearrange("p a b -> p (a b)"),
                                      probs1[:, t, :, :].rearrange("p a b -> p (a b)")).then_inc(s1_flat, 1)

                for k in range(16):
                    rotate(k // 8, k % 8)
                for i in range(8):
                    if i:
                        dve.wait_ge(s1_flat, 2 * i)
                    soft_pull(i, SOFT0, probs1)
                    for k in range(8):
                        if i + 2 < 8:
                            rotate(i + 2, k)
                        if k == 0:
                            soft_max(i, SOFT0, probs1, stat1)
                        if k == 3:
                            soft_sum(i, SOFT0, probs1, stat1)
                        if k == 6:
                            turn_flat(i)
                for k in range(1, 8, 2):
                    half, r_out = k // 4, k % 4
                    dve.wait_ge(s1_out, k + 1)
                    dve.tensor_copy(fresh[:, half * 16:half * 16 + 16, r_out, :],
                                    ps[:, FFN_BANK[k], :].rearrange("p (b c) -> p b c", c=C)).then_inc(s1_odve, 1)

            for st in stages:
                if st[0] == "c":
                    conv_stack(int(st[1]))
                if st == "a0":
                    dve.wait_ge(s_const_loaded, 48)
                    attention0()
                    dve.wait_ge(s_wlo, 16)
                    zero_pads()
                    dve.wait_ge(s_again, 16)
                    add_back(0)
                if st == "f0":
                    ffn(0)
                    add_back(1)
                if st == "a1":
                    attention1()
                    dve.wait_ge(s_score, SOFT0 + 16)
                    dve.wait_ge(s1_place, 16)
                    zero_pads()
                    add_back(2)
                if st == "f1":
                    ffn(1)
                    add_back(3)

        @block.gpsimd
        def _(pool):
            ch = Chain(pool, pool_steps)
            pool.wait_ge(s_setup, N_SETUP)
            pool.wait_ge(s_scales, 1)

            def conv_stack(net):
                for g in range(NGROUP):
                    if net != nets[0]:
                        pool.wait_ge(s_added[net - 1], g + 1)
                    elif g % 2 == 0:
                        pool.wait_ge(s_stream[g // 2], 16)
                    if g >= 2:
                        pool.wait_ge(s_conv[0], done(net, 8) + g - 1)
                    pool.tensor_tensor(act0[:, g % 2, :, 1:T + 1], stream[:, g * G:(g + 1) * G, :],
                                       in_scale[:, net, 0, g * G:(g + 1) * G].unsqueeze(2).broadcast_to([P, G, T]),
                                       ALU.mult).then_inc(s_in, 1)
                    if net == nets[0] and g in (3, 5, 7) and (g - 1) // 2 < len(nets):
                        conv_blocks(pool, ch, tmpw[:, 1, :], nets[(g - 1) // 2])

            def soft_mask(i, n0, probs):
                for t in range(2):
                    pool.wait_ge(s_pull, n0 + 2 * i + t + 1)
                    pool.tensor_tensor(probs[:, t], probs[:, t], causal[:, :].unsqueeze(1)
                                       .broadcast_to([P, 16, C]), ALU.add).then_inc(s_masked, 1)

            def soft_shift(i, n0, probs, stat):
                for t in range(2):
                    pool.wait_ge(s_max, n0 + 2 * i + t + 1)
                    pool.tensor_tensor(probs[:, t], probs[:, t], stat[:, t, 0, :].unsqueeze(2)
                                       .broadcast_to([P, 16, C]), ALU.subtract).then_inc(s_shift, 1)

            def soft_scale(i, n0, probs, stat):
                for t in range(2):
                    pool.wait_ge(s_recip, n0 + 2 * i + t + 1)
                    pool.tensor_tensor(probs[:, t], probs[:, t], stat[:, t, 1, :].unsqueeze(2)
                                       .broadcast_to([P, 16, C]), ALU.mult).then_inc(s_prob, 1)

            def attention1():
                pool.wait_ge(s1_wcc, 8)
                pool.wait_ge(s1_wqc, 2)
                pool.memset(made, 0.0).then_inc(s1_zero, 1)
                pool.wait_ge(s1_zero, 1)

                def rope_add(i, k):
                    n = 8 * i + k
                    pool.wait_ge(s1_rot, n + 1)
                    if i >= 2 and k == 0:
                        pool.wait_ge(s_score, SOFT0 + 2 * (i - 1))
                    pool.tensor_tensor(q1[i % 2][0:QK1, k // 2, (k % 2) * HALF:(k % 2 + 1) * HALF],
                                       rot1[0:QK1, k % 2, 0, :], rot1[0:QK1, k % 2, 1, :],
                                       ALU.add).then_inc(s1_rope, 1)

                for k in range(16):
                    rope_add(k // 8, k % 8)
                for i in range(8):
                    soft_mask(i, SOFT0, probs1)
                    for k in range(8):
                        if i + 2 < 8:
                            rope_add(i + 2, k)
                        if k == 1:
                            soft_shift(i, SOFT0, probs1, stat1)
                        if k == 4:
                            soft_scale(i, SOFT0, probs1, stat1)

            def attention0():
                def rope_add(i, k):
                    n = 10 * i + k
                    pool.wait_ge(s_rot, n + 1)
                    if i and k == 0:
                        pool.wait_ge(s_score, 2 * i)
                    pool.tensor_tensor(qk[:, k // 2, (k % 2) * HALF:(k % 2 + 1) * HALF], rot[:, k % 2, 0, :],
                                       rot[:, k % 2, 1, :], ALU.add).then_inc(s_rope, 1)

                stage = stage1.rearrange("p (r n) -> p r n", r=R)

                def split_qkv(i):
                    n = wcols(i)
                    src = stage if i else stage0
                    for r in range(R):
                        pool.wait_ge(s_whi, R * part(i) + r + 1)
                        last = pool.tensor_tensor(w_lo[:, r, 0:n], src[:, r, 0:n], w_hi[:, r, 0:n].bitcast(F32),
                                                  ALU.subtract)
                    last.then_inc(s_wlo, 1)

                def split_o(i):
                    for g in range(GQ):
                        pool.wait_ge(s_whi, R * part_o(i) + g + 1)
                        last = pool.tensor_tensor(wo_lo[:, g, :, :].rearrange("d r t -> d (r t)"),
                                                  stage1[:, g * R * P:(g + 1) * R * P],
                                                  wo_hi[:, g, :, :].rearrange("d r t -> d (r t)").bitcast(F32),
                                                  ALU.subtract)
                    last.then_inc(s_wlo, 1)

                split_qkv(0)
                pool.memset(fresh[:, :, :, :], 0.0).then_inc(s_zero, 1)
                pool.memset(probs_t[:, :, :, :, :], 0.0).then_inc(s_zero, 1)
                for k in range(10):
                    rope_add(0, k)
                split_qkv(1)
                for i in range(NKV):
                    soft_mask(i, 0, probs)
                    for k in range(10):
                        if i + 1 < NKV:
                            rope_add(i + 1, k)
                        if k == 1:
                            soft_shift(i, 0, probs, stat)
                        if k == 4:
                            soft_scale(i, 0, probs, stat)
                        if k == 7:
                            split_o(i)
                    if i + 2 < NKV:
                        split_qkv(i + 2)

            for st in stages:
                if st[0] == "c":
                    conv_stack(int(st[1]))
                if st == "a0":
                    attention0()
                if st == "a1":
                    attention1()

def lay_out(inp):
    a = {}
    a["x"] = inp["x"].reshape(B, C, T, R).transpose(3, 1, 0, 2).reshape(P, B, T)
    a["style"] = inp["cond_512"].T
    nets = ["L0_cond", "L0_cond2", "L1_cond", "L1_cond2"]
    n = NET * LAYER
    mod_w = np.stack([inp[k + "_mod_w"] for k in nets]).reshape(n, 1, C, STYLE)
    a["modw"] = np.broadcast_to(mod_w, (n, R, C, STYLE)).reshape(n, P, STYLE).transpose(2, 0, 1)
    mod_b = np.stack([inp[k + "_mod_b"] for k in nets]).reshape(n, 1, C)
    a["modb"] = np.broadcast_to(mod_b, (n, R, C)).reshape(n, P).T
    bias = np.stack([inp[k + "_biases"] for k in nets]).reshape(NET, LAYER, 1, C)
    a["cbias"] = np.broadcast_to(bias, (NET, LAYER, R, C)).reshape(NET, LAYER, P).transpose(2, 0, 1)
    w = np.stack([inp[k + "_weights"] for k in nets]).reshape(NET, LAYER, C, C, TAPS)
    by_in = w.transpose(3, 0, 1, 4, 2)
    a["wsq"] = by_in.reshape(C, n, TAPS, C)
    contracted = by_in.copy()
    contracted[:, :, 1] = w.transpose(2, 0, 1, 4, 3)[:, :, 1]
    a["wrep"] = contracted.reshape(C, n, TAPS, C)

    qkv = inp["L0_attn_Wqkv"].reshape((NH + 2 * NKV) * HD, T, R)
    q = qkv[:NH * HD].reshape(NKV, GQ, HD, T, R)
    k = qkv[NH * HD:(NH + NKV) * HD].reshape(NKV, 1, HD, T, R)
    v = qkv[(NH + NKV) * HD:].reshape(NKV, 1, HD, T, R)
    v2 = np.concatenate([v, np.roll(v, -1, 0)], 1)
    a["w_qkv"] = np.concatenate([k, q, v2], 1).transpose(0, 3, 4, 1, 2).reshape(NKV, T, R, 7 * HD)
    a["w_o"] = inp["L0_attn_Wo"].reshape(T, R, NKV, GQ, HD).transpose(2, 4, 3, 1, 0)

    def into(x):
        return x.reshape(x.shape[0], T, R).transpose(1, 2, 0)

    def out_of(x):
        return x.reshape(T, R, x.shape[1]).transpose(2, 1, 0)

    def rows(*vs):
        v = np.concatenate([x.reshape(-1) for x in vs])
        return np.broadcast_to(v, (P, v.size))

    lora_a = inp["L0_ffn_lora_A"].transpose(0, 2, 1).reshape(NE * RANK, L)
    a["f0_in"] = np.concatenate([into(inp["L0_ffn_gw1"]), into(lora_a)], 2)
    a["f0_main"] = inp["L0_ffn_weight"].reshape(T, R, T, R).transpose(2, 3, 1, 0)
    a["f0_out"] = out_of(inp["L0_ffn_lora_B"].transpose(2, 0, 1).reshape(L, NE * RANK))
    a["f0_rows"] = rows(*(inp["L0_ffn_" + k] for k in ("gb1", "ln_gamma", "ln_beta", "gw2", "gb2")))
    a["f1_in"] = np.concatenate([into(inp["L1_ffn_W_router"]), into(inp["L1_ffn_A"].reshape(NE * RANK, L))], 2)
    a["f1_main"] = inp["L1_ffn_W_base"].reshape(T, R, T, R).transpose(2, 3, 1, 0)
    a["f1_out"] = out_of(inp["L1_ffn_B"].transpose(1, 0, 2).reshape(L, NE * RANK))
    a["f1_bias"] = inp["L1_ffn_b_base"].reshape(T, R)

    kv_a = inp["L1_attn_wkv_a"]
    a["a1_in"] = np.concatenate([into(inp["L1_attn_wq_a"]), into(kv_a[LAT::2]), into(kv_a[LAT + 1::2]),
                                 into(kv_a[:LAT])], 2)
    q_b = inp["L1_attn_wq_b"].reshape(NH, NOPE + ROT, QA)
    a["a1_pe"] = np.concatenate([q_b[:, NOPE::2], q_b[:, NOPE + 1::2]], 1).transpose(2, 0, 1)
    a["a1_nope"] = q_b[:, :NOPE].reshape(NH // 2, 2 * NOPE, QA).transpose(1, 0, 2)
    kv_b = inp["L1_attn_wkv_b"].reshape(NH, NOPE + VD, LAT)
    pairs = np.zeros((2, NOPE, NH // 2, 2, LAT), np.float32)
    for h in range(2):
        pairs[h, :, :, h] = kv_b[h::2, :NOPE].transpose(1, 0, 2)
    a["a1_kb"] = pairs.reshape(2 * NOPE, NH // 2, 2 * LAT)
    a["a1_v"] = kv_b[:, NOPE:].transpose(1, 0, 2)
    a["a1_wo"] = inp["L1_attn_wo"].reshape(T, R, NH // GQ, GQ, VD).transpose(2, 4, 3, 1, 0)\
        .reshape(NH // GQ, VD, GQ, L)
    a["a1_ln"] = np.concatenate([inp["L1_attn_q_a_ln_w"].reshape(QA, 1), rows(inp["L1_attn_kv_a_ln_w"])], 1)

    a["factor"] = tap_factors().reshape(P, TAPS, NBLKS)
    a["ident"] = np.eye(P, dtype=np.float32)
    a["rope0"] = rope0_tables().reshape(P, 2, C)
    a["rope1r"] = rope1_rows().reshape(P, 2, LAT)
    a["rope1c"] = rope1_cols()
    a["causal"] = causal_mask()
    a["rank"] = np.tile(np.arange(NE, 0, -1, dtype=np.float32), (P, 1))
    return {k: np.ascontiguousarray(v) for k, v in a.items()}


def kernel(**inputs):
    import concourse.bacc as bacc
    from concourse.bass_utils import run_bass_kernel_spmd

    arrays = lay_out({k: np.asarray(v) for k, v in inputs.items()})
    nc = bacc.Bacc("TRN2", target_bir_lowering=False, num_devices=1)
    args = {k: nc.dram_tensor(f"in_{k}_dram", v.shape, F32, kind="ExternalInput").ap() for k, v in arrays.items()}
    out = nc.dram_tensor("out_dram", (P, B, T), F32, kind="ExternalOutput").ap()
    build(nc, args, out)
    r = run_bass_kernel_spmd(nc, [{f"in_{k}_dram": v for k, v in arrays.items()}], core_ids=[0])
    y = r.results[0]["out_dram"]
    return y.reshape(R, C, B, T).transpose(2, 1, 3, 0).reshape(B, C, L)
```

```python
import math
from contextlib import ExitStack

import numpy as np
import concourse.bass as bass
from concourse import mybir

F32 = mybir.dt.float32
F32R = mybir.dt.float32r
ACT = mybir.ActivationFunctionType
ALU = mybir.AluOpType
AX = mybir.AxisListType

B, C, L = 32, 32, 512
P = 128
R = P // C
T = L // R
G = 4
NGROUP = B // G
TOK = B * C
NTILE = TOK // P
HALF = 512
NHALF = TOK // HALF
NET, LAYER, TAPS = 4, 4, 3
STYLE = 64
CONV_SCALE = 1.0 / float(np.sqrt(C * TAPS ** 2))
CONV_EPS = 1e-8
HD, NH, NKV = 128, 32, 8
GQ = NH // NKV
MASKED = -1e30
R0_SCALE = 1.0 / float(np.sqrt(HD))

PLAIN = (0, 1, 2, 3)
ORDER_A, ORDER_B = (0, 3, 1, 2), (5, 6, 4, 7)


def shifted(order, by):
    return tuple(p + by for p in order)


BLOCKS = [
    [(PLAIN, po) for po in range(4)] + [(shifted(PLAIN, -4), 0), (shifted(PLAIN, 4), 3)],
    [(PLAIN, po) for po in range(8)] + [(shifted(PLAIN, -4), po) for po in (0, 1)]
    + [(shifted(PLAIN, 4), po) for po in (6, 7)],
    [(PLAIN, po) for po in ORDER_A] + [(PLAIN, po - 4) for po in ORDER_B]
    + [(shifted(PLAIN, -4), 0), (shifted(PLAIN, 4), 3)],
    [(ORDER_A, po) for po in range(4)] + [(ORDER_B, po) for po in range(4)]
    + [(shifted(ORDER_B, -8), 0), (shifted(ORDER_A, 8), 3)],
]
NBLK = [len(b) for b in BLOCKS]
BLK0 = [sum(NBLK[:n]) for n in range(LAYER)]
NBLKS = sum(NBLK)
FFN_BANK = (4, 5, 6, 7, 0, 1, 2, 3)
CONV_STEPS = [(layer, p) for layer in range(LAYER) for p in range(2)]
ADD = dict(start=False, stop=True, skip_group_check=True)
BLUR = [1 / 8, 3 / 8, 3 / 8, 1 / 8]


def tap_factor(layer, pi, po, k):
    if layer == 1:
        j = 2 * pi + k - po + 1
        return 2 * BLUR[j] if 0 <= j < 4 else 0.0
    if layer == 3:
        j = pi - 2 * po - k + 2
        return BLUR[j] if 0 <= j < 4 else 0.0
    return 1.0 if pi - po + 1 == k else 0.0


def tap_factors():
    out = np.zeros((R, C, TAPS, NBLKS), np.float32)
    for layer in range(LAYER):
        for n, (pi, po) in enumerate(BLOCKS[layer]):
            for r in range(R):
                for k in range(TAPS):
                    out[r, :, k, BLK0[layer] + n] = tap_factor(layer, pi[r], po, k)
    return out.reshape(P, TAPS * NBLKS)


def rope0_tables():
    inv = (1.0 / np.float32(10000.0) ** (np.arange(0, HD, 2, dtype=np.float32) / HD)).astype(np.float32)
    f = np.outer(np.arange(C, dtype=np.float32), inv).astype(np.float32).T
    cos, sin = np.cos(f), np.sin(f)
    return np.concatenate([np.concatenate([cos, cos]), np.concatenate([sin, -sin])], 1).astype(np.float32)


def block_mask():
    return np.repeat(np.eye(R, dtype=np.float32), C, 0)


def causal_mask():
    q, k = np.mgrid[0:C, 0:C]
    return np.tile(np.where(k <= q, 0.0, MASKED), (R, 1)).astype(np.float32)


NE, RANK, TOPK = 8, 16, 2
NGATE = 32
NAT0, NAT1 = NGATE + NE * RANK, NE + NE * RANK
CAPACITY = int(3.0 * TOK / NE)
LN_EPS = 1e-5
LORA0, LORA1 = 1.0 / RANK, 32 / RANK

QA, LAT, ROT, NOPE, VD = 128, 32, 64, 64, 128
QK1 = ROT + LAT
RMS_EPS = 1e-6
R1_SCALE = (NOPE + ROT) ** (-0.5) * (0.1 * math.log(128.0) + 1.0) ** 2


def yarn_tables():
    dim, base, factor, orig_max = ROT, 10000.0, 128.0, 1024

    def corr_dim(r):
        return dim * math.log(orig_max / (r * 2 * math.pi)) / (2 * math.log(base))
    low = max(math.floor(corr_dim(32.0)), 0)
    high = min(math.ceil(corr_dim(1.0)), dim - 1)
    hi = high + 0.001 if low == high else float(high)
    ramp = np.clip((np.arange(dim // 2, dtype=np.float32) - low) / (hi - low), 0.0, 1.0)
    keep = 1.0 - ramp
    extra = 1.0 / base ** (np.arange(0, dim, 2, dtype=np.float32) / dim)
    inv = extra / factor * (1.0 - keep) + extra * keep
    f = np.outer(np.arange(C, dtype=np.float32), inv)
    return np.cos(f).astype(np.float32), np.sin(f).astype(np.float32)


def rope1_rows():
    cos, sin = yarn_tables()
    return np.tile(np.concatenate([cos, sin], 1), (R, 1)).astype(np.float32)


def rope1_cols():
    cos, sin = (x.T for x in yarn_tables())
    c = np.concatenate([cos, cos, np.ones((2 * LAT, C), np.float32)])
    z = np.concatenate([-sin, sin, np.zeros((2 * LAT, C), np.float32)])
    return np.stack([c, z], 1).astype(np.float32)


class Chain:

    def __init__(self, eng, sem):
        self.eng, self.sem, self.n = eng, sem, 0

    def mark(self, ins):
        self.n = self.n + 1
        ins.then_inc(self.sem, 1)

    def wait(self):
        self.eng.wait_ge(self.sem, self.n)

    def link(self, ins):
        self.mark(ins)
        self.wait()


def build(nc, a, out):
    ctx = ExitStack()
    with ctx:
        place = {}

        def sb(name, shape):
            at = place[name] = -(-nc.sbuf_base // 32) * 32
            t = ctx.enter_context(nc.sbuf_tensor(name, shape, F32))
            assert nc.sbuf_base == at + 4 * int(np.prod(shape[1:]))
            return t

        def rounded(name, shape, where, skip=0):
            return nc.alloc_sbuf_tensor_at(name, shape, F32R, offset=place[where] + 4 * skip)

        def sem(name):
            return ctx.enter_context(nc.semaphore(name))

        ps = ctx.enter_context(nc.psum_tensor("ps", [P, 8, 512], F32))
        stream = sb("stream", [P, B, T])
        xt = sb("xt", [P, R, TOK])
        wblk = sb("wblk", [P, NET, NBLKS, C])
        ident = sb("ident", [P, P])
        in_scale = sb("in_scale", [P, NET, LAYER, B])
        mid_scale = sb("mid_scale", [P, NET, LAYER, B])
        mid_bias = sb("mid_bias", [P, NET, LAYER, B])
        edge = sb("edge", [P, NET, B])
        cbias = sb("cbias", [P, NET, LAYER])
        NACT = 2 * G * (T + 2)
        acts = sb("acts", [P, 6 * NACT])
        act0, act1 = (acts[:, n * NACT:(n + 1) * NACT].rearrange("p (a g t) -> p a g t", a=2, g=G) for n in range(2))
        act2, act3 = (acts[:, n * NACT:(n + 2) * NACT].rearrange("p (a h g t) -> p a h g t", a=2, h=2, g=G)
                      for n in (2, 4))
        fresh = sb("fresh", [P, B, R, C])
        WPART = 7 * HD
        w_l0 = sb("w_l0", [P, 2 * R * WPART + GQ * R * P])
        w_hi = rounded("w_hi", [P, R, WPART], "w_l0")
        w_lo = rounded("w_lo", [P, R, WPART], "w_l0", R * WPART)
        wo_lo = rounded("wo_lo", [P, GQ, R, P], "w_l0", 2 * R * WPART)
        wo_hi = rounded("wo_hi", [P, GQ, R, P], "acts", R * WPART)
        xt_hi = rounded("xt_hi", [P, R, TOK], "xt")
        xt_lo = rounded("xt_lo", [P, NGROUP, R, P], "stream")
        rope0 = sb("rope0", [P, 2, C])
        causal = sb("causal", [P, C])
        eps = sb("eps", [P, 1])

        ARENA = 18496
        arena = sb("arena", [P, ARENA])

        class Region:
            def __init__(self):
                self.at = 0

            def take(self, *shape, parts=P):
                n = int(np.prod(shape))
                v = arena[0:parts, self.at:self.at + n]
                self.at += n
                assert self.at <= ARENA, self.at
                if len(shape) == 1:
                    return v
                names = "abcd"[:len(shape)]
                return v.rearrange(f"p ({' '.join(names)}) -> p {' '.join(names)}", **dict(zip(names, shape)))

        NSPARE = 12 * R * HD
        spare = w_l0[:, 0:NSPARE]

        class Spare(Region):
            def take(self, *shape):
                n = int(np.prod(shape))
                v = spare[:, self.at:self.at + n]
                self.at += n
                assert self.at <= NSPARE, self.at
                names = "abcd"[:len(shape)]
                return v.rearrange(f"p ({' '.join(names)}) -> p {' '.join(names)}", **dict(zip(names, shape)))

        sp0 = Spare()
        f1_in = sp0.take(R, NAT1)
        f1_out = sp0.take(R, P)
        f1_bias = sp0.take(1, R)
        sp1 = Spare()
        sp1.at = sp0.at
        f0_in = sp1.take(R, NAT0)
        f0_main = sp1.take(R, R, P)
        f0_out = sp1.take(R, P)
        f0_rows = sp1.take(1, 3 * NGATE + NE * NGATE + NE)
        sp2 = Spare()
        sp2.at = sp0.at
        late = sp2.take(4, TOK)
        sp3 = Spare()
        sp3.at = sp0.at
        nat1 = sp3.take(NTILE, QA + QK1)
        keys_n = sp3.take(NTILE, QK1)
        tmp_k = sp3.take(2, NTILE, QA)
        f1_main = w_l0[:, NSPARE:NSPARE + R * R * P].rearrange("p (a r t) -> p a r t", a=R, r=R)
        rank_const = sb("rank_const", [P, NE])
        ones = sb("ones", [P, P])
        rms_eps = sb("rms_eps", [P, 2])

        conv = Region()
        act4 = conv.take(2, G, T)
        setup = Region()
        setup.at = 2048
        wrep = setup.take(NET * LAYER, TAPS, C)
        factor = setup.take(TAPS, NBLKS)
        tmpw = setup.take(2, 12 * C)
        modw = setup.take(NET * LAYER, C, parts=STYLE)
        style = setup.take(P, parts=STYLE)
        modb = setup.take(NET * LAYER)
        wsq = setup.take(NET, TAPS, C)
        wsum = setup.take(NET, C)
        wsum4 = setup.take(NET, P)
        sval = setup.take(NET * LAYER, B)
        ssq = setup.take(NET, LAYER, B)
        dval = setup.take(NET * LAYER, B)
        warm = setup.take(1)
        att0 = Region()
        rot = att0.take(2, 2, HALF)
        qk = att0.take(1 + GQ, TOK)
        vals = att0.take(2, NTILE, HD)
        probs = att0.take(2, 16, C)
        probs_t = att0.take(NTILE, GQ, G, C)
        h_hi = rounded("h_hi", [P, GQ, HALF], "arena", att0.at)
        h_lo = rounded("h_lo", [P, GQ, HALF], "arena", att0.at + GQ * HALF)
        assert setup.at <= att0.at
        stage0 = att0.take(R, WPART)
        att0.take(2 * GQ * HALF - R * WPART)
        stat = att0.take(2, 2, 16)
        ffn = Region()
        ffn.at = 2048
        nat = ffn.take(NTILE, NAT0)
        gate_a = ffn.take(NTILE, NGATE)
        gate_b = ffn.take(NTILE, NGATE)
        gate_p = ffn.take(NTILE, NE, NGATE)
        vote = ffn.take(8, NTILE, NE)
        both = ffn.take(NTILE, 2, NE)
        col = ffn.take(8, NTILE)
        count = ffn.take(2, 2 * NE)
        lora_t = ffn.take(TOK)
        att1 = Region()
        rot1 = att1.take(2, 2, HALF)
        a1_in = att1.take(R, QA + QK1)
        wq1 = att1.take(NH, QK1)
        wcomb = att1.take(8, R, P)
        qa_t = att1.take(TOK)
        keys_t = att1.take(TOK)
        a1_ln = att1.take(1, 1 + LAT)
        rope1r = att1.take(2, LAT)
        rope1c = att1.take(2, C)
        stat1 = att1.take(2, 2, 16)
        rms = att1.take(4, NTILE)
        probs1 = att1.take(2, 16, C)
        values1 = att1.take(NTILE, LAT)
        q1 = [att1.take(GQ, TOK),
              acts[:, 2 * NACT:2 * NACT + GQ * TOK].rearrange("p (g n) -> p g n", g=GQ)]
        stage1 = acts[:, 0:R * WPART]
        assert R * WPART + GQ * R * P <= 6 * NACT
        flat = acts[:, 0:2 * 16 * C].rearrange("p (t n q) -> p t n q", t=2, n=16)
        spot = acts[:, 2 * 16 * C:2 * 16 * C + 2 * HALF].rearrange("p (n t) -> p n t", n=2)
        assert 2 * 16 * C + 2 * HALF <= 2 * NACT
        rot_ring = [rot1[:, 0], rot1[:, 1], spot]
        att1b = Region()
        att1b.at = att1.at - GQ * TOK
        wo1 = [att1b.take(GQ, R * P), att1b.take(GQ, R * P),
               rot1.rearrange("p a n t -> p (a n t)").rearrange("p (g n) -> p g n", g=GQ)]
        probs1_t = fresh[:, :, :, :].rearrange("p b r c -> p (b r c)").rearrange(
            "p (a g j q) -> p a g j q", a=NTILE, g=GQ, j=G)
        made = fresh[:, :, :, :].rearrange("p b r c -> p (b r c)")
        w_nope = made[:, 0:2048].rearrange("p (a b) -> p a b", a=16)
        w_kb = made[:, 2048:3072].rearrange("p (a b) -> p a b", a=16)
        w_v = made[:, 3072:4096].rearrange("p (a b) -> p a b", a=NH)

        WIDE = [[0, 1], [2, 3]]
        NARROW = [4, 5]
        TURN = [6, 7]

        s_mod = sem("modulation_loaded")
        s_taps = sem("taps_loaded")
        s_setup = sem("setup_loaded")
        s_stream = [sem(f"stream_pair{i}_loaded") for i in range(NGROUP // 2)]
        s_const = sem("constants_made")
        s_style = sem("style_product_done")
        s_wsq = sem("squared_taps_ready")
        s_sq = sem("squared_scales_ready")
        s_demod = sem("demod_sums_done")
        s_sqrt = sem("demod_roots_ready")
        s_scales = sem("scales_ready")
        s_blk0 = [sem(f"net0_layer{n}_blocks_ready") for n in range(LAYER)]
        s_wblk = [sem(f"net{n}_conv_blocks_ready") for n in range(1, NET)]
        dve_steps = sem("dve_steps")
        pool_steps = sem("pool_steps")
        s_in = sem("conv_input_ready")
        s_conv = [sem(f"conv_layer{k}_done") for k in range(LAYER)]
        s_eva = [sem(f"conv_layer{k}_act_part") for k in range(LAYER)]
        s_evd = [sem(f"conv_layer{k}_dve_part") for k in range(LAYER)]
        s_turn = sem("conv_output_turned")
        s_xt = [sem(f"tokens_ready{p}") for p in range(2)]
        s_out = sem("outputs_written")
        s_const_loaded = sem("tables_loaded")
        s_zero = sem("zeros_made")
        s_xhi = sem("l0_tokens_rounded")
        s_wst = sem("l0_weights_loaded")
        s_whi = sem("l0_weights_rounded")
        s_wlo = sem("l0_weights_split")
        s_again = sem("stream_loaded_again")
        s_qkv = sem("l0_kq_tile_done")
        s_vt = sem("l0_value_tile_done")
        s_rot = sem("l0_rotary_products_done")
        s_rope = sem("l0_rotary_sum_done")
        s_v = sem("l0_values_copied")
        s_score = sem("l0_scores_done")
        s_pull = sem("scores_turned")
        s_masked = sem("scores_masked")
        s_max = sem("row_maxima_ready")
        s_shift = sem("scores_shifted")
        s_exp = sem("exponentials_ready")
        s_recip = sem("row_sums_inverted")
        s_prob = sem("probabilities_ready")
        s_pt = sem("probabilities_turned")
        s_pv = sem("l0_pv_done")
        s_hhi = sem("l0_heads_rounded")
        s_head = sem("l0_heads_split")
        s_proj = sem("l0_projection_done")
        s_fresh = sem("l0_fresh_added")
        s_fw = [sem(f"ffn{n}_weights_loaded") for n in range(2)]
        s_nat = [sem(f"ffn{n}_token_products_done") for n in range(2)]
        s_natc = [sem(f"ffn{n}_token_products_copied") for n in range(2)]
        s_gact = [sem(f"ffn{n}_gate_scalar_steps") for n in range(2)]
        s_gate = [sem(f"ffn{n}_gate_waiting_for_scalar") for n in range(2)]
        s_both = sem("choices_ready")
        s_count = sem("choices_counted")
        s_lora = [sem(f"ffn{n}_lora_weighted") for n in range(2)]
        s_lturn = [sem(f"ffn{n}_lora_turned") for n in range(2)]
        s_lcopy = [sem(f"ffn{n}_lora_copied") for n in range(2)]
        s_ffn = [sem(f"ffn{n}_output_tile_done") for n in range(2)]
        s_fact = [sem(f"ffn{n}_act_copied") for n in range(2)]
        s_fdve = [sem(f"ffn{n}_dve_copied") for n in range(2)]
        s1_w = sem("l1_arena_weights_loaded")
        s1_wm = sem("l1_factor_weights_loaded")
        s1_wo = [sem(f"l1_wo{p}_loaded") for p in range(3)]
        s1_nat = sem("l1_projection_bank_done")
        s1_natc = sem("l1_projection_copied")
        s1_sq = sem("l1_square_sums_ready")
        s1_root = sem("l1_roots_ready")
        s1_qn = sem("l1_queries_normalised")
        s1_kn = sem("l1_keys_ready")
        s1_turn = sem("l1_turned")
        s1_turnc = sem("l1_turned_copied")
        s1_wq = sem("l1_absorbed_query_done")
        s1_wqc = sem("l1_absorbed_query_copied")
        s1_wc = sem("l1_absorbed_output_done")
        s1_wcc = sem("l1_absorbed_output_copied")
        s1_zero = sem("l1_zeros_made")
        s1_q = sem("l1_query_tile_done")
        s1_shift = sem("l1_scores_shifted_by_dve")
        s1_swap = sem("l1_halves_swapped")
        s1_rot = sem("l1_rotary_products_done")
        s1_rope = sem("l1_rotary_sum_done")
        s1_pv = sem("l1_pv_done")
        s1_head = sem("l1_heads_copied")
        s1_flat = sem("l1_probabilities_flat")
        s1_place = sem("l1_probabilities_placed")
        s1_out = sem("l1_output_tile_done")
        s1_oact = sem("l1_act_copied")
        s1_odve = sem("l1_dve_copied")
        s_back = [sem(f"stage{n}_turned_back") for n in range(4)]
        s_added = [sem(f"stage{n}_stream_updated") for n in range(4)]

        SOFT0 = 2 * NKV

        def done(net, per):
            return net * per
        block = ctx.enter_context(nc.Block())

        def tokens_of(g):
            return xt[:, :, g * P:(g + 1) * P].rearrange("t r (b c) -> t b r c", b=G)

        def tokens_hi(g):
            return xt_hi[:, :, g * P:(g + 1) * P].rearrange("t r (b c) -> t b r c", b=G)

        def tokens_lo(g):
            return xt_lo[:, g, :, :].rearrange("t r (b c) -> t b r c", b=G)

        def turned(p):
            return ps[:, TURN[p], :].rearrange("t (b r c) -> t b r c", b=G, r=R)

        def part(i):
            return 2 * i - 1 if i else 0

        def part_o(i):
            return min(2 * i + 2, 2 * NKV - 1)

        def wcols(i):
            return WPART if i % 2 == 0 else 5 * HD

        def latent(i):
            return xt[:, i, :] if i < R else late[:, i - R, :]

        def conv_blocks(eng, ch, tmp, net, layers, ready):
            for layer in layers:
                n, b = NBLK[layer], BLK0[layer]
                acc = wblk[:, net, b:b + n, :]
                t = tmp[:, 0:n * C].rearrange("p (n c) -> p n c", c=C)
                for k in range(TAPS):
                    w = wrep[:, net * LAYER + layer, k, :].unsqueeze(1).broadcast_to([P, n, C])
                    f = factor[:, k, b:b + n].unsqueeze(2).broadcast_to([P, n, C])
                    ch.link(eng.tensor_tensor(acc if k == 0 else t, w, f, ALU.mult))
                    if k:
                        last = eng.tensor_tensor(acc, acc, t, ALU.add)
                        if k < TAPS - 1:
                            ch.link(last)
                if layer != layers[-1]:
                    ch.link(last)
            last.then_inc(ready, 1)

        @block.sync
        def _(sp):
            sp.dma_start(style, a["style"]).then_inc(s_mod, 16)
            sp.dma_start(modw[:, :, :], a["modw"]).then_inc(s_mod, 16)
            sp.dma_start(wsq, a["wsq"]).then_inc(s_taps, 16)
            sp.dma_start(modb[:, :], a["modb"]).then_inc(s_mod, 16)
            sp.dma_start(cbias[:, :, :], a["cbias"]).then_inc(s_setup, 16)
            sp.dma_start(factor[:, :, :], a["factor"]).then_inc(s_setup, 16)
            sp.dma_start(ident[:, :], a["ident"]).then_inc(s_setup, 16)
            for r in range(R):
                sp.dma_start(wrep[r * C:(r + 1) * C, :, :, :], a["wrep"]).then_inc(s_setup, 16)
            for i in range(NGROUP // 2):
                pair = slice(2 * i * G, 2 * (i + 1) * G)
                sp.dma_start(stream[:, pair, :], a["x"][:, pair, :]).then_inc(s_stream[i], 16)
            sp.dma_start(rope0[:, :, :], a["rope0"]).then_inc(s_const_loaded, 16)
            sp.dma_start(causal[:, :], a["causal"]).then_inc(s_const_loaded, 16)
            sp.dma_start(rank_const[:, :], a["rank"]).then_inc(s_const_loaded, 16)
            sp.dma_start(stage0, a["w_qkv"][0]).then_inc(s_wst, 16)

            def load_qkv(i):
                sp.wait_ge(s_wlo, R * part(i))
                n = wcols(i)
                sp.dma_start(stage1.rearrange("p (r n) -> p r n", r=R)[:, :, 0:n],
                             a["w_qkv"][i][:, :, 0:n]).then_inc(s_wst, 16)

            for p in range(2):
                sp.wait_ge(s_xt[p], done(0, 4) + NGROUP // 2)
            load_qkv(1)
            for i in range(NKV):
                sp.wait_ge(s_wlo, R * part_o(i))
                sp.dma_start(stage1[:, 0:GQ * R * P], a["w_o"][i].rearrange("d g r t -> d (g r t)"))\
                    .then_inc(s_wst, 16)
                if i + 2 < NKV:
                    load_qkv(i + 2)
            sp.wait_ge(s_qkv, 10 * NKV)
            sp.wait_ge(s_vt, 2 * NKV)
            sp.dma_start(stream[:, :, :], a["x"]).then_inc(s_again, 16)
            sp.dma_start(f0_in, a["f0_in"]).then_inc(s_fw[0], 16)
            sp.dma_start(f0_main, a["f0_main"]).then_inc(s_fw[0], 16)
            sp.dma_start(f0_out, a["f0_out"]).then_inc(s_fw[0], 16)
            sp.dma_start(f0_rows[:, 0, :], a["f0_rows"]).then_inc(s_fw[0], 16)
            sp.dma_start(f1_in, a["f1_in"]).then_inc(s_fw[1], 16)
            sp.dma_start(f1_out, a["f1_out"]).then_inc(s_fw[1], 16)
            sp.dma_start(f1_bias[:, 0, :], a["f1_bias"]).then_inc(s_fw[1], 16)
            sp.wait_ge(s_proj, 8 * NKV)
            sp.dma_start(f1_main, a["f1_main"]).then_inc(s_fw[1], 16)
            sp.wait_ge(s_fact[0], 4)
            sp.wait_ge(s_fdve[0], 4)
            sp.dma_start(a1_in, a["a1_in"]).then_inc(s1_w, 16)
            sp.dma_start(wq1[:, :, 0:ROT], a["a1_pe"]).then_inc(s1_w, 16)
            sp.dma_start(a1_ln[:, 0, :], a["a1_ln"]).then_inc(s1_w, 16)
            sp.dma_start(rope1r, a["rope1r"]).then_inc(s1_w, 16)
            sp.dma_start(rope1c, a["rope1c"]).then_inc(s1_w, 16)
            for i in range(2):
                sp.dma_start(wo1[i], a["a1_wo"][i]).then_inc(s1_wo[i], 16)
            sp.wait_ge(s_back[1], NGROUP)
            sp.dma_start(w_nope, a["a1_nope"]).then_inc(s1_wm, 16)
            sp.dma_start(w_kb, a["a1_kb"]).then_inc(s1_wm, 16)
            sp.dma_start(w_v, a["a1_v"]).then_inc(s1_wm, 16)
            for i in range(2, 8):
                if i == 2:
                    for p in range(2):
                        sp.wait_ge(s_xt[p], done(2, 4) + NGROUP // 2)
                else:
                    sp.wait_ge(s1_wc, i - 2)
                sp.dma_start(wo1[i % 3], a["a1_wo"][i]).then_inc(s1_wo[i % 3], 16)
            for i in range(NGROUP // 2):
                pair = slice(2 * i * G, 2 * (i + 1) * G)
                sp.wait_ge(s_added[3], 2 * i + 2)
                sp.dma_start(out[:, pair, :], stream[:, pair, :]).then_inc(s_out, 16)
            sp.wait_ge(s_out, 16 * (NGROUP // 2))

        N_SETUP = 16 * 7

        @block.tensor
        def _(pe):
            pe.wait_ge(s_mod, 48)
            pe.matmul(ps[:, 0, :], style, modw.rearrange("p n c -> p (n c)"), start=True, stop=True)\
                .then_inc(s_style, 1)
            pe.wait_ge(s_sq, 1)
            for net in range(NET):
                last = pe.matmul(ps[:, 1, net * P:(net + 1) * P], wsum4[:, net, :],
                                 ssq[:, net, :, :].rearrange("p l b -> p (l b)"), start=True, stop=True)
            last.then_inc(s_demod, 1)
            pe.wait_ge(s_setup, N_SETUP)

            def blk(net, layer, first, count=4):
                b = BLK0[layer] + first
                return wblk[:, net, b:b + count, :].rearrange("p n c -> p (n c)")

            def conv_stack(net, between):
                if net == 0:
                    pe.wait_ge(s_sqrt, 1)
                else:
                    pe.wait_ge(s_wblk[net - 1], 1)

                def first_blocks(layer, i, p):
                    if net == 0 and i == 0 and p == 0:
                        pe.wait_ge(s_blk0[layer], 1)

                if net in (1, 3):
                    pe.wait_ge(s_const, 3 + net // 2)
                def first(i, p):
                    g = 2 * i + p
                    o = ps[:, NARROW[p], :]
                    first_blocks(0, i, p)
                    pe.wait_ge(s_in, done(net, 8) + g + 1)
                    x = act0[:, p]
                    pe.matmul(o, blk(net, 0, 0), x[:, :, 1:T + 1], start=True, stop=True)
                    pe.matmul(o[0:32], blk(net, 0, 4, 1), x[:, :, 0:T], **ADD)
                    pe.matmul(o[96:128], blk(net, 0, 5, 1), x[:, :, 2:T + 2], **ADD).then_inc(s_conv[0], 1)

                first(0, 0)
                first(0, 1)
                for i in range(NGROUP // 2):
                    for p in range(2):
                        first_blocks(1, i, p)
                        pe.wait_ge((s_eva, s_evd)[p][0], done(net, 4) + i + 1)
                        oa, ob = ps[:, WIDE[p][0], :], ps[:, WIDE[p][1], :]
                        x = act1[:, p]
                        pe.matmul(oa, blk(net, 1, 0), x[:, :, 1:T + 1], start=True, stop=True)
                        pe.matmul(ob, blk(net, 1, 4), x[:, :, 1:T + 1], start=True, stop=True)
                        pe.matmul(oa[0:64], blk(net, 1, 8, 2), x[:, :, 0:T], **ADD)\
                            .then_inc(s_conv[1], 1)
                        pe.matmul(ob[64:128], blk(net, 1, 10, 2), x[:, :, 2:T + 2], **ADD)\
                            .then_inc(s_conv[1], 1)
                    for p in range(2):
                        g = 2 * i + p
                        first_blocks(2, i, p)
                        pe.wait_ge(s_evd[1], done(net, 8) + g + 1)
                        oa, ob = ps[:, WIDE[p][0], :], ps[:, WIDE[p][1], :]
                        xa, xb = act2[:, p, 0], act2[:, p, 1]
                        pe.matmul(oa, blk(net, 2, 0), xa[:, :, 1:T + 1], start=True, stop=True)
                        pe.matmul(ob, blk(net, 2, 4), xb[:, :, 1:T + 1], start=True, stop=True)
                        pe.matmul(oa[0:32], blk(net, 2, 8, 1), xb[:, :, 0:T], **ADD)
                        pe.matmul(oa[32:64], blk(net, 2, 9, 1), xb[:, :, 1:T + 1], **ADD)
                        pe.matmul(ob[64:96], blk(net, 2, 8, 1), xa[:, :, 1:T + 1], **ADD)
                        pe.matmul(ob[96:128], blk(net, 2, 9, 1), xa[:, :, 2:T + 2], **ADD)\
                            .then_inc(s_conv[2], 2)
                    for p in range(2):
                        g = 2 * i + p
                        first_blocks(3, i, p)
                        pe.wait_ge(s_eva[2], done(net, 8) + g + 1)
                        pe.wait_ge(s_evd[2], done(net, 8) + g + 1)
                        o = ps[:, NARROW[p], :]
                        xa, xb = act3[:, p, 0], act3[:, p, 1]
                        pe.matmul(o, blk(net, 3, 0), xa[:, :, 1:T + 1], start=True, stop=True)
                        pe.matmul(o, blk(net, 3, 4), xb[:, :, 1:T + 1], **ADD)
                        pe.matmul(o[0:32], blk(net, 3, 8, 1), xb[:, :, 0:T], **ADD)
                        pe.matmul(o[96:128], blk(net, 3, 9, 1), xa[:, :, 2:T + 2], **ADD)\
                            .then_inc(s_conv[3], 1)
                    for p in range(2):
                        g = 2 * i + p
                        if g == NGROUP - 1:
                            between()
                        pe.wait_ge((s_eva, s_evd)[p][3], done(net, 4) + i + 1)
                        if i:
                            pe.wait_ge(s_xt[p], done(net, 4) + i)
                        for j in range(G):
                            last = pe.transpose(ps[:, TURN[p], j * P:(j + 1) * P], act4[:, p, j, :], ident[:, :])
                        last.then_inc(s_turn, 1)
                        if g + 2 < NGROUP:
                            first(i + 1, p)

            def attention0():
                def keys_queries(i, tiles):
                    for k in tiles:
                        if k < 3 and i >= 2:
                            pe.wait_ge(s_fresh, 8 * (i - 2) + (7, 8, 8)[k])
                        if k < 3 and i == 1:
                            pe.wait_ge(s_v, (4, 4, 4)[k])
                        if k >= 3:
                            pe.wait_ge(s_rot, 10 * i + k - 2)
                        chunk, half = k % (1 + GQ), k // (1 + GQ)
                        cols = slice(chunk * HD, (chunk + 1) * HD)
                        for r in range(R):
                            if k == 0:
                                pe.wait_ge(s_wlo, R * part(i) + r + 1)
                            x_hi = xt_hi[:, r, half * HALF:(half + 1) * HALF]
                            x_lo = xt_lo[:, half * G:(half + 1) * G, r, :]
                            for n, (w, x) in enumerate(((w_hi, x_hi), (w_hi, x_lo), (w_lo, x_hi))):
                                last = pe.matmul(ps[:, k % 3, :], w[:, r, cols], x,
                                                 start=(r == 0 and n == 0), stop=(r == R - 1 and n == 2))
                        last.then_inc(s_qkv, 1)

                def values(i):
                    for v in range(4):
                        if v < 3 and i:
                            pe.wait_ge(s_fresh, 8 * (i - 1) + 2 + v)
                        if v < 3 and i == 0:
                            pe.wait_ge(s_rot, (9, 10, 8)[v])
                        if v == 3:
                            pe.wait_ge(s_v, 2 * i + 1)
                        for m in range(2):
                            tile = 2 * v + m
                            for r in range(R):
                                x_hi = xt_hi[:, r, tile * P:(tile + 1) * P]
                                x_lo = xt_lo[:, tile, r, :]
                                for n, (x, w) in enumerate(((x_hi, w_hi), (x_hi, w_lo), (x_lo, w_hi))):
                                    last = pe.matmul(ps[:, (2, 0, 1, 2)[v], m * 2 * HD:(m + 1) * 2 * HD], x,
                                                     w[:, r, 5 * HD:7 * HD],
                                                     start=(r == 0 and n == 0), stop=(r == R - 1 and n == 2))
                        last.then_inc(s_vt, 1)

                def scores(i, t):
                    pe.wait_ge(s_rope, 10 * (i + 1))
                    if i:
                        pe.wait_ge(s_pull, 2 * (i - 1) + t + 1)
                    for m in range(4):
                        for j in range(G):
                            b = (4 * t + m) * G + j
                            last = pe.matmul(ps[32 * j:32 * j + 32, 3 + t, m * P:(m + 1) * P],
                                             qk[:, 0, b * C:(b + 1) * C], qk[:, 1:1 + GQ, b * C:(b + 1) * C],
                                             start=True, stop=True)
                    last.then_inc(s_score, 1)

                def pv(i, tiles):
                    pe.wait_ge(s_v, 4 * (i // 2) + 4)
                    for q in tiles:
                        if q % 4 == 0:
                            pe.wait_ge(s_pt, 2 * i + q // 4 + 1)
                        if i or q >= 2:
                            pe.wait_ge(s_head, 8 * i + q - 1)
                        pe.matmul(ps[:, 5 + q % 2, :], vals[:, i % 2, q, :],
                                  probs_t[:, q, :, :, :].rearrange("k g j q -> k (g j q)"),
                                  start=True, stop=True).then_inc(s_pv, 1)

                def project(i, half):
                    pe.wait_ge(s_wlo, R * (part_o(i) + 1))
                    pe.wait_ge(s_head, 8 * i + 4 * half + 4)
                    for r in range(R):
                        n = 4 * half + r
                        if i or half:
                            pe.wait_ge(s_fresh, 8 * i + n - 3)
                        if half == 0 and r and i + 1 < NKV:
                            pe.wait_ge(s_rot, 10 * (i + 1) + (9, 10, 8)[r - 1])
                        if half and r and i % 2 and i + 1 < NKV:
                            pe.wait_ge(s_v, 2 * (i + 1) + (4, 2, 3)[r - 1])
                        for g in range(GQ):
                            for m, (w, x) in enumerate(((wo_hi, h_hi), (wo_hi, h_lo), (wo_lo, h_hi))):
                                last = pe.matmul(ps[:, (7, 2, 0, 1)[r], :], w[:, g, r, :], x[:, g, :],
                                                 start=(g == 0 and m == 0), stop=(g == GQ - 1 and m == 2))
                        last.then_inc(s_proj, 1)

                def first_keys():
                    for p in range(2):
                        pe.wait_ge(s_xt[p], NGROUP // 4)
                    keys_queries(0, range(2))

                conv_stack(0, first_keys)
                keys_queries(0, range(2, 1 + GQ))
                for p in range(2):
                    pe.wait_ge(s_xt[p], NGROUP // 2)
                keys_queries(0, range(1 + GQ, 2 * (1 + GQ)))
                values(0)
                scores(0, 0)
                scores(0, 1)
                for i in range(NKV):
                    if i + 1 < NKV:
                        keys_queries(i + 1, range(8))
                    pv(i, range(2))
                    if i + 1 < NKV:
                        keys_queries(i + 1, range(8, 9))
                    pv(i, range(2, 4))
                    if i + 1 < NKV:
                        keys_queries(i + 1, range(9, 10))
                    project(i, 0)
                    pv(i, range(4, 6))
                    if i + 1 < NKV:
                        scores(i + 1, 0)
                    pv(i, range(6, 8))
                    if i + 1 < NKV:
                        scores(i + 1, 1)
                    if i % 2 and i + 1 < NKV:
                        values(i + 1)
                    project(i, 1)

            def ffn(n):
                w_in, width, lora_at = ((f0_in, NAT0, NGATE), (f1_in, NAT1, NE))[n]
                w_main, w_out = ((f0_main, f0_out), (f1_main, f1_out))[n]
                net = 2 * n + 1

                def token_products(m):
                    if m == 0:
                        pe.wait_ge(s_fw[n], 64)
                    pe.wait_ge(s_xt[m % 2], done(net, 4) + m // 2 + 1)
                    o = ps[:, m // 2, (m % 2) * 256:(m % 2) * 256 + width]
                    for r in range(R):
                        last = pe.matmul(o, xt[:, r, m * P:(m + 1) * P], w_in[:, r, :],
                                         start=(r == 0), stop=(r == R - 1))
                    if m % 2:
                        last.then_inc(s_nat[n], 1)

                conv_stack(net, lambda: token_products(0))
                for m in range(1, NTILE):
                    token_products(m)

                def main(k):
                    half, r_out = k // 4, k % 4
                    for r in range(R):
                        pe.matmul(ps[:, FFN_BANK[k], :], w_main[:, r, r_out, :],
                                  xt[:, r, half * HALF:(half + 1) * HALF], start=(r == 0), stop=False)

                def lora(k):
                    half, r_out = k // 4, k % 4
                    pe.matmul(ps[:, FFN_BANK[k], :], w_out[:, r_out, :], lora_t[:, half * HALF:(half + 1) * HALF],
                              start=False, stop=True).then_inc(s_ffn[n], 1)

                for k in range(6):
                    if k >= 4:
                        pe.wait_ge(s_natc[n], k - 3)
                    main(k)
                pe.wait_ge(s_natc[n], 4)
                if n == 0:
                    pe.wait_ge(s_both, 1)
                    pe.matmul(ps[:, 2, 0:P], ones[:, :], both.rearrange("p m k e -> p (m k e)"),
                              start=True, stop=True).then_inc(s_count, 1)
                pe.wait_ge(s_lora[n], 1)
                for m in range(NTILE):
                    last = pe.transpose(ps[:, 2 + m // 4, (m % 4) * P:(m % 4 + 1) * P],
                                        nat[:, m, lora_at:lora_at + P], ident[:, :])
                    if m % 4 == 3:
                        last.then_inc(s_lturn[n], 1)
                pe.wait_ge(s_lcopy[n], 2)
                for k in range(6):
                    lora(k)
                for k in range(6, 8):
                    main(k)
                    lora(k)

            def attention1():
                def project(m):
                    if m == 0:
                        pe.wait_ge(s1_w, 80)
                    pe.wait_ge(s_xt[m % 2], done(2, 4) + m // 2 + 1)
                    o = ps[:, m // 2, (m % 2) * 256:(m % 2) * 256 + QA + QK1]
                    for r in range(R):
                        last = pe.matmul(o, xt[:, r, m * P:(m + 1) * P], a1_in[:, r, :],
                                         start=(r == 0), stop=(r == R - 1))
                    if m % 2:
                        last.then_inc(s1_nat, 1)

                def absorb_keys(m):
                    ins = pe.matmul(ps[:, 4 + m // 8, (m % 8) * 64:(m % 8 + 1) * 64], w_nope[:, m, :], w_kb[:, m, :],
                                    start=True, stop=True)
                    if m % 8 == 7:
                        ins.then_inc(s1_wq, 1)

                def absorb_output(i):
                    pe.wait_ge(s1_wo[i % 3], 16 * (i // 3 + 1))
                    if i >= 2:
                        pe.wait_ge(s1_wcc, i - 1)
                    for g in range(GQ):
                        last = pe.matmul(ps[32 * g:32 * g + 32, 6 + i % 2, :], w_v[:, GQ * i + g, :],
                                         wo1[i % 3][:, g, :], start=True, stop=True)
                    last.then_inc(s1_wc, 1)

                conv_stack(2, lambda: project(0))
                pe.wait_ge(s1_wm, 48)
                for i in range(8):
                    for m in (range(1, 4), range(4, 6), range(6, 8), ())[min(i, 3)]:
                        project(m)
                    if i == 0:
                        for p in range(2):
                            pe.wait_ge(s_xt[p], done(2, 4) + NGROUP // 2)
                    for m in (range(4 * (i - 4), 4 * (i - 3)) if i >= 4 else ()):
                        absorb_keys(m)
                    absorb_output(i)
                pe.wait_ge(s1_natc, 4)
                pe.wait_ge(s1_qn, 1)
                for m in range(NTILE):
                    last = pe.transpose(ps[:, m // 4, (m % 4) * P:(m % 4 + 1) * P], nat1[:, m, 0:QA], ident[:, :])
                    if m % 4 == 3:
                        last.then_inc(s1_turn, 1)
                pe.wait_ge(s1_kn, 1)
                for m in range(NTILE):
                    last = pe.transpose(ps[0:QK1, 2 + m // 4, (m % 4) * P:(m % 4 + 1) * P], keys_n[:, m, :],
                                        ident[:, :])
                    if m % 4 == 3:
                        last.then_inc(s1_turn, 1)

                def queries(i, tiles):
                    for k in tiles:
                        if k >= 4 or i:
                            pe.wait_ge(s1_rot, 8 * i + k - 3)
                        g, half = k // 2, k % 2
                        pe.matmul(ps[0:QK1, (0, 1, 2, 7)[k % 4], :], wq1[:, GQ * i + g, :],
                                  qa_t[:, half * HALF:(half + 1) * HALF], start=True, stop=True).then_inc(s1_q, 1)

                def scores(i):
                    pe.wait_ge(s1_rope, 8 * (i + 1))
                    for t in range(2):
                        if i:
                            pe.wait_ge(s_pull, SOFT0 + 2 * (i - 1) + t + 1)
                        for m in range(4):
                            for j in range(G):
                                b = (4 * t + m) * G + j
                                last = pe.matmul(ps[32 * j:32 * j + 32, 3 + t, m * P:(m + 1) * P],
                                                 keys_t[0:QK1, b * C:(b + 1) * C],
                                                 q1[i % 2][0:QK1, :, b * C:(b + 1) * C], start=True, stop=True)
                        last.then_inc(s_score, 1)

                def pv(i):
                    for half in range(2):
                        pe.wait_ge(s1_place, 2 * i + half + 1)
                        if i:
                            pe.wait_ge(s1_head, 2 * i + half - 1)
                        for m in range(4):
                            q = 4 * half + m
                            for g in range(GQ):
                                last = pe.matmul(ps[32 * g:32 * g + 32, 5 + half, m * P:(m + 1) * P],
                                                 values1[:, q, :], probs1_t[:, q, g, :, :].rearrange("k j q -> k (j q)"),
                                                 start=True, stop=True)
                        last.then_inc(s1_pv, 1)

                pe.wait_ge(s1_turnc, 4)
                pe.wait_ge(s1_wqc, 2)
                pe.wait_ge(s1_wcc, 8)
                queries(0, range(8))
                queries(1, range(4))
                scores(0)
                queries(1, range(4, 8))
                for i in range(8):
                    if i + 2 < 8:
                        queries(i + 2, range(5))
                    if i:
                        pv(i - 1)
                    if i + 2 < 8:
                        queries(i + 2, range(5, 8))
                    if i + 1 < 8:
                        scores(i + 1)
                pv(7)
                pe.wait_ge(s1_head, 16)
                for n in range(8):
                    half, r_out = n // 4, n % 4
                    for i in range(8):
                        last = pe.matmul(ps[:, FFN_BANK[n], :], wcomb[:, i, r_out, :],
                                         latent(i)[:, half * HALF:(half + 1) * HALF], start=(i == 0), stop=(i == 7))
                    last.then_inc(s1_out, 1)

            def turn_back(stage, half_ready, all_ready):
                for g in range(NGROUP):
                    for what, count in {0: half_ready, NGROUP // 2: all_ready}.get(g, ()):
                        pe.wait_ge(what, count)
                    if g >= 2:
                        pe.wait_ge(s_added[stage], g - 1)
                    for j in range(G):
                        last = pe.transpose(ps[:, TURN[g % 2], j * P:(j + 1) * P],
                                            fresh[:, g * G + j, :, :].rearrange("t r c -> t (r c)"), ident[:, :])
                    last.then_inc(s_back[stage], 1)

            attention0()
            turn_back(0, ((s_fresh, 8 * NKV - 3),), ((s_fresh, 8 * NKV),))
            ffn(0)
            turn_back(1, ((s_fact[0], 2), (s_fdve[0], 2)), ((s_fact[0], 4), (s_fdve[0], 4)))
            attention1()
            turn_back(2, ((s1_oact, 2), (s1_odve, 2)), ((s1_oact, 4), (s1_odve, 4)))
            ffn(1)
            turn_back(3, ((s_fact[1], 2), (s_fdve[1], 2)), ((s_fact[1], 4), (s_fdve[1], 4)))

        @block.scalar
        def _(act):
            act.wait_ge(s_taps, 16)
            act.activation(wsq, wsq, ACT.Square).then_inc(s_wsq, 1)
            act.wait_ge(s_const, 2)
            act.activation(warm, eps[:, 0:1], ACT.Sqrt)
            act.wait_ge(s_demod, 1)
            act.activation(dval[:, :, :], ps[:, 1, :].rearrange("p (n b) -> p n b", b=B), ACT.Sqrt,
                           bias=eps[:, 0:1], scale=CONV_SCALE ** 2).then_inc(s_sqrt, 1)

            def conv_stack(net):
                act.wait_ge(s_scales, 1 if net == 0 else 2)
                for i in range(NGROUP // 2):
                    for layer, p in CONV_STEPS:
                        g = 2 * i + p
                        wide = layer in (1, 2)
                        if not wide and p == 1:
                            continue
                        bank = ps[:, WIDE[p][0] if wide else NARROW[p], :]
                        dst = [act1[:, p], act2[:, p, 0], act3[:, p, 0], act4[:, p]][layer]
                        off = 0 if layer == 3 else 1
                        act.wait_ge(s_conv[layer], done(net, 16) + 2 * g + 1 if wide else done(net, 8) + g + 1)
                        for j in range(G):
                            b = g * G + j
                            bias = cbias[:, net, 3:4] if layer == 3 else mid_bias[:, net, layer, b:b + 1]
                            last = act.activation(dst[:, j, off:off + T], bank[:, j * T:(j + 1) * T],
                                                  ACT.Identity, bias=bias, scale=mid_scale[:, net, layer, b:b + 1])
                        last.then_inc(s_eva[layer], 1)
                    g = 2 * i
                    act.wait_ge(s_turn, done(net, 8) + g + 1)
                    if net:
                        act.activation(tokens_of(g), turned(0), ACT.Copy).then_inc(s_xt[0], 1)
                    else:
                        act.activation(tokens_hi(g), turned(0), ACT.Copy).then_inc(s_xhi, 1)
                        for r in ((0, 1), (2, 3), (), ())[i]:
                            act.wait_ge(s_wst, 16)
                            act.activation(w_hi[:, r, :], stage0[:, r, :], ACT.Copy).then_inc(s_whi, 1)

            def attention0():
                def values(i):
                    for v in range(4):
                        act.wait_ge(s_vt, 2 * i + v + 1)
                        if i:
                            act.wait_ge(s_pv, 8 * i)
                        act.activation(vals[:, :, 2 * v:2 * v + 2, :],
                                       ps[:, (2, 0, 1, 2)[v], :].rearrange("p (m h d) -> p h m d", m=2, h=2),
                                       ACT.Copy).then_inc(s_v, 1)

                def round_qkv(i):
                    act.wait_ge(s_wst, 16 * (part(i) + 1))
                    act.wait_ge(s_qkv, 10 * i)
                    act.wait_ge(s_vt, 4 * ((i - 1) // 2) + 4)
                    n = wcols(i)
                    stage = stage1.rearrange("p (r n) -> p r n", r=R)
                    for r in range(R):
                        act.activation(w_hi[:, r, 0:n], stage[:, r, 0:n], ACT.Copy).then_inc(s_whi, 1)

                def round_o(i):
                    act.wait_ge(s_wst, 16 * (part_o(i) + 1))
                    if i:
                        act.wait_ge(s_proj, 8 * i)
                    for g in range(GQ):
                        act.activation(wo_hi[:, g, :, :].rearrange("d r t -> d (r t)"),
                                       stage1[:, g * R * P:(g + 1) * R * P], ACT.Copy).then_inc(s_whi, 1)

                values(0)
                round_qkv(1)
                for i in range(NKV):
                    for t in range(2):
                        act.wait_ge(s_shift, 2 * i + t + 1)
                        x = probs[:, t, :, :].rearrange("p a b -> p (a b)")
                        act.activation(x, x, ACT.Exp, scale=R0_SCALE).then_inc(s_exp, 1)
                    round_o(i)
                    for q in range(NTILE):
                        act.wait_ge(s_pv, 8 * i + q + 1)
                        if q % 4 == 0 and (i or q):
                            act.wait_ge(s_proj, 8 * i + q)
                        act.activation(h_hi[:, :, (q % 4) * P:(q % 4 + 1) * P],
                                       ps[:, 5 + q % 2, :].rearrange("d (g n) -> d g n", g=GQ),
                                       ACT.Copy).then_inc(s_hhi, 1)
                    if i % 2 and i + 1 < NKV:
                        values(i + 1)
                    if i + 2 < NKV:
                        round_qkv(i + 2)

            def ffn(n):
                width = (NAT0, NAT1)[n]
                for q in range(4):
                    act.wait_ge(s_nat[n], q + 1)
                    act.activation(nat[:, 2 * q:2 * q + 2, 0:width],
                                   ps[:, q, :].rearrange("p (a b) -> p a b", a=2)[:, :, 0:width],
                                   ACT.Copy).then_inc(s_natc[n], 1)
                act.wait_ge(s_gate[n], 1)
                if n == 0:
                    act.activation(col[:, 1, :], col[:, 1, :], ACT.Sqrt, bias=rms_eps[:, 1:2],
                                   scale=1.0 / NGATE).then_inc(s_gact[n], 1)
                    act.wait_ge(s_gate[n], 2)
                    act.activation(col[:, 4, :], col[:, 4, :], ACT.Exp).then_inc(s_gact[n], 1)
                else:
                    act.activation(vote[:, 0], vote[:, 0], ACT.Exp).then_inc(s_gact[n], 1)
                for q in range(2):
                    act.wait_ge(s_lturn[n], q + 1)
                    act.activation(lora_t[:, q * HALF:(q + 1) * HALF], ps[:, 2 + q, :], ACT.Copy)\
                        .then_inc(s_lcopy[n], 1)
                for k in range(0, 8, 2):
                    half, r_out = k // 4, k % 4
                    act.wait_ge(s_ffn[n], k + 1)
                    act.activation(fresh[:, half * 16:half * 16 + 16, r_out, :],
                                   ps[:, FFN_BANK[k], :].rearrange("p (b c) -> p b c", c=C),
                                   ACT.Identity, bias=f1_bias[:, 0, r_out:r_out + 1] if n else 0.0)\
                        .then_inc(s_fact[n], 1)

            def attention1():
                def copy_projection(q):
                    act.wait_ge(s1_nat, q + 1)
                    act.activation(nat1[:, 2 * q:2 * q + 2, :],
                                   ps[:, q, :].rearrange("p (a b) -> p a b", a=2)[:, :, 0:QA + QK1],
                                   ACT.Copy).then_inc(s1_natc, 1)

                def copy_query_weights(q):
                    act.wait_ge(s1_wq, q + 1)
                    act.activation(wq1[:, 16 * q:16 * q + 16, ROT:QK1],
                                   ps[:, 4 + q, :].rearrange("p (h l) -> p h l", l=LAT), ACT.Copy).then_inc(s1_wqc, 1)

                def copy_output_weights(i):
                    act.wait_ge(s1_wc, i + 1)
                    act.activation(wcomb[:, i].rearrange("p r t -> p (r t)"), ps[:, 6 + i % 2, :], ACT.Copy)\
                        .then_inc(s1_wcc, 1)

                for i in range(8):
                    for q in ((0, 1), (2,), (3,), ())[min(i, 3)]:
                        copy_projection(q)
                    if i >= 4 and i % 2:
                        copy_query_weights(i // 2 - 2)
                    copy_output_weights(i)
                    if i == 5:
                        act.wait_ge(s1_sq, 1)
                        act.activation(rms[:, 2, :], rms[:, 0, :], ACT.Sqrt, bias=rms_eps[:, 0:1], scale=1.0 / QA)\
                            .then_inc(s1_root, 1)
                        act.activation(rms[:, 3, :], rms[:, 1, :], ACT.Sqrt, bias=rms_eps[:, 0:1], scale=1.0 / LAT)\
                            .then_inc(s1_root, 1)
                for q in range(2):
                    act.wait_ge(s1_turn, q + 1)
                    act.activation(qa_t[:, q * HALF:(q + 1) * HALF], ps[:, q, :], ACT.Copy,
                                   scale=a1_ln[:, 0, 0:1]).then_inc(s1_turnc, 1)
                for q in range(2):
                    act.wait_ge(s1_turn, q + 3)
                    act.activation(keys_t[0:QK1, q * HALF:(q + 1) * HALF], ps[0:QK1, 2 + q, :], ACT.Copy)\
                        .then_inc(s1_turnc, 1)

                def swap(i, k):
                    n = 8 * i + k
                    act.wait_ge(s1_q, n + 1)
                    if n >= 3:
                        act.wait_ge(s1_rope, n - 2)
                    x = ps[:, (0, 1, 2, 7)[k % 4], :]
                    for h in range(2):
                        last = act.activation(rot_ring[n % 3][32 - 32 * h:64 - 32 * h, 1, :], x[32 * h:32 * h + 32],
                                              ACT.Copy)
                    last.then_inc(s1_swap, 1)

                def exponentials(i):
                    for t in range(2):
                        if t == 0:
                            act.wait_ge(s_shift, SOFT0 + i + 1)
                        else:
                            act.wait_ge(s1_shift, i + 1)
                        x = probs1[:, t, :, :].rearrange("p a b -> p (a b)")
                        act.activation(x, x, ACT.Exp, scale=R1_SCALE).then_inc(s_exp, 1)

                def spread(i, t):
                    act.wait_ge(s1_flat, 2 * i + t + 1)
                    if i:
                        act.wait_ge(s1_pv, 2 * (i - 1) + t + 1)
                    for j in range(G):
                        q = slice(32 * j, 32 * j + 32)
                        last = act.activation(probs1_t[q, 4 * t:4 * t + 4, :, j, :].rearrange("p a g q -> p (a g) q"),
                                              flat[q, t, :, :], ACT.Copy)
                    last.then_inc(s1_place, 1)

                def heads_out(i):
                    for half in range(2):
                        act.wait_ge(s1_pv, 2 * i + half + 1)
                        act.activation(latent(i)[:, half * HALF:(half + 1) * HALF], ps[:, 5 + half, :],
                                       ACT.Copy).then_inc(s1_head, 1)

                for k in range(16):
                    swap(k // 8, k % 8)
                for i in range(9):
                    for k in range(8):
                        if i + 2 < 8:
                            swap(i + 2, k)
                        if i and k < 2:
                            spread(i - 1, k)
                        if i < 8 and k == 3:
                            exponentials(i)
                        if i and k == 5:
                            heads_out(i - 1)
                for k in range(0, 8, 2):
                    half, r_out = k // 4, k % 4
                    act.wait_ge(s1_out, k + 1)
                    act.activation(fresh[:, half * 16:half * 16 + 16, r_out, :],
                                   ps[:, FFN_BANK[k], :].rearrange("p (b c) -> p b c", c=C),
                                   ACT.Copy).then_inc(s1_oact, 1)

            conv_stack(0)
            attention0()
            conv_stack(1)
            ffn(0)
            conv_stack(2)
            attention1()
            conv_stack(3)
            ffn(1)

        @block.vector
        def _(dve):
            ch = Chain(dve, dve_steps)
            dve.memset(rms_eps[:, 0:1], RMS_EPS)
            dve.memset(rms_eps[:, 1:2], LN_EPS)
            dve.memset(ones[:, :], 1.0)
            ch.link(dve.memset(ssq, 0.0))
            dve.memset(eps[:, :], CONV_EPS).then_inc(s_const, 1)

            def zero_pads():
                rows_of = acts[:, :].rearrange("p (n t) -> p n t", t=T + 2)
                dve.memset(rows_of[:, :, 0:1], 0.0)
                dve.memset(rows_of[:, :, T + 1:T + 2], 0.0).then_inc(s_const, 1)

            zero_pads()
            dve.wait_ge(s_wsq, 1)
            ch.link(dve.tensor_tensor(wsum, wsq[:, :, 0, :], wsq[:, :, 1, :], ALU.add))
            over_r = [P, NET, R, C]
            dve.tensor_tensor(wsum4.rearrange("i n (r o) -> i n r o", r=R), wsum.unsqueeze(2).broadcast_to(over_r),
                              wsq[:, :, 2, :].unsqueeze(2).broadcast_to(over_r), ALU.add)
            s4 = sval[:, :, :].rearrange("p (n l) b -> p n l b", l=LAYER)
            d4 = dval[:, :, :].rearrange("p (n l) b -> p n l b", l=LAYER)

            dve.wait_ge(s_style, 1)
            ch.link(dve.transpose(sval.rearrange("p n b -> p (n b)"), ps[:, 0, :]))
            ch.link(dve.tensor_tensor(sval, sval, modb.unsqueeze(2).broadcast_to([P, NET * LAYER, B]), ALU.add))
            for layer in range(LAYER):
                rows = slice(C * layer, C * layer + C)
                last = dve.tensor_tensor(ssq[rows, :, layer, :], s4[rows, :, layer, :], s4[rows, :, layer, :], ALU.mult)
            last.then_inc(s_sq, 1)

            def scales(ns):
                many = ns.stop - ns.start
                dve.wait_ge(s_sqrt, 1)
                ch.link(dve.reciprocal(d4[:, ns], d4[:, ns]))
                dve.tensor_copy(in_scale[:, ns, 0, :], s4[:, ns, 0, :])
                dve.tensor_copy(in_scale[:, ns, 1, :], d4[:, ns, 1, :])
                dve.tensor_copy(in_scale[:, ns, 2:4, :], s4[:, ns, 2:4, :])
                ch.link(dve.tensor_scalar(cbias[:, ns, 1], cbias[:, ns, 1], 2.0, None, ALU.mult))
                for k in range(3):
                    src = s4 if k == 1 else d4
                    dve.scalar_tensor_tensor(mid_scale[:, ns, k, :], src[:, ns, k, :], CONV_SCALE,
                                             in_scale[:, ns, k + 1, :], ALU.mult, ALU.mult)
                    ch.mark(dve.tensor_tensor(mid_bias[:, ns, k, :], in_scale[:, ns, k + 1, :],
                                              cbias[:, ns, k].unsqueeze(2).broadcast_to([P, many, B]), ALU.mult))
                dve.tensor_scalar(mid_scale[:, ns, 3, :], d4[:, ns, 3, :], CONV_SCALE, None, ALU.mult)
                ch.wait()
                dve.tensor_scalar(edge[:, ns, :], mid_bias[:, ns, 1, :], -0.125, None, ALU.mult).then_inc(s_scales, 1)

            dve.wait_ge(s_setup, N_SETUP)
            conv_blocks(dve, ch, tmpw[:, 0, :], 0, (0,), s_blk0[0])
            scales(slice(0, 1))
            conv_blocks(dve, ch, tmpw[:, 0, :], 0, (3,), s_blk0[3])
            scales(slice(1, NET))

            def conv_stack(net):
                for i in range(NGROUP // 2):
                    for layer, p in CONV_STEPS:
                        g = 2 * i + p
                        wide = layer in (1, 2)
                        if not wide and p == 0:
                            continue
                        bank = ps[:, WIDE[p][1] if wide else NARROW[p], :]
                        dst = [act1[:, p], act2[:, p, 1], act3[:, p, 1], act4[:, p]][layer]
                        off = 0 if layer == 3 else 1
                        dve.wait_ge(s_conv[layer], done(net, 16) + 2 * g + 2 if wide else done(net, 8) + g + 1)
                        for j in range(G):
                            b = g * G + j
                            bias = cbias[:, net, 3:4] if layer == 3 else mid_bias[:, net, layer, b:b + 1]
                            last = dve.tensor_scalar(dst[:, j, off:off + T], bank[:, j * T:(j + 1) * T],
                                                     mid_scale[:, net, layer, b:b + 1], bias, ALU.mult, ALU.add)
                        if layer == 1:
                            ch.link(last)
                            samples = slice(g * G, (g + 1) * G)
                            end = act2[96:128, p, 1, :, T]
                            dve.tensor_tensor(end, end, edge[96:128, net, samples], ALU.add)
                            dve.wait_ge(s_eva[layer], done(net, 8) + g + 1)
                            end = act2[0:32, p, 0, :, 1]
                            last = dve.tensor_tensor(end, end, edge[0:32, net, samples], ALU.add)
                        last.then_inc(s_evd[layer], 1)
                    g = 2 * i + 1
                    dve.wait_ge(s_turn, done(net, 8) + g + 1)
                    if net:
                        dve.tensor_copy(tokens_of(g), turned(1)).then_inc(s_xt[1], 1)
                        continue
                    ch.link(dve.tensor_copy(tokens_hi(g), turned(1)))
                    dve.tensor_tensor(tokens_lo(g), turned(1), tokens_hi(g).bitcast(F32), ALU.subtract)\
                        .then_inc(s_xt[1], 1)
                    dve.wait_ge(s_xhi, i + 1)
                    dve.tensor_tensor(tokens_lo(g - 1), turned(0), tokens_hi(g - 1).bitcast(F32), ALU.subtract)\
                        .then_inc(s_xt[0], 1)

            def soft_pull(i, n0, probs):
                for t in range(2):
                    dve.wait_ge(s_score, n0 + 2 * i + t + 1)
                    dve.transpose(probs[:, t, :, :].rearrange("p a b -> p (a b)"), ps[:, 3 + t, :])\
                        .then_inc(s_pull, 1)

            def soft_max(i, n0, probs, stat):
                for t in range(2):
                    dve.wait_ge(s_masked, n0 + 2 * i + t + 1)
                    dve.tensor_reduce(stat[:, t, 0, :], probs[:, t, :, :], AX.X, ALU.max).then_inc(s_max, 1)

            def soft_sum(i, n0, probs, stat):
                for t in range(2):
                    dve.wait_ge(s_exp, n0 + 2 * i + t + 1)
                    ch.link(dve.tensor_reduce(stat[:, t, 1, :], probs[:, t, :, :], AX.X, ALU.add))
                    dve.reciprocal(stat[:, t, 1, :], stat[:, t, 1, :]).then_inc(s_recip, 1)

            def soft_turn(i, n0, probs, turned, used, per):
                for t in range(2):
                    dve.wait_ge(s_prob, n0 + 2 * i + t + 1)
                    if i:
                        dve.wait_ge(used, per * i)
                    for j in range(G):
                        q = slice(32 * j, 32 * j + 32)
                        last = dve.transpose(turned[q, 4 * t:4 * t + 4, :, j, :].rearrange("p a g q -> p (a g) q"),
                                             probs[q, t, :, :])
                    last.then_inc(s_pt, 1)

            def attention0():
                cos = rope0[:, 0, :]
                sin = rope0[:, 1, :]

                def rotate(i, k):
                    dve.wait_ge(s_qkv, 10 * i + k + 1)
                    n = 10 * i + k
                    if n >= 2:
                        dve.wait_ge(s_rope, n - 1)
                    x = ps[:, k % 3, :].rearrange("p (b s) -> p b s", s=C)
                    y = rot[:, k % 2, :, :].rearrange("p a (b s) -> p a b s", s=C)
                    dve.tensor_tensor(y[:, 0], x, cos.unsqueeze(1).broadcast_to([P, HALF // C, C]), ALU.mult)
                    for h in range(2):
                        src, dst = slice(64 * h, 64 * h + 64), slice(64 - 64 * h, 128 - 64 * h)
                        last = dve.tensor_tensor(y[dst, 1], x[src],
                                                 sin[src].unsqueeze(1).broadcast_to([64, HALF // C, C]), ALU.mult)
                    last.then_inc(s_rot, 1)

                def split_heads(i, tiles):
                    for q in tiles:
                        dve.wait_ge(s_hhi, 8 * i + q + 1)
                        cols = slice((q % 4) * P, (q % 4 + 1) * P)
                        dve.tensor_tensor(h_lo[:, :, cols], ps[:, 5 + q % 2, :].rearrange("d (g n) -> d g n", g=GQ),
                                          h_hi[:, :, cols].bitcast(F32), ALU.subtract).then_inc(s_head, 1)

                def add_projection(i, tiles):
                    for n in tiles:
                        half, r = n // 4, n % 4
                        dve.wait_ge(s_proj, 8 * i + n + 1)
                        dst = fresh[:, half * 16:half * 16 + 16, r, :]
                        dve.tensor_tensor(dst, ps[:, (7, 2, 0, 1)[r], :].rearrange("p (b c) -> p b c", c=C), dst,
                                          ALU.add).then_inc(s_fresh, 1)

                for k in range(10):
                    rotate(0, k)
                dve.wait_ge(s_zero, 2)
                soft_pull(0, 0, probs)
                for i in range(NKV):
                    for k in range(10):
                        if i + 1 < NKV:
                            rotate(i + 1, k)
                        if k == 0 and i + 1 < NKV:
                            soft_max(i, 0, probs, stat)
                        if k == 2 and i + 1 < NKV:
                            soft_sum(i, 0, probs, stat)
                        if k == 5 and i + 1 < NKV:
                            soft_turn(i, 0, probs, probs_t, s_pv, 8)
                        if k in (6, 7):
                            split_heads(i, range(2 * k - 12, 2 * k - 10))
                    add_projection(i, range(4))
                    split_heads(i, range(4, 8))
                    if i + 1 < NKV:
                        soft_pull(i + 1, 0, probs)
                    for n in range(4, 8):
                        add_projection(i, (n,))
                        if i == NKV - 2 and n == 4:
                            soft_max(i + 1, 0, probs, stat)
                        if i == NKV - 2 and n == 5:
                            soft_sum(i + 1, 0, probs, stat)
                        if i == NKV - 2 and n == 6:
                            soft_turn(i + 1, 0, probs, probs_t, s_pv, 8)

            def add_back(stage):
                for g in range(NGROUP):
                    dve.wait_ge(s_back[stage], g + 1)
                    x = stream[:, g * G:(g + 1) * G, :]
                    dve.tensor_tensor(x, ps[:, TURN[g % 2], :].rearrange("p (b t) -> p b t", t=T), x, ALU.add)\
                        .then_inc(s_added[stage], 1)

            def over(x, shape):
                return x.unsqueeze(len(shape) - 1).broadcast_to(shape)

            def choose(v, first, second, m1, m2, key, top):
                shape = [P, NTILE, NE]
                rank = rank_const[:, :].unsqueeze(1).broadcast_to(shape)
                for src, hot, most in ((v, first, m1), (key, second, m2)):
                    ch.link(dve.tensor_reduce(most, src, AX.X, ALU.max))
                    ch.link(dve.tensor_tensor(hot, src, over(most, shape), ALU.is_equal))
                    ch.link(dve.tensor_tensor(hot, hot, rank, ALU.mult))
                    ch.link(dve.tensor_reduce(top, hot, AX.X, ALU.max))
                    ch.link(dve.tensor_tensor(hot, hot, over(top, shape), ALU.is_equal))
                    if hot is first:
                        ch.link(dve.scalar_tensor_tensor(key, first, MASKED, v, ALU.mult, ALU.add))

            def gate0():
                row = lambda k, n: f0_rows[:, 0, k:k + n]
                tiles = [P, NTILE, NGATE]
                shape = [P, NTILE, NE]
                per_tile = lambda x: x.unsqueeze(1).broadcast_to([P, NTILE, x.shape[-1]])
                dve.wait_ge(s_fw[0], 64)
                dve.wait_ge(s_natc[0], 4)
                ch.link(dve.tensor_tensor(gate_a, nat[:, :, 0:NGATE], per_tile(row(0, NGATE)), ALU.add))
                ch.link(dve.tensor_reduce(col[:, 0, :], gate_a, AX.X, ALU.add))
                ch.link(dve.tensor_scalar(col[:, 0, :], col[:, 0, :], 1.0 / NGATE, None, ALU.mult))
                ch.link(dve.tensor_tensor(gate_a, gate_a, over(col[:, 0, :], tiles), ALU.subtract))
                ch.link(dve.tensor_tensor(gate_b, gate_a, gate_a, ALU.mult))
                dve.tensor_reduce(col[:, 1, :], gate_b, AX.X, ALU.add).then_inc(s_gate[0], 1)
                dve.wait_ge(s_gact[0], 1)
                ch.link(dve.reciprocal(col[:, 1, :], col[:, 1, :]))
                ch.link(dve.tensor_tensor(gate_a, gate_a, over(col[:, 1, :], tiles), ALU.mult))
                ch.link(dve.tensor_tensor(gate_a, gate_a, per_tile(row(NGATE, NGATE)), ALU.mult))
                ch.link(dve.tensor_tensor(gate_a, gate_a, per_tile(row(2 * NGATE, NGATE)), ALU.add))
                ch.link(dve.tensor_scalar(gate_a, gate_a, 0.0, None, ALU.max))
                big = [P, NTILE, NE, NGATE]
                w2 = row(3 * NGATE, NE * NGATE).rearrange("p (e k) -> p e k", e=NE)
                ch.link(dve.tensor_tensor(gate_p, gate_a.unsqueeze(2).broadcast_to(big),
                                          w2.unsqueeze(1).broadcast_to(big), ALU.mult))
                gates, first, second, key, w = (vote[:, n] for n in range(5))
                ch.link(dve.tensor_reduce(gates, gate_p, AX.X, ALU.add))
                ch.link(dve.tensor_tensor(gates, gates, per_tile(row(3 * NGATE + NE * NGATE, NE)), ALU.add))
                first, second = both[:, :, 0, :], both[:, :, 1, :]
                choose(gates, first, second, col[:, 2, :], col[:, 3, :], key, col[:, 5, :])
                dve.tensor_tensor(col[:, 4, :], col[:, 3, :], col[:, 2, :], ALU.subtract).then_inc(s_both, 1)
                dve.engine_nop().then_inc(s_gate[0], 1)
                dve.wait_ge(s_gact[0], 2)
                ch.link(dve.tensor_scalar(col[:, 5, :], col[:, 4, :], 1.0, None, ALU.add))
                ch.link(dve.reciprocal(col[:, 5, :], col[:, 5, :]))
                ch.link(dve.tensor_tensor(col[:, 6, :], col[:, 5, :], col[:, 4, :], ALU.mult))
                dve.wait_ge(s_count, 1)
                ch.link(dve.tensor_reduce(count[:, 0, :], ps[:, 2, 0:P].rearrange("p (m k) -> p k m", m=NTILE),
                                          AX.X, ALU.add))
                ch.link(dve.tensor_scalar(count[:, 1, :], count[:, 0, :], float(CAPACITY), LORA0, ALU.is_le, ALU.mult))
                for n, g in ((0, 5), (1, 6)):
                    hot = both[:, :, n, :]
                    ch.link(dve.tensor_tensor(hot, hot, per_tile(count[:, 1, n * NE:(n + 1) * NE]), ALU.mult))
                    ch.link(dve.tensor_tensor(hot, hot, over(col[:, g, :], shape), ALU.mult))
                ch.link(dve.tensor_tensor(w, first, second, ALU.add))
                weigh(0, w, NGATE)

            def weigh(n, w, at):
                x = nat[:, :, at:at + P].rearrange("p m (e k) -> p m e k", e=NE)
                dve.tensor_tensor(x, x, w.unsqueeze(3).broadcast_to([P, NTILE, NE, RANK]), ALU.mult)\
                    .then_inc(s_lora[n], 1)

            def gate1():
                shape = [P, NTILE, NE]
                p, first, second, key, w = (vote[:, n] for n in range(5))
                dve.wait_ge(s_natc[1], 4)
                ch.link(dve.tensor_reduce(col[:, 0, :], nat[:, :, 0:NE], AX.X, ALU.max))
                dve.tensor_tensor(p, nat[:, :, 0:NE], over(col[:, 0, :], shape), ALU.subtract).then_inc(s_gate[1], 1)
                dve.wait_ge(s_gact[1], 1)
                ch.link(dve.tensor_reduce(col[:, 1, :], p, AX.X, ALU.add))
                ch.link(dve.reciprocal(col[:, 1, :], col[:, 1, :]))
                ch.link(dve.tensor_tensor(p, p, over(col[:, 1, :], shape), ALU.mult))
                choose(p, first, second, col[:, 2, :], col[:, 3, :], key, col[:, 5, :])
                ch.link(dve.tensor_tensor(col[:, 4, :], col[:, 2, :], col[:, 3, :], ALU.add))
                ch.link(dve.reciprocal(col[:, 4, :], col[:, 4, :]))
                ch.link(dve.tensor_tensor(w, first, second, ALU.add))
                ch.link(dve.tensor_tensor(w, w, p, ALU.mult))
                ch.link(dve.tensor_scalar(col[:, 4, :], col[:, 4, :], LORA1, None, ALU.mult))
                ch.link(dve.tensor_tensor(w, w, over(col[:, 4, :], shape), ALU.mult))
                weigh(1, w, NE)

            def ffn(n):
                (gate0, gate1)[n]()
                for k in range(1, 8, 2):
                    half, r_out = k // 4, k % 4
                    dve.wait_ge(s_ffn[n], k + 1)
                    dst = fresh[:, half * 16:half * 16 + 16, r_out, :]
                    src = ps[:, FFN_BANK[k], :].rearrange("p (b c) -> p b c", c=C)
                    if n:
                        last = dve.tensor_scalar(dst, src, f1_bias[:, 0, r_out:r_out + 1], None, ALU.add)
                    else:
                        last = dve.tensor_copy(dst, src)
                    last.then_inc(s_fdve[n], 1)

            def attention1():
                dve.wait_ge(s1_w, 80)
                dve.wait_ge(s1_natc, 4)
                q, pe1, pe2, lat = (nat1[:, :, x:y] for x, y in ((0, QA), (QA, QA + 32), (QA + 32, QA + 64),
                                                                (QA + 64, QA + 96)))
                sq, t1 = tmp_k[:, 0], tmp_k[:, 1]
                ch.link(dve.tensor_tensor(sq, q, q, ALU.mult))
                ch.link(dve.tensor_reduce(rms[:, 0, :], sq, AX.X, ALU.add))
                ch.link(dve.tensor_tensor(t1[:, :, 0:LAT], lat, lat, ALU.mult))
                dve.tensor_reduce(rms[:, 1, :], t1[:, :, 0:LAT], AX.X, ALU.add).then_inc(s1_sq, 1)
                cos, sin = (rope1r[:, n, :].unsqueeze(1).broadcast_to([P, NTILE, 32]) for n in range(2))
                parts = [sq[:, :, 32 * n:32 * n + 32] for n in range(4)]
                ch.wait()
                for dst, x, y in zip(parts, (pe1, pe2, pe2, pe1), (cos, sin, cos, sin)):
                    ch.mark(dve.tensor_tensor(dst, x, y, ALU.mult))
                ch.wait()
                dve.tensor_tensor(keys_n[:, :, 0:32], parts[0], parts[1], ALU.subtract)
                dve.tensor_tensor(keys_n[:, :, 32:64], parts[2], parts[3], ALU.add)
                dve.wait_ge(s1_root, 2)
                ch.link(dve.reciprocal(rms[:, 2:4, :], rms[:, 2:4, :]))
                dve.tensor_tensor(q, q, over(rms[:, 2, :], [P, NTILE, QA]), ALU.mult).then_inc(s1_qn, 1)
                ch.link(dve.tensor_tensor(values1, lat, over(rms[:, 3, :], [P, NTILE, LAT]), ALU.mult))
                ch.link(dve.tensor_tensor(values1, values1, a1_ln[:, 0, 1:1 + LAT].unsqueeze(1)
                                          .broadcast_to([P, NTILE, LAT]), ALU.mult))
                dve.tensor_copy(keys_n[:, :, 64:96], values1).then_inc(s1_kn, 1)

                def rotate(i, k):
                    dve.wait_ge(s1_swap, 8 * i + k + 1)
                    n = 8 * i + k
                    if n >= 3:
                        dve.wait_ge(s1_rope, n - 2)
                    x = ps[0:QK1, (0, 1, 2, 7)[k % 4], :].rearrange("p (b s) -> p b s", s=C)
                    y = rot_ring[n % 3][0:QK1, :, :].rearrange("p a (b s) -> p a b s", s=C)
                    dve.tensor_tensor(y[:, 0], x, rope1c[0:QK1, 0, :].unsqueeze(1)
                                      .broadcast_to([QK1, HALF // C, C]), ALU.mult)
                    dve.tensor_tensor(y[0:ROT, 1], y[0:ROT, 1], rope1c[0:ROT, 1, :].unsqueeze(1)
                                      .broadcast_to([ROT, HALF // C, C]), ALU.mult).then_inc(s1_rot, 1)

                dve.wait_ge(s1_wc, 8)
                for slot in rot_ring:
                    ch.mark(dve.memset(slot[64:96, 1, :], 0.0))
                ch.wait()
                dve.wait_ge(s1_zero, 1)
                def turn_flat(i):
                    for t in range(2):
                        dve.wait_ge(s_prob, SOFT0 + 2 * i + t + 1)
                        if i:
                            dve.wait_ge(s1_place, 2 * (i - 1) + t + 1)
                        dve.transpose(flat[:, t, :, :].rearrange("p a b -> p (a b)"),
                                      probs1[:, t, :, :].rearrange("p a b -> p (a b)")).then_inc(s1_flat, 1)

                for k in range(16):
                    rotate(k // 8, k % 8)
                for i in range(8):
                    if i:
                        dve.wait_ge(s1_flat, 2 * i)
                    soft_pull(i, SOFT0, probs1)
                    for k in range(8):
                        if i + 2 < 8:
                            rotate(i + 2, k)
                        if k == 1:
                            soft_max(i, SOFT0, probs1, stat1)
                            dve.wait_ge(s_max, SOFT0 + 2 * i + 2)
                            dve.tensor_tensor(probs1[:, 1], probs1[:, 1], stat1[:, 1, 0, :].unsqueeze(2)
                                              .broadcast_to([P, 16, C]), ALU.subtract).then_inc(s1_shift, 1)
                        if k == 3:
                            soft_sum(i, SOFT0, probs1, stat1)
                        if k == 6:
                            turn_flat(i)
                for k in range(1, 8, 2):
                    half, r_out = k // 4, k % 4
                    dve.wait_ge(s1_out, k + 1)
                    dve.tensor_copy(fresh[:, half * 16:half * 16 + 16, r_out, :],
                                    ps[:, FFN_BANK[k], :].rearrange("p (b c) -> p b c", c=C)).then_inc(s1_odve, 1)

            conv_stack(0)
            dve.wait_ge(s_const_loaded, 48)
            attention0()
            dve.wait_ge(s_wlo, R * 2 * NKV)
            zero_pads()
            dve.wait_ge(s_again, 16)
            add_back(0)
            conv_stack(1)
            ffn(0)
            add_back(1)
            conv_stack(2)
            attention1()
            dve.wait_ge(s_score, SOFT0 + 16)
            dve.wait_ge(s1_place, 16)
            zero_pads()
            add_back(2)
            conv_stack(3)
            ffn(1)
            add_back(3)

        @block.gpsimd
        def _(pool):
            ch = Chain(pool, pool_steps)
            pool.memset(fresh[:, :, :, :], 0.0).then_inc(s_zero, 1)
            pool.wait_ge(s_setup, N_SETUP)
            conv_blocks(pool, ch, tmpw[:, 1, :], 0, (1,), s_blk0[1])

            stage = stage1.rearrange("p (r n) -> p r n", r=R)

            def split_qkv(i):
                n = wcols(i)
                src = stage if i else stage0
                for r in range(R):
                    pool.wait_ge(s_whi, R * part(i) + r + 1)
                    pool.tensor_tensor(w_lo[:, r, 0:n], src[:, r, 0:n], w_hi[:, r, 0:n].bitcast(F32),
                                       ALU.subtract).then_inc(s_wlo, 1)

            def conv_stack(net):
                pool.wait_ge(s_scales, 1 if net == 0 else 2)
                for g in range(NGROUP):
                    if net:
                        pool.wait_ge(s_added[net - 1], g + 1)
                    elif g % 2 == 0:
                        pool.wait_ge(s_stream[g // 2], 16)
                    if g >= 2:
                        pool.wait_ge(s_conv[0], done(net, 8) + g - 1)
                    pool.tensor_tensor(act0[:, g % 2, :, 1:T + 1], stream[:, g * G:(g + 1) * G, :],
                                       in_scale[:, net, 0, g * G:(g + 1) * G].unsqueeze(2).broadcast_to([P, G, T]),
                                       ALU.mult).then_inc(s_in, 1)
                    if net == 0 and g == 1:
                        conv_blocks(pool, ch, tmpw[:, 1, :], 0, (2,), s_blk0[2])
                    if net == 0 and g == 7:
                        split_qkv(0)
                    if net == 0 and g in (3, 5, 7):
                        n = (g - 1) // 2
                        conv_blocks(pool, ch, tmpw[:, 1, :], n, range(LAYER), s_wblk[n - 1])

            def soft_mask(i, n0, probs):
                for t in range(2):
                    pool.wait_ge(s_pull, n0 + 2 * i + t + 1)
                    pool.tensor_tensor(probs[:, t], probs[:, t], causal[:, :].unsqueeze(1)
                                       .broadcast_to([P, 16, C]), ALU.add).then_inc(s_masked, 1)

            def soft_shift(i, n0, probs, stat, tiles=(0, 1)):
                for t in tiles:
                    pool.wait_ge(s_max, n0 + 2 * i + t + 1)
                    pool.tensor_tensor(probs[:, t], probs[:, t], stat[:, t, 0, :].unsqueeze(2)
                                       .broadcast_to([P, 16, C]), ALU.subtract).then_inc(s_shift, 1)

            def soft_scale(i, n0, probs, stat):
                for t in range(2):
                    pool.wait_ge(s_recip, n0 + 2 * i + t + 1)
                    pool.tensor_tensor(probs[:, t], probs[:, t], stat[:, t, 1, :].unsqueeze(2)
                                       .broadcast_to([P, 16, C]), ALU.mult).then_inc(s_prob, 1)

            def attention1():
                pool.wait_ge(s1_wcc, 8)
                pool.wait_ge(s1_wqc, 2)
                pool.memset(made, 0.0).then_inc(s1_zero, 1)
                pool.wait_ge(s1_zero, 1)

                def rope_add(i, k):
                    n = 8 * i + k
                    pool.wait_ge(s1_rot, n + 1)
                    if i >= 2 and k == 0:
                        pool.wait_ge(s_score, SOFT0 + 2 * (i - 1))
                    pool.tensor_tensor(q1[i % 2][0:QK1, k // 2, (k % 2) * HALF:(k % 2 + 1) * HALF],
                                       rot_ring[n % 3][0:QK1, 0, :], rot_ring[n % 3][0:QK1, 1, :],
                                       ALU.add).then_inc(s1_rope, 1)

                for k in range(16):
                    rope_add(k // 8, k % 8)
                for i in range(8):
                    soft_mask(i, SOFT0, probs1)
                    for k in range(8):
                        if i + 2 < 8:
                            rope_add(i + 2, k)
                        if k == 0:
                            soft_shift(i, SOFT0, probs1, stat1, (0,))
                        if k == 3:
                            soft_scale(i, SOFT0, probs1, stat1)

            def attention0():
                def rope_add(i, k):
                    n = 10 * i + k
                    pool.wait_ge(s_rot, n + 1)
                    if i and k == 0:
                        pool.wait_ge(s_score, 2 * i)
                    chunk, half = k % (1 + GQ), k // (1 + GQ)
                    pool.tensor_tensor(qk[:, chunk, half * HALF:(half + 1) * HALF], rot[:, k % 2, 0, :],
                                       rot[:, k % 2, 1, :], ALU.add).then_inc(s_rope, 1)

                def split_o(i):
                    for g in range(GQ):
                        pool.wait_ge(s_whi, R * part_o(i) + g + 1)
                        pool.tensor_tensor(wo_lo[:, g, :, :].rearrange("d r t -> d (r t)"),
                                           stage1[:, g * R * P:(g + 1) * R * P],
                                           wo_hi[:, g, :, :].rearrange("d r t -> d (r t)").bitcast(F32),
                                           ALU.subtract).then_inc(s_wlo, 1)

                pool.memset(probs_t[:, :, :, :, :], 0.0).then_inc(s_zero, 1)
                for k in range(10):
                    rope_add(0, k)
                split_qkv(1)
                for i in range(NKV):
                    soft_mask(i, 0, probs)
                    for k in range(10):
                        if i + 1 < NKV:
                            rope_add(i + 1, k)
                        if k == 0:
                            soft_shift(i, 0, probs, stat)
                        if k == 3:
                            soft_scale(i, 0, probs, stat)
                        if k == 5:
                            split_o(i)
                    if i + 2 < NKV:
                        split_qkv(i + 2)

            conv_stack(0)
            attention0()
            conv_stack(1)
            conv_stack(2)
            attention1()
            conv_stack(3)


def lay_out(inp):
    a = {}
    a["x"] = inp["x"].reshape(B, C, T, R).transpose(3, 1, 0, 2).reshape(P, B, T)
    a["style"] = np.tile(inp["cond_512"].T, (1, R))
    nets = ["L0_cond", "L0_cond2", "L1_cond", "L1_cond2"]
    n = NET * LAYER
    a["modw"] = np.stack([inp[k + "_mod_w"] for k in nets]).reshape(n, C, STYLE).transpose(2, 0, 1)
    mod_b = np.stack([inp[k + "_mod_b"] for k in nets]).reshape(n, 1, C)
    a["modb"] = np.broadcast_to(mod_b, (n, R, C)).reshape(n, P).T
    bias = np.stack([inp[k + "_biases"] for k in nets]).reshape(NET, LAYER, 1, C)
    a["cbias"] = np.broadcast_to(bias, (NET, LAYER, R, C)).reshape(NET, LAYER, P).transpose(2, 0, 1)
    w = np.stack([inp[k + "_weights"] for k in nets]).reshape(NET, LAYER, C, C, TAPS)
    by_in = w.transpose(3, 0, 1, 4, 2)
    a["wsq"] = by_in.transpose(2, 0, 1, 3, 4).reshape(P, NET, TAPS, C)
    contracted = by_in.copy()
    contracted[:, :, 1] = w.transpose(2, 0, 1, 4, 3)[:, :, 1]
    a["wrep"] = contracted.reshape(C, n, TAPS, C)

    qkv = inp["L0_attn_Wqkv"].reshape((NH + 2 * NKV) * HD, T, R)
    q = qkv[:NH * HD].reshape(NKV, GQ, HD, T, R)
    k = qkv[NH * HD:(NH + NKV) * HD].reshape(NKV, 1, HD, T, R)
    v = qkv[(NH + NKV) * HD:].reshape(NKV, 1, HD, T, R)
    v2 = np.concatenate([v, np.roll(v, -1, 0)], 1)
    a["w_qkv"] = np.concatenate([k, q, v2], 1).transpose(0, 3, 4, 1, 2).reshape(NKV, T, R, 7 * HD)
    a["w_o"] = inp["L0_attn_Wo"].reshape(T, R, NKV, GQ, HD).transpose(2, 4, 3, 1, 0)

    def into(x):
        return x.reshape(x.shape[0], T, R).transpose(1, 2, 0)

    def out_of(x):
        return x.reshape(T, R, x.shape[1]).transpose(2, 1, 0)

    def rows(*vs):
        v = np.concatenate([x.reshape(-1) for x in vs])
        return np.broadcast_to(v, (P, v.size))

    lora_a = inp["L0_ffn_lora_A"].transpose(0, 2, 1).reshape(NE * RANK, L)
    a["f0_in"] = np.concatenate([into(inp["L0_ffn_gw1"]), into(lora_a)], 2)
    a["f0_main"] = inp["L0_ffn_weight"].reshape(T, R, T, R).transpose(2, 3, 1, 0)
    a["f0_out"] = out_of(inp["L0_ffn_lora_B"].transpose(2, 0, 1).reshape(L, NE * RANK))
    a["f0_rows"] = rows(*(inp["L0_ffn_" + k] for k in ("gb1", "ln_gamma", "ln_beta", "gw2", "gb2")))
    a["f1_in"] = np.concatenate([into(inp["L1_ffn_W_router"]), into(inp["L1_ffn_A"].reshape(NE * RANK, L))], 2)
    a["f1_main"] = inp["L1_ffn_W_base"].reshape(T, R, T, R).transpose(2, 3, 1, 0)
    a["f1_out"] = out_of(inp["L1_ffn_B"].transpose(1, 0, 2).reshape(L, NE * RANK))
    a["f1_bias"] = inp["L1_ffn_b_base"].reshape(T, R)

    kv_a = inp["L1_attn_wkv_a"]
    a["a1_in"] = np.concatenate([into(inp["L1_attn_wq_a"]), into(kv_a[LAT::2]), into(kv_a[LAT + 1::2]),
                                 into(kv_a[:LAT])], 2)
    q_b = inp["L1_attn_wq_b"].reshape(NH, NOPE + ROT, QA)
    a["a1_pe"] = np.concatenate([q_b[:, NOPE::2], q_b[:, NOPE + 1::2]], 1).transpose(2, 0, 1)
    a["a1_nope"] = q_b[:, :NOPE].reshape(NH // 2, 2 * NOPE, QA).transpose(1, 0, 2)
    kv_b = inp["L1_attn_wkv_b"].reshape(NH, NOPE + VD, LAT)
    pairs = np.zeros((2, NOPE, NH // 2, 2, LAT), np.float32)
    for h in range(2):
        pairs[h, :, :, h] = kv_b[h::2, :NOPE].transpose(1, 0, 2)
    a["a1_kb"] = pairs.reshape(2 * NOPE, NH // 2, 2 * LAT)
    a["a1_v"] = kv_b[:, NOPE:].transpose(1, 0, 2)
    a["a1_wo"] = inp["L1_attn_wo"].reshape(T, R, NH // GQ, GQ, VD).transpose(2, 4, 3, 1, 0)\
        .reshape(NH // GQ, VD, GQ, L)
    a["a1_ln"] = np.concatenate([inp["L1_attn_q_a_ln_w"].reshape(QA, 1), rows(inp["L1_attn_kv_a_ln_w"])], 1)

    a["factor"] = tap_factors().reshape(P, TAPS, NBLKS)
    a["ident"] = np.eye(P, dtype=np.float32)
    a["rope0"] = rope0_tables().reshape(P, 2, C)
    a["rope1r"] = rope1_rows().reshape(P, 2, LAT)
    a["rope1c"] = rope1_cols()
    a["causal"] = causal_mask()
    a["rank"] = np.tile(np.arange(NE, 0, -1, dtype=np.float32), (P, 1))
    return {k: np.ascontiguousarray(v) for k, v in a.items()}


def kernel(**inputs):
    import concourse.bacc as bacc
    from concourse.bass_utils import run_bass_kernel_spmd

    arrays = lay_out({k: np.asarray(v) for k, v in inputs.items()})
    nc = bacc.Bacc("TRN2", target_bir_lowering=False, num_devices=1)
    args = {k: nc.dram_tensor(f"in_{k}_dram", v.shape, F32, kind="ExternalInput").ap() for k, v in arrays.items()}
    out = nc.dram_tensor("out_dram", (P, B, T), F32, kind="ExternalOutput").ap()
    build(nc, args, out)
    r = run_bass_kernel_spmd(nc, [{f"in_{k}_dram": v for k, v in arrays.items()}], core_ids=[0])
    y = r.results[0]["out_dram"]
    return y.reshape(R, C, B, T).transpose(2, 1, 3, 0).reshape(B, C, L)
```
